# Optimizing a Trainium2 kernel written in Bass

```python
import numpy as np
import jax
import jax.numpy as jnp

def _softmax(x, axis=-1):
    return jax.nn.softmax(x, axis=axis)

def _gelu(x):
    return jax.nn.gelu(x, approximate=True)

def _silu(x):
    return jax.nn.silu(x)

def _sigmoid(x):
    return jax.nn.sigmoid(x)

def _layernorm(x, axis=-1, eps=1e-05):
    m = jnp.mean(x, axis=axis, keepdims=True)
    v = jnp.var(x, axis=axis, keepdims=True)
    return (x - m) / jnp.sqrt(v + eps)

def _scatter_add(tgt, idx, src, axis=0):
    return tgt.at[idx].add(src)

def _segment_sum(src, seg, n):
    return jax.ops.segment_sum(src, seg, n)
kernel_name = 'mk_gnn_ffn_d2_gnn_r8_acd887'

def setup_inputs(seed: int=0):
    np.random.seed(seed)
    _w = jnp.asarray

    def _rec_inputs():
        import jax
        import jax.numpy as jnp
        _gk = jax.random.key(seed)
        x = -0.0001394 + 0.9999 * jax.random.normal(jax.random.fold_in(_gk, 1), (1250, 768), jnp.float32)
        src = jax.random.randint(jax.random.fold_in(_gk, 2), (20000,), 0, 1250, jnp.int32)
        dst = jnp.minimum((1250 * jax.random.uniform(jax.random.fold_in(_gk, 3), (20000,)) ** 2.0).astype(jnp.int32), 9999)
        _o = jnp.argsort(dst, stable=True)
        src = src[_o]
        dst = dst[_o]
        edge_type_3 = jax.random.randint(jax.random.fold_in(_gk, 13), (20000,), 0, 3, jnp.int32)
        return (x, src, dst, edge_type_3)
    x, src, dst, edge_type_3 = _rec_inputs()

    def _L0_gnn_setup():
        import jax, jax.numpy as jnp
        import numpy as np
        N = 6250
        E = 31250
        H = 12
        D = 64
        NEG_SLOPE = 0.2
        key = jax.random.key(seed)
        k1, k2, k3, k4, k5, k6, k7 = jax.random.split(key, 7)
        h = jax.random.normal(k1, (N, H * D), dtype=jnp.float32)
        src = jnp.concatenate([jnp.arange(N, dtype=jnp.int32), jax.random.randint(k2, (E - N,), 0, N, dtype=jnp.int32)])
        dst = jnp.concatenate([jnp.arange(N, dtype=jnp.int32), jax.random.randint(k3, (E - N,), 0, N, dtype=jnp.int32)])
        xav = 1.414 / np.sqrt(D)
        W_fc = jax.random.normal(k4, (D, D), dtype=jnp.float32) * xav
        attn_l = jax.random.normal(k5, (H, D), dtype=jnp.float32) * 0.15
        attn_r = jax.random.normal(k6, (H, D), dtype=jnp.float32) * 0.15
        W_res = jax.random.normal(k7, (D, D), dtype=jnp.float32) * xav
        return {'h': h, 'W_fc': W_fc, 'attn_l': attn_l, 'attn_r': attn_r, 'W_res': W_res, 'src': src, 'dst': dst}
    _L0_gnn_all = _L0_gnn_setup()
    _L0_gnn_in = {k: v for k, v in _L0_gnn_all.items() if k in ('W_fc', 'attn_l', 'attn_r', 'W_res')}
    del _L0_gnn_all

    def _L0_ffn_setup():
        import jax, jax.numpy as jnp
        import numpy as np
        E, C, F, K = (8, 768, 384, 2)
        key = jax.random.key(seed)
        k0, k1, k2, k3 = jax.random.split(key, 4)
        B, T = (8, 256)
        return {'x': jax.random.normal(k0, (B, T, C), jnp.float32), 'router_w': jax.random.normal(k1, (E, C), jnp.float32) * 0.02, 'w1': jax.random.normal(k2, (E, C, F), jnp.float32) * 0.02, 'b1': jnp.zeros((E, F), jnp.float32), 'w2': jax.random.normal(k3, (E, F, C), jnp.float32) * 0.02, 'b2': jnp.zeros((E, C), jnp.float32)}
    _L0_ffn_all = _L0_ffn_setup()
    _L0_ffn_in = {k: v for k, v in _L0_ffn_all.items() if k in ('router_w', 'w1', 'b1', 'w2', 'b2')}
    del _L0_ffn_all

    def _L1_gnn_setup():
        import jax, jax.numpy as jnp
        import numpy as np
        NEG_SLOPE = 0.2
        EPS = 1e-16
        N_NODES = 4096
        N_EDGES = 20000
        DIM = 768
        HEADS1 = 4
        OUT1 = DIM // HEADS1
        HEADS2 = 1
        OUT2 = DIM
        N_REL = 3

        def rgat_conv(x, W, q, k, b, src, dst, etype, heads, out_ch, n_nodes):
            xr = jnp.einsum('nd,rdf->rnf', x, W)
            oi = xr[etype, dst]
            oj = xr[etype, src]
            qi = oi @ q
            kj = oj @ k
            alpha = jax.nn.leaky_relu(qi + kj, NEG_SLOPE)
            m = jax.ops.segment_max(alpha, dst, num_segments=n_nodes)
            e = jnp.exp(alpha - m[dst])
            z = jax.ops.segment_sum(e, dst, num_segments=n_nodes)
            a = e / (z[dst] + EPS)
            msg = (a[:, :, None] * oj.reshape(-1, heads, out_ch)).reshape(-1, heads * out_ch)
            out = jax.ops.segment_sum(msg, dst, num_segments=n_nodes)
            return out + b
        key = jax.random.key(seed)
        ks = jax.random.split(key, 12)
        s = 0.02
        return {'x': jax.random.normal(ks[0], (N_NODES, DIM), dtype=jnp.float32), 'edge_index': jax.random.randint(ks[1], (2, N_EDGES), 0, N_NODES, dtype=jnp.int64), 'edge_type': jax.random.randint(ks[2], (N_EDGES,), 0, N_REL, dtype=jnp.int64), 'W1': jax.random.normal(ks[3], (N_REL, DIM, HEADS1 * OUT1), dtype=jnp.float32) * s, 'q1': jax.random.normal(ks[4], (HEADS1 * OUT1, HEADS1), dtype=jnp.float32) * s, 'k1': jax.random.normal(ks[5], (HEADS1 * OUT1, HEADS1), dtype=jnp.float32) * s, 'b1': jnp.zeros((HEADS1 * OUT1,), dtype=jnp.float32), 'W2': jax.random.normal(ks[6], (N_REL, DIM, HEADS2 * OUT2), dtype=jnp.float32) * s, 'q2': jax.random.normal(ks[7], (HEADS2 * OUT2, HEADS2), dtype=jnp.float32) * s, 'k2': jax.random.normal(ks[8], (HEADS2 * OUT2, HEADS2), dtype=jnp.float32) * s, 'b2': jnp.zeros((HEADS2 * OUT2,), dtype=jnp.float32)}
    _L1_gnn_all = _L1_gnn_setup()
    _L1_gnn_in = {k: v for k, v in _L1_gnn_all.items() if k in ('W1', 'q1', 'k1', 'b1', 'W2', 'q2', 'k2', 'b2')}
    del _L1_gnn_all

    def _L1_ffn_setup():
        import jax, jax.numpy as jnp
        import numpy as np
        B, L, D, H, F = (4, 256, 768, 12, 384)
        ROUTE_FRAC = 0.15
        LN_EPS = 1e-05

        def _ln(x, g, b):
            m = jnp.mean(x, axis=-1, keepdims=True)
            v = jnp.mean((x - m) ** 2, axis=-1, keepdims=True)
            return (x - m) * jax.lax.rsqrt(v + LN_EPS) * g + b
        key = jax.random.key(seed)
        ks = jax.random.split(key, 20)
        s = 0.02
        return {'hidden_states': jax.random.normal(ks[0], (B, L, D), dtype=jnp.float32), 'g1': jnp.ones((D,), jnp.float32), 'b1': jnp.zeros((D,), jnp.float32), 'g2': jnp.ones((D,), jnp.float32), 'b2': jnp.zeros((D,), jnp.float32), 'Wr': jax.random.normal(ks[1], (D,), jnp.float32) * s, 'br': jnp.zeros((), jnp.float32), 'Wq': jax.random.normal(ks[2], (D, D), jnp.float32) * s, 'bq': jnp.zeros((D,), jnp.float32), 'Wk': jax.random.normal(ks[3], (D, D), jnp.float32) * s, 'bk': jnp.zeros((D,), jnp.float32), 'Wv': jax.random.normal(ks[4], (D, D), jnp.float32) * s, 'bv': jnp.zeros((D,), jnp.float32), 'Wo': jax.random.normal(ks[5], (D, D), jnp.float32) * s, 'bo': jnp.zeros((D,), jnp.float32), 'Wm': jax.random.normal(ks[6], (D, D), jnp.float32) * s, 'bm': jnp.zeros((D,), jnp.float32), 'W1': jax.random.normal(ks[7], (D, F), jnp.float32) * s, 'bf1': jnp.zeros((F,), jnp.float32), 'W2': jax.random.normal(ks[8], (F, D), jnp.float32) * s, 'bf2': jnp.zeros((D,), jnp.float32)}
    _L1_ffn_all = _L1_ffn_setup()
    _L1_ffn_in = {k: v for k, v in _L1_ffn_all.items() if k in ('g1', 'b1', 'g2', 'b2', 'Wr', 'br', 'Wq', 'bq', 'Wk', 'bk', 'Wv', 'bv', 'Wo', 'bo', 'Wm', 'bm', 'W1', 'bf1', 'W2', 'bf2')}
    del _L1_ffn_all
    return {'x': x, 'src': src, 'dst': dst, 'edge_type_3': edge_type_3, 'L0_gnn_W_fc': _L0_gnn_in['W_fc'], 'L0_gnn_attn_l': _L0_gnn_in['attn_l'], 'L0_gnn_attn_r': _L0_gnn_in['attn_r'], 'L0_gnn_W_res': _L0_gnn_in['W_res'], 'L0_ffn_router_w': _L0_ffn_in['router_w'], 'L0_ffn_w1': _L0_ffn_in['w1'], 'L0_ffn_b1': _L0_ffn_in['b1'], 'L0_ffn_w2': _L0_ffn_in['w2'], 'L0_ffn_b2': _L0_ffn_in['b2'], 'L1_gnn_W1': _L1_gnn_in['W1'], 'L1_gnn_q1': _L1_gnn_in['q1'], 'L1_gnn_k1': _L1_gnn_in['k1'], 'L1_gnn_b1': _L1_gnn_in['b1'], 'L1_gnn_W2': _L1_gnn_in['W2'], 'L1_gnn_q2': _L1_gnn_in['q2'], 'L1_gnn_k2': _L1_gnn_in['k2'], 'L1_gnn_b2': _L1_gnn_in['b2'], 'L1_ffn_g1': _L1_ffn_in['g1'], 'L1_ffn_b1': _L1_ffn_in['b1'], 'L1_ffn_g2': _L1_ffn_in['g2'], 'L1_ffn_b2': _L1_ffn_in['b2'], 'L1_ffn_Wr': _L1_ffn_in['Wr'], 'L1_ffn_br': _L1_ffn_in['br'], 'L1_ffn_Wq': _L1_ffn_in['Wq'], 'L1_ffn_bq': _L1_ffn_in['bq'], 'L1_ffn_Wk': _L1_ffn_in['Wk'], 'L1_ffn_bk': _L1_ffn_in['bk'], 'L1_ffn_Wv': _L1_ffn_in['Wv'], 'L1_ffn_bv': _L1_ffn_in['bv'], 'L1_ffn_Wo': _L1_ffn_in['Wo'], 'L1_ffn_bo': _L1_ffn_in['bo'], 'L1_ffn_Wm': _L1_ffn_in['Wm'], 'L1_ffn_bm': _L1_ffn_in['bm'], 'L1_ffn_W1': _L1_ffn_in['W1'], 'L1_ffn_bf1': _L1_ffn_in['bf1'], 'L1_ffn_W2': _L1_ffn_in['W2'], 'L1_ffn_bf2': _L1_ffn_in['bf2']}

def reference(x, src, dst, edge_type_3, L0_gnn_W_fc, L0_gnn_attn_l, L0_gnn_attn_r, L0_gnn_W_res, L0_ffn_router_w, L0_ffn_w1, L0_ffn_b1, L0_ffn_w2, L0_ffn_b2, L1_gnn_W1, L1_gnn_q1, L1_gnn_k1, L1_gnn_b1, L1_gnn_W2, L1_gnn_q2, L1_gnn_k2, L1_gnn_b2, L1_ffn_g1, L1_ffn_b1, L1_ffn_g2, L1_ffn_b2, L1_ffn_Wr, L1_ffn_br, L1_ffn_Wq, L1_ffn_bq, L1_ffn_Wk, L1_ffn_bk, L1_ffn_Wv, L1_ffn_bv, L1_ffn_Wo, L1_ffn_bo, L1_ffn_Wm, L1_ffn_bm, L1_ffn_W1, L1_ffn_bf1, L1_ffn_W2, L1_ffn_bf2):
    import jax
    import jax.numpy as jnp

    def _L0_gnn_ref(h, W_fc, attn_l, attn_r, W_res, src, dst):
        import jax, jax.numpy as jnp
        import numpy as np
        N = 6250
        E = 31250
        H = 12
        D = 64
        NEG_SLOPE = 0.2
        n = h.shape[0]
        hh = h.reshape(n, H, D)
        ft = jnp.einsum('nhd,ed->nhe', hh, W_fc)
        a1 = jnp.einsum('nhd,hd->nh', ft, attn_l)
        a2 = jnp.einsum('nhd,hd->nh', ft, attn_r)
        e = jax.nn.leaky_relu(a1[src] + a2[dst], negative_slope=NEG_SLOPE)
        m = jax.ops.segment_max(e, dst, num_segments=n)
        ee = jnp.exp(e - m[dst])
        denom = jax.ops.segment_sum(ee, dst, num_segments=n)
        alpha = ee / denom[dst]
        agg = jax.ops.segment_sum(alpha[:, :, None] * ft[src], dst, num_segments=n)
        res = jnp.einsum('nhd,ed->nhe', hh, W_res)
        return jax.nn.relu((res + agg).reshape(n, H * D))

    def _L0_ffn_ref(x, router_w, w1, b1, w2, b2):
        import jax, jax.numpy as jnp
        import numpy as np
        E, C, F, K = (8, 768, 384, 2)
        B, T, Cc = x.shape
        flat = x.reshape(-1, Cc)
        logits = flat @ router_w.T
        probs = jax.nn.softmax(logits.astype(jnp.float32), axis=-1)
        top_w, top_i = jax.lax.top_k(probs, K)
        top_w = (top_w / top_w.sum(-1, keepdims=True)).astype(x.dtype)
        out = jnp.zeros_like(flat)
        for e in range(E):
            w_e = jnp.sum(top_w * (top_i == e), axis=-1)[:, None]
            h = jax.nn.gelu(flat @ w1[e] + b1[e], approximate=False)
            out = out + w_e * (h @ w2[e] + b2[e])
        return out.reshape(B, T, Cc)

    def _L1_gnn_ref(x, edge_index, edge_type, W1, q1, k1, b1, W2, q2, k2, b2):
        import jax, jax.numpy as jnp
        import numpy as np
        NEG_SLOPE = 0.2
        EPS = 1e-16
        N_NODES = 4096
        N_EDGES = 20000
        DIM = 768
        HEADS1 = 4
        OUT1 = DIM // HEADS1
        HEADS2 = 1
        OUT2 = DIM
        N_REL = 3

        def rgat_conv(x, W, q, k, b, src, dst, etype, heads, out_ch, n_nodes):
            xr = jnp.einsum('nd,rdf->rnf', x, W)
            oi = xr[etype, dst]
            oj = xr[etype, src]
            qi = oi @ q
            kj = oj @ k
            alpha = jax.nn.leaky_relu(qi + kj, NEG_SLOPE)
            m = jax.ops.segment_max(alpha, dst, num_segments=n_nodes)
            e = jnp.exp(alpha - m[dst])
            z = jax.ops.segment_sum(e, dst, num_segments=n_nodes)
            a = e / (z[dst] + EPS)
            msg = (a[:, :, None] * oj.reshape(-1, heads, out_ch)).reshape(-1, heads * out_ch)
            out = jax.ops.segment_sum(msg, dst, num_segments=n_nodes)
            return out + b
        src, dst = (edge_index[0], edge_index[1])
        n = x.shape[0]
        h = rgat_conv(x, W1, q1, k1, b1, src, dst, edge_type, HEADS1, OUT1, n)
        h = jax.nn.elu(h)
        out = rgat_conv(h, W2, q2, k2, b2, src, dst, edge_type, HEADS2, OUT2, n)
        return out

    def _L1_ffn_ref(hidden_states, g1, b1, g2, b2, Wr, br, Wq, bq, Wk, bk, Wv, bv, Wo, bo, Wm, bm, W1, bf1, W2, bf2):
        import jax, jax.numpy as jnp
        import numpy as np
        B, L, D, H, F = (4, 256, 768, 12, 384)
        ROUTE_FRAC = 0.15
        LN_EPS = 1e-05

        def _ln(x, g, b):
            m = jnp.mean(x, axis=-1, keepdims=True)
            v = jnp.mean((x - m) ** 2, axis=-1, keepdims=True)
            return (x - m) * jax.lax.rsqrt(v + LN_EPS) * g + b
        b, l, d = hidden_states.shape
        dh = d // H
        normed = _ln(hidden_states, g1, b1)
        scores = jax.nn.sigmoid(jnp.einsum('bld,d->bl', normed, Wr) + br)
        k = max(1, int(round(ROUTE_FRAC * l)))
        _, idx = jax.lax.top_k(-scores, k)
        attn_mask = jnp.zeros((b, l), bool).at[jnp.arange(b)[:, None], idx].set(True)
        q = (normed @ Wq + bq).reshape(b, l, H, dh)
        kk = (normed @ Wk + bk).reshape(b, l, H, dh)
        v = (normed @ Wv + bv).reshape(b, l, H, dh)
        logits = jnp.einsum('blhd,bmhd->bhlm', q, kk) / jnp.sqrt(jnp.float32(dh))
        probs = jax.nn.softmax(logits, axis=-1)
        ctx = jnp.einsum('bhlm,bmhd->blhd', probs, v).reshape(b, l, d)
        attn_out = ctx @ Wo + bo
        w = scores / (jnp.sum(scores, axis=1, keepdims=True) + 1e-06)
        pooled = jnp.einsum('bl,bld->bd', w, normed)
        mix_out = (normed + scores[..., None] * pooled[:, None, :]) @ Wm + bm
        merged = jnp.where(attn_mask[..., None], attn_out, mix_out)
        h = hidden_states + merged
        n2 = _ln(h, g2, b2)
        ffn = jax.nn.gelu(n2 @ W1 + bf1, approximate=False) @ W2 + bf2
        return h + ffn
    edge_index = jnp.stack([src, dst])
    x = x + _L0_gnn_ref(_layernorm(x, axis=-1), L0_gnn_W_fc, L0_gnn_attn_l, L0_gnn_attn_r, L0_gnn_W_res, src, dst)
    x = x + _L0_ffn_ref(_layernorm(x, axis=-1)[None], L0_ffn_router_w, L0_ffn_w1, L0_ffn_b1, L0_ffn_w2, L0_ffn_b2)[0]
    x = x + _L1_gnn_ref(_layernorm(x, axis=-1), edge_index, edge_type_3, L1_gnn_W1, L1_gnn_q1, L1_gnn_k1, L1_gnn_b1, L1_gnn_W2, L1_gnn_q2, L1_gnn_k2, L1_gnn_b2)
    x = x + _L1_ffn_ref(_layernorm(x, axis=-1)[None], L1_ffn_g1, L1_ffn_b1, L1_ffn_g2, L1_ffn_b2, L1_ffn_Wr, L1_ffn_br, L1_ffn_Wq, L1_ffn_bq, L1_ffn_Wk, L1_ffn_bk, L1_ffn_Wv, L1_ffn_bv, L1_ffn_Wo, L1_ffn_bo, L1_ffn_Wm, L1_ffn_bm, L1_ffn_W1, L1_ffn_bf1, L1_ffn_W2, L1_ffn_bf2)[0]
    return x

_drawn_inputs = setup_inputs


def setup_inputs(seed=0):
    import zlib

    import numpy as np

    out = dict(_drawn_inputs(seed))
    spreads = {'L0_ffn_b1': (0.0, 0.381),
     'L0_ffn_b2': (0.0, 0.1),
     'L1_gnn_b1': (0.0, 0.295),
     'L1_gnn_b2': (0.0, 0.1),
     'L1_ffn_g1': (1.0, 0.2),
     'L1_ffn_b1': (0.0, 0.1),
     'L1_ffn_g2': (1.0, 0.6),
     'L1_ffn_b2': (0.0, 2.0),
     'L1_ffn_bq': (0.0, 0.8),
     'L1_ffn_bk': (0.0, 2.0),
     'L1_ffn_bv': (0.0, 0.8),
     'L1_ffn_bo': (0.0, 0.538),
     'L1_ffn_bm': (0.0, 0.438),
     'L1_ffn_bf1': (0.0, 0.8),
     'L1_ffn_bf2': (0.0, 0.409)}
    factors = {'L1_gnn_q1': 4.562,
     'L1_gnn_k1': 5.301,
     'L1_gnn_q2': 8.0,
     'L1_gnn_k2': 8.0,
     'L1_ffn_Wq': 8.0,
     'L1_ffn_Wk': 8.0,
     'L1_ffn_Wv': 7.496,
     'L1_ffn_Wo': 5.109}
    for name, (base, spread) in spreads.items():
        noise = np.random.default_rng([zlib.crc32(name.encode()), seed]).standard_normal(out[name].shape)
        drawn = base * np.exp(spread * noise) if base else spread * noise
        out[name] = jnp.asarray(drawn.astype(out[name].dtype))
    for name, factor in factors.items():
        out[name] = (out[name] * factor).astype(out[name].dtype)
    return out
```

```python
from contextlib import ExitStack

import numpy as np

import concourse.bass as bass
from concourse import mybir

F32 = mybir.dt.float32
BF16 = mybir.dt.bfloat16
U16 = mybir.dt.uint16
I32 = mybir.dt.int32
ALU = mybir.AluOpType
ACT = mybir.ActivationFunctionType
AX_X = mybir.AxisListType.X

N = 1250
D = 768
E = 20000
R = 3
TP = 125
NT = N // TP
ET = E // TP
EH = ET // 2
KEYS = R * N
KT = KEYS // TP
KC = D // 128
SEMAPHORES = 150
FAR = -1.0e30


class Shared:
    pass


class Scope:

    ROOM = 40

    def __init__(self, g, ctx):
        self.g, self.nc, self.ctx = g, g.nc, ctx
        if not g.semaphores_live and g.semaphores_used > len(g.semaphore_ids) - self.ROOM:
            g.nc.all_engine_barrier(sems_to_clear=g.semaphore_ids)
            g.semaphores_used = 0

    def sb(self, name, shape, dt=F32):
        return self.ctx.enter_context(self.nc.sbuf_tensor(name, shape, dt))

    def ps(self, name, shape):
        return self.ctx.enter_context(self.nc.psum_tensor(name, shape, F32))

    def sem(self, name):
        handle = self.nc.alloc_semaphore(name, self.g.semaphore_ids[self.g.semaphores_used])
        self.g.semaphores_used += 1
        self.g.semaphores_live += 1
        self.ctx.callback(self.give_back, handle)
        return handle

    def give_back(self, handle):
        self.g.semaphores_live -= 1
        self.nc.release_semaphore(handle)

    def sems(self, name, n):
        return [self.sem(f"{name}{i}") for i in range(n)]

    def block(self):
        return self.ctx.enter_context(self.nc.Block())


def rows_of(ap, partitions, offset, width):
    return bass.AP(tensor=ap.tensor, offset=offset, ap=[[0, partitions], [1, width]])


def chain(engine, sem):
    count = [0]

    def link(instruction):
        count[0] += 1
        instruction.then_inc(sem, 1)
        engine.wait_ge(sem, count[0])

    return link


def constants(g):
    with ExitStack() as ctx:
        s = Scope(g, ctx)
        ident_zero, ident_done = s.sem("ident_zero"), s.sem("ident_done")
        block = s.block()

        @block.gpsimd
        def _(pool):
            pool.memset(g.ident[:, :], 0.0).then_inc(ident_zero, 1)
            pool.wait_ge(ident_zero, 1)
            pool.affine_select(out=g.ident[:, :], in_=g.ident[:, :], compare_op=ALU.not_equal, fill=1.0,
                               base=0, pattern=[[-1, 128]], channel_multiplier=1).then_inc(ident_done, 1)
            pool.wait_ge(ident_done, 1)


def count_edges(g, src, dst, etype):
    with ExitStack() as ctx:
        s = Scope(g, ctx)
        sb, sem = s.sb, s.sem

        edges_i = sb("edges_i", [EH, 3, 2, TP], I32)
        edges_f = sb("edges_f", [EH, 3, 2, TP], F32)
        key_f = sb("key_f", [EH, 2, TP], F32)
        span = sb("span", [EH, 2, 2], F32)
        srcT = sb("srcT", [TP, ET + 1], F32)
        keyT = sb("keyT", [TP, ET + 1], F32)
        spans = sb("spans", [KT, 2, ET], F32)
        tile_no = sb("tile_no", [KT, ET], F32)
        first_key = sb("first_key", [KT, 1], F32)
        end_key = sb("end_key", [KT, 1], F32)
        hits = sb("hits", [KT, 2, ET], F32)
        range_f = sb("range_f", [KT, 2], F32)
        range_i = sb("range_i", [KT, 2], I32)
        ranges = sb("ranges", [1, 2 * KT], I32)
        number = sb("number", [TP, KEYS], U16)
        src_hot = [sb(f"src_hot{u}", [TP, N], BF16) for u in range(2)]
        key_hot = [sb(f"key_hot{u}", [TP, TP], BF16) for u in range(2)]
        zeros = sb("zeros", [TP, 512], BF16)
        cnt = [sb(f"cnt{b}", [TP, N], F32) for b in range(2)]
        far = [sb(f"far{b}", [TP, N], BF16) for b in range(2)]
        sums = [s.ps(f"sums{b}", [TP, 3, 512]) for b in range(2)]
        turned = [s.ps(f"turned{b}", [TP, 512]) for b in range(2)]
        sums_flat = [x[:, :, :].rearrange("p a b -> p (a b)") for x in sums]

        loaded = sem("edges_loaded")
        spans_out = sem("spans_out")
        spans_in = sem("spans_in")
        ranges_out = sem("ranges_out")
        ranges_in = sem("ranges_in")
        numbers = sem("numbers")
        v_chain = sem("v_chain")
        keys_done = sem("keys_done")
        edges_turned = sem("edges_turned")
        columns_done = sem("columns_done")
        span_done = sem("span_done")
        range_done = sem("range_done")
        hot_ready = [sem(f"hot_ready{u}") for u in range(2)]
        hot_used = [sem(f"hot_used{u}") for u in range(2)]
        sums_done = sem("sums_done")
        sums_copied = sem("sums_copied")
        far_done = sem("far_done")
        far_out = [sem(f"far_out{b}") for b in range(2)]
        far_free = [sem(f"far_free{b}") for b in range(2)]
        turned_done = [sem(f"turned_done{b}") for b in range(2)]
        turned_copied = [sem(f"turned_copied{b}") for b in range(2)]

        groups = [(0, 4), (4, 8), (8, NT)]
        block = s.block()

        @block.sync
        def _(sp):
            for i, v in enumerate((src, dst, etype)):
                sp.dma_start(edges_i[:, i, :, :], v.rearrange("(c t p) -> t c p", c=2, p=TP)).then_inc(loaded, 16)
            sp.wait_ge(span_done, 2)
            for i in range(2):
                sp.dma_start(g.span_dram[i, :, :].rearrange("c t -> t c"), span[:, i, :],
                             allow_slow_non_contiguous=True).then_inc(spans_out, 16)
            sp.wait_ge(spans_out, 32)
            sp.dma_start(spans[:, :, :].rearrange("k i t -> k (i t)"),
                         rows_of(g.span_dram, KT, 0, 2 * ET)).then_inc(spans_in, 16)
            sp.wait_ge(range_done, 1)
            sp.dma_start(g.range_dram, range_i[:, :]).then_inc(ranges_out, 16)
            sp.wait_ge(ranges_out, 16)
            sp.dma_start(ranges[:, :], rows_of(g.range_dram, 1, 0, 2 * KT)).then_inc(ranges_in, 16)
            for b in range(2):
                sp.nop().then_inc(far_free[b], 1)
            with sp.Fori(0, KT // 2) as i2:
                for b in range(2):
                    sp.wait_ge(far_done, i2 * 2 + (b + 3))
                    sp.dma_start(g.far_dram[bass.ds((i2 * 2 + b) * TP, TP), :], far[b][:, :]).then_inc(far_out[b], 16)
                for b in range(2):
                    sp.wait_ge(far_out[b], i2 * 16 + 16)
                    sp.nop().then_inc(far_free[b], 1)

        @block.gpsimd
        def _(pool):
            pool.iota(number[:, :], [[1, KEYS]], base=0, channel_multiplier=0).then_inc(numbers, 1)
            pool.iota(tile_no[:, :], [[1, ET]], base=-ET, channel_multiplier=0,
                      allow_small_or_imprecise_dtypes=True).then_inc(numbers, 1)
            pool.iota(first_key[:, :], [[0, 1]], base=0, channel_multiplier=TP,
                      allow_small_or_imprecise_dtypes=True).then_inc(numbers, 1)
            pool.iota(end_key[:, :], [[0, 1]], base=TP, channel_multiplier=TP,
                      allow_small_or_imprecise_dtypes=True).then_inc(numbers, 1)
            pool.memset(srcT[:, ET:ET + 1], -1.0).then_inc(numbers, 1)
            pool.memset(keyT[:, ET:ET + 1], -1.0).then_inc(numbers, 1)
            pool.memset(zeros[:, :], 0.0).then_inc(numbers, 1)

        @block.vector
        def _(dve):
            link = chain(dve, v_chain)
            dve.wait_ge(loaded, 48)
            link(dve.tensor_copy(edges_f[:, :, :, :], edges_i[:, :, :, :]))
            link(dve.scalar_tensor_tensor(out=key_f[:, :, :], in0=edges_f[:, 1, :, :], scalar=float(R),
                                          in1=edges_f[:, 2, :, :], op0=ALU.mult, op1=ALU.add))
            dve.tensor_reduce(out=span[:, 0, :], in_=key_f[:, :, :], op=ALU.min, axis=AX_X).then_inc(span_done, 1)
            dve.tensor_reduce(out=span[:, 1, :], in_=key_f[:, :, :], op=ALU.max, axis=AX_X).then_inc(span_done, 1)
            dve.nop().then_inc(keys_done, 1)
            dve.wait_ge(edges_turned, 1)
            dve.tensor_copy(srcT[:, 0:ET], turned[0][:, 0:ET]).then_inc(columns_done, 1)
            dve.tensor_copy(keyT[:, 0:ET], turned[1][:, 0:ET]).then_inc(columns_done, 1)
            dve.wait_ge(spans_in, 16)
            dve.wait_ge(numbers, 7)
            link(dve.scalar_tensor_tensor(out=hits[:, 0, :], in0=spans[:, 1, :], scalar=first_key[:, 0:1],
                                          in1=tile_no[:, :], op0=ALU.is_ge, op1=ALU.mult))
            link(dve.tensor_scalar(tile_no[:, :], tile_no[:, :], float(ET + 1), None, op0=ALU.add))
            link(dve.scalar_tensor_tensor(out=hits[:, 1, :], in0=spans[:, 0, :], scalar=end_key[:, 0:1],
                                          in1=tile_no[:, :], op0=ALU.is_lt, op1=ALU.mult))
            link(dve.tensor_reduce(out=range_f[:, 0:1], in_=hits[:, 0, :], op=ALU.min, axis=AX_X))
            link(dve.tensor_reduce(out=range_f[:, 1:2], in_=hits[:, 1, :], op=ALU.max, axis=AX_X))
            link(dve.tensor_scalar(range_f[:, 0:1], range_f[:, 0:1], float(ET), float(ET - 1),
                                   op0=ALU.add, op1=ALU.min))
            link(dve.scalar_tensor_tensor(out=range_f[:, 1:2], in0=range_f[:, 0:1], scalar=1.0,
                                          in1=range_f[:, 1:2], op0=ALU.add, op1=ALU.max))
            dve.tensor_copy(range_i[:, :], range_f[:, :]).then_inc(range_done, 1)
            dve.wait_ge(columns_done, 2)
            dve.wait_ge(ranges_in, 16)
            for b in range(2):
                dve.nop().then_inc(far_done, 1)
            turn = dve.alloc_register("hot_turn")
            dve.reg_mov(turn, 1)
            with dve.Fori(0, KT // 2) as i2:
                for b in range(2):
                    lo = dve.value_load(ranges[0:1, bass.ds((i2 * 2 + b) * 2, 1)], min_val=0, max_val=ET - 1)
                    hi = dve.value_load(ranges[0:1, bass.ds((i2 * 2 + b) * 2 + 1, 1)], min_val=1, max_val=ET)
                    with dve.Fori(lo, hi, 2) as t:
                        for u in range(2):
                            dve.wait_ge(hot_used[u], turn)
                            dve.tensor_scalar(src_hot[u][:, :], number[:, 0:N], srcT[:, bass.ds(t + u, 1)], None,
                                              op0=ALU.is_equal)
                            dve.tensor_scalar(key_hot[u][:, :], number[:, bass.ds((i2 * 2 + b) * TP, TP)],
                                              keyT[:, bass.ds(t + u, 1)], None,
                                              op0=ALU.is_equal).then_inc(hot_ready[u], 1)
                        dve.reg_add(turn, turn, 1)
                    dve.wait_ge(sums_copied, i2 * 2 + (b + 1))
                    dve.wait_ge(far_free[b], i2 + 1)
                    dve.tensor_scalar(far[b][:, :], cnt[b][:, :], 0.5, FAR, op0=ALU.is_lt,
                                      op1=ALU.mult).then_inc(far_done, 1)

        @block.tensor
        def _(pe):
            pe.wait_ge(keys_done, 1)
            for c in range(2):
                pe.transpose(turned[0][:, c * EH:(c + 1) * EH], edges_f[:, 0, c, :], g.ident[0:EH, 0:EH])
                last = pe.transpose(turned[1][:, c * EH:(c + 1) * EH], key_f[:, c, :], g.ident[0:EH, 0:EH])
            last.then_inc(edges_turned, 1)
            pe.wait_ge(columns_done, 2)
            pe.wait_ge(numbers, 7)
            pe.wait_ge(ranges_in, 16)
            for b in range(2):
                pe.nop().then_inc(hot_used[b], 1)
                pe.nop().then_inc(turned_copied[b], 1)
            turn = pe.alloc_register("sum_turn")
            pe.reg_mov(turn, 1)
            with pe.Fori(0, KT // 2) as i2:
                for b in range(2):
                    lo = pe.value_load(ranges[0:1, bass.ds((i2 * 2 + b) * 2, 1)], min_val=0, max_val=ET - 1)
                    hi = pe.value_load(ranges[0:1, bass.ds((i2 * 2 + b) * 2 + 1, 1)], min_val=1, max_val=ET)
                    for k in range(3):
                        w = min(512, N - 512 * k)
                        pe.matmul(sums_flat[b][:, 512 * k:512 * k + w], zeros[:, 0:TP], zeros[:, 0:w],
                                  start=True, stop=False, skip_group_check=True)
                    with pe.Fori(lo, hi, 2) as t:
                        for u in range(2):
                            pe.wait_ge(hot_ready[u], turn)
                            for k in range(3):
                                w = min(512, N - 512 * k)
                                last = pe.matmul(sums_flat[b][:, 512 * k:512 * k + w], key_hot[u][:, :],
                                                 src_hot[u][:, 512 * k:512 * k + w],
                                                 start=False, stop=False, skip_group_check=True)
                            last.then_inc(hot_used[u], 1)
                        pe.reg_add(turn, turn, 1)
                    pe.matmul(sums_flat[b][:, 0:1], zeros[:, 0:TP], zeros[:, 0:1], start=False, stop=True,
                              skip_group_check=True).then_inc(sums_done, 1)
                    pe.wait_ge(sums_copied, i2 * 2 + (b + 1))
                    for i, (s0, s1) in enumerate(groups):
                        n = 3 * b + i
                        pe.wait_ge(turned_copied[n % 2], i2 * 3 + (n // 2 + 1))
                        for s in range(s0, s1):
                            last = pe.transpose(turned[n % 2][:, (s - s0) * TP:(s - s0 + 1) * TP],
                                                cnt[b][:, s * TP:(s + 1) * TP], g.ident[0:TP, 0:TP])
                        last.then_inc(turned_done[n % 2], 1)

        @block.scalar
        def _(act):
            with act.Fori(0, KT // 2) as i2:
                for b in range(2):
                    act.wait_ge(sums_done, i2 * 2 + (b + 1))
                    act.wait_ge(far_done, i2 * 2 + (b + 1))
                    act.activation(cnt[b][:, :], sums_flat[b][:, 0:N], ACT.Copy).then_inc(sums_copied, 1)
                    for i, (s0, s1) in enumerate(groups):
                        n = 3 * b + i
                        act.wait_ge(turned_done[n % 2], i2 * 3 + (n // 2 + 1))
                        act.activation(g.counts[:, s0:s1, bass.ds((i2 * 2 + b) * TP, TP)],
                                       turned[n % 2][:, 0:(s1 - s0) * TP].rearrange("p (s k) -> p s k", k=TP),
                                       ACT.Copy).then_inc(turned_copied[n % 2], 1)
            act.nop()


def turn_tile(pe, g, out, rows, t, tiled):
    for c in range(KC):
        last = pe.transpose(out[c // 3][:, (c % 3) * TP:(c % 3 + 1) * TP], rows[:, t, c * 128:(c + 1) * 128],
                            g.ident[0:TP, 0:TP])
    last.then_inc(tiled, 1)


def normalize(g, tag, src, dst, dstT, gamma=None, beta=None, eps=1e-5):
    with ExitStack() as ctx:
        s = Scope(g, ctx)
        parts = s.sb(f"{tag}_parts", [TP, NT, 2, 6])
        mean_var = s.sb(f"{tag}_mean_var", [TP, NT, 2])
        var = s.sb(f"{tag}_var", [TP, NT])
        inv = s.sb(f"{tag}_inv", [TP, NT])
        std_inv = s.sb(f"{tag}_std_inv", [TP, NT])
        square = s.sb(f"{tag}_square", [TP, NT])
        affine = s.sb(f"{tag}_affine", [TP, 2, D]) if gamma is not None else None
        banks = [[s.ps(f"{tag}_turn{i}{j}", [128, 512]) for j in range(2)] for i in range(2)] if dstT is not None else []
        v_chain, inv_done, root_done = s.sem(f"{tag}_chain"), s.sem(f"{tag}_inv_done"), s.sem(f"{tag}_root_done")
        rows_done, turned, copied = s.sem(f"{tag}_rows"), s.sem(f"{tag}_turned"), s.sem(f"{tag}_copied")
        affine_in = s.sem(f"{tag}_affine_in")
        block = s.block()

        if gamma is not None:
            @block.sync
            def _(sp):
                for i, v in enumerate((gamma, beta)):
                    sp.dma_start(affine[:, i, :], rows_of(v, TP, 0, D)).then_inc(affine_in, 16)

        @block.vector
        def _(dve):
            link = chain(dve, v_chain)
            for t in range(NT):
                for i in range(2):
                    last = dve.bn_stats(parts[:, t, i, :], src[:, t, i * 384:(i + 1) * 384])
            link(last)
            for t in range(NT):
                last = dve.bn_aggr(mean_var[:, t, :], parts[:, t, :, :].rearrange("p a b -> p (a b)"))
            link(last)
            link(dve.tensor_scalar(var[:, :], mean_var[:, :, 1], eps, None, op0=ALU.add))
            dve.reciprocal(inv[:, :], var[:, :]).then_inc(inv_done, 1)
            dve.wait_ge(root_done, 1)
            link(dve.tensor_tensor(square[:, :], std_inv[:, :], std_inv[:, :], op=ALU.mult))
            link(dve.tensor_tensor(square[:, :], square[:, :], var[:, :], op=ALU.mult))
            link(dve.tensor_scalar(square[:, :], square[:, :], -0.5, 1.5, op0=ALU.mult, op1=ALU.add))
            link(dve.tensor_tensor(std_inv[:, :], std_inv[:, :], square[:, :], op=ALU.mult))
            if gamma is None:
                for t in range(NT):
                    dve.tensor_scalar(dst[:, t, :], src[:, t, :], mean_var[:, t, 0:1], std_inv[:, t:t + 1],
                                      op0=ALU.subtract, op1=ALU.mult).then_inc(rows_done, 1)
            else:
                dve.wait_ge(affine_in, 32)
                for t in range(NT):
                    link(dve.tensor_scalar(dst[:, t, :], src[:, t, :], mean_var[:, t, 0:1], std_inv[:, t:t + 1],
                                           op0=ALU.subtract, op1=ALU.mult))
                    link(dve.tensor_tensor(dst[:, t, :], dst[:, t, :], affine[:, 0, :], op=ALU.mult))
                    dve.tensor_tensor(dst[:, t, :], dst[:, t, :], affine[:, 1, :], op=ALU.add).then_inc(rows_done, 1)
            dve.wait_ge(rows_done, NT)

        @block.scalar
        def _(act):
            act.wait_ge(inv_done, 1)
            act.activation(std_inv[:, :], inv[:, :], ACT.Sqrt).then_inc(root_done, 1)
            if dstT is not None:
                for t in range(NT):
                    act.wait_ge(turned, t + 1)
                    for j in range(2):
                        act.activation(dstT[:, 3 * j:3 * j + 3, t * TP:(t + 1) * TP],
                                       banks[t % 2][j][:, 0:3 * TP].rearrange("p (c t) -> p c t", t=TP),
                                       ACT.Copy).then_inc(copied, 1)
                act.wait_ge(copied, 2 * NT)

        if dstT is not None:
            @block.tensor
            def _(pe):
                for t in range(NT):
                    pe.wait_ge(rows_done, t + 1)
                    if t >= 2:
                        pe.wait_ge(copied, 2 * (t - 1))
                    turn_tile(pe, g, banks[t % 2], dst, t, turned)


def save_counts(g):
    with ExitStack() as ctx:
        s = Scope(g, ctx)
        saved = s.sem("counts_saved")
        block = s.block()

        @block.sync
        def _(sp):
            sp.dma_start(g.counts_dram, g.counts[:, :, :]).then_inc(saved, 16)
            sp.wait_ge(saved, 16)


def merge_edges(g):
    with ExitStack() as ctx:
        s = Scope(g, ctx)
        masks = [s.sb(f"masks{i}", [TP, R, N], BF16) for i in range(2)]
        masks_in, merged, summed = s.sems("masks_in", 2), s.sem("masks_merged"), s.sem("counts_summed")
        v_chain = s.sem("merge_vc")
        block = s.block()

        @block.sync
        def _(sp):
            for t in range(NT):
                if t >= 2:
                    sp.wait_ge(merged, t - 1)
                sp.dma_start(masks[t % 2][:, :, :], g.far_dram[t * TP * R:(t + 1) * TP * R, :]
                             .rearrange("(d r) s -> d r s", r=R)).then_inc(masks_in[t % 2], 16)

        @block.vector
        def _(dve):
            link = chain(dve, v_chain)
            for t in range(NT):
                dve.wait_ge(masks_in[t % 2], t // 2 * 16 + 16)
                link(dve.tensor_tensor(g.far_u[:, t, :], masks[t % 2][:, 0, :], masks[t % 2][:, 1, :], op=ALU.max))
                dve.tensor_tensor(g.far_u[:, t, :], g.far_u[:, t, :], masks[t % 2][:, 2, :],
                                  op=ALU.max).then_inc(merged, 1)
                by_rel = g.counts[:, t, :].rearrange("p (d r) -> p r d", r=R)
                link(dve.tensor_tensor(g.counts_u[:, t, :], by_rel[:, 0, :], by_rel[:, 1, :], op=ALU.add))
                dve.tensor_tensor(g.counts_u[:, t, :], g.counts_u[:, t, :], by_rel[:, 2, :],
                                  op=ALU.add).then_inc(summed, 1)
            dve.wait_ge(merged, NT)
            dve.wait_ge(summed, NT)


def project_gat(g, hT, w_fc, w_res, attn_l, attn_r, ft, res, ks, qd):
    H, DH = 12, 64
    with ExitStack() as ctx:
        s = Scope(g, ctx)
        w2 = s.sb("gat_w2", [DH, 2, 2 * DH])
        pair = s.sb("gat_pair", [128, 2, 128])
        attn = s.sb("gat_attn", [2 * H, DH])
        attnT = s.sb("gat_attnT", [DH, 2 * H])
        score_w = s.sb("gat_score_w", [128, KC, 2, H])
        score_flat = score_w[:, :, :, :].rearrange("p c l h -> p (c l h)")
        out_ps = [s.ps(f"gat_out{i}", [128, 3, 512]) for i in range(2)]
        chunks = [o[0:TP, :, :].rearrange("p a b -> p (a b)").rearrange("p (c i e) -> p c i e", c=KC, i=2)
                  for o in out_ps]
        score_ps = [s.ps(f"gat_score{i}", [128, 512]) for i in range(2)]
        w_in = s.sem("gat_w_in")
        zeroed, w_turned, w_copied = s.sem("gat_zeroed"), s.sem("gat_w_turned"), s.sem("gat_w_copied")
        s_made, s_copied = s.sem("gat_s_made"), s.sem("gat_s_copied")
        made, values_out, rest_out = s.sem("gat_made"), s.sem("gat_values_out"), s.sem("gat_rest_out")
        block = s.block()

        @block.sync
        def _(sp):
            for i, w in enumerate((w_fc, w_res)):
                for k in range(2):
                    sp.dma_start(w2[:, i, k * DH:(k + 1) * DH], w).then_inc(w_in, 16)
            for i, a in enumerate((attn_l, attn_r)):
                sp.dma_start(attn[i * H:(i + 1) * H, :], a).then_inc(w_in, 16)

        @block.gpsimd
        def _(pool):
            pool.memset(pair[:, :, :], 0.0).then_inc(zeroed, 1)
            pool.memset(score_w[:, :, :, :], 0.0).then_inc(zeroed, 1)
            pool.memset(ft[:, :, :, DH:DH + 1], 1.0).then_inc(zeroed, 1)

        @block.vector
        def _(dve):
            dve.wait_ge(w_turned, 1)
            dve.wait_ge(zeroed, 2)
            for i in range(2):
                for k in range(2):
                    dve.tensor_copy(pair[k * DH:(k + 1) * DH, i, k * DH:(k + 1) * DH],
                                    out_ps[0][k * DH:(k + 1) * DH, i, 0:DH])
            dve.tensor_copy(attnT[:, :], out_ps[0][0:DH, 2, 0:2 * H]).then_inc(w_copied, 1)
            dve.wait_ge(s_made, 1)
            for k in range(2):
                for lr in range(2):
                    first = lr * H + k
                    last = dve.tensor_copy(score_flat[k * DH:(k + 1) * DH, first:first + 26 * (KC - 1) + 1:26],
                                           score_ps[0][k * DH:(k + 1) * DH, lr * H + k:lr * H + H:2])
            last.then_inc(s_copied, 1)
            for t in range(NT):
                dve.wait_ge(made, t + 1)
                dve.tensor_copy(ks[:, t, :], score_ps[t % 2][0:TP, 0:H])
                dve.tensor_copy(qd[:, t, :], score_ps[t % 2][0:TP, H:2 * H]).then_inc(rest_out, 1)

        @block.tensor
        def _(pe):
            pe.wait_ge(w_in, 96)
            for i in range(2):
                pe.transpose(out_ps[0][:, i, 0:DH], w2[:, i, :], g.ident[0:DH, 0:DH])
            pe.transpose(out_ps[0][0:DH, 2, 0:2 * H], attn[:, :], g.ident[0:2 * H, 0:2 * H]).then_inc(w_turned, 1)
            pe.wait_ge(w_copied, 1)
            pe.matmul(score_ps[0][:, 0:2 * H], w2[:, 0, :], attnT[:, :], start=True, stop=True).then_inc(s_made, 1)
            pe.wait_ge(s_copied, 1)
            for t in range(NT):
                if t >= 2:
                    pe.wait_ge(values_out, t - 1)
                    pe.wait_ge(rest_out, t - 1)
                for c in range(KC):
                    x_c = hT[:, c, t * TP:(t + 1) * TP]
                    pe.matmul(out_ps[t % 2][0:TP, c // 2, (c % 2) * 256:(c % 2 + 1) * 256], x_c,
                              pair[:, :, :].rearrange("p i e -> p (i e)"), start=True, stop=True)
                    last = pe.matmul(score_ps[t % 2][0:TP, 0:2 * H], x_c,
                                     score_w[:, c, :, :].rearrange("p l h -> p (l h)"),
                                     start=(c == 0), stop=(c == KC - 1))
                last.then_inc(made, 1)

        @block.scalar
        def _(act):
            for t in range(NT):
                act.wait_ge(made, t + 1)
                act.activation(res[:, t, :].rearrange("p (c e) -> p c e", c=KC), chunks[t % 2][:, :, 1, :], ACT.Copy)
                act.activation(ft[:, t, :, 0:DH].rearrange("p (c k) e -> p c k e", k=2),
                               chunks[t % 2][:, :, 0, :].rearrange("p c (k e) -> p c k e", k=2),
                               ACT.Copy).then_inc(values_out, 1)
            act.wait_ge(values_out, NT)


def attend(g, tag, heads, width, span, far_of, ks, qd, value_of, finish):
    rels = ks.shape[2] // heads
    CH = heads * rels
    with ExitStack() as outer:
        so = Scope(g, outer)
        least = so.sb(f"{tag}_least", [TP, CH])
        most = so.sb(f"{tag}_most", [TP, NT, CH])
        leaky = so.sb(f"{tag}_leaky", [TP, NT, CH])
        top = so.sb(f"{tag}_top", [TP, NT, heads])
        shifted = so.sb(f"{tag}_shifted", [TP, NT, 2, CH])
        ks_low = so.sb(f"{tag}_ks_low", [TP, NT, CH])
        with ExitStack() as ctx:
            s = Scope(g, ctx)
            rowsT = s.sb(f"{tag}_rowsT", [CH, N])
            low = s.sb(f"{tag}_low", [CH, 1])
            row = [s.sb(f"{tag}_row{i}", [TP, N]) for i in range(3)]
            junk = [s.sb(f"{tag}_junk{i}", [TP, N]) for i in range(2)]
            far = None if rels == 1 else [s.sb(f"{tag}_far{i}", [TP, NT, N], BF16) for i in range(2)]
            turn_ps = s.ps(f"{tag}_turn", [CH, 3, 512])
            turned, copied, low_done, out_done = s.sem(f"{tag}_a"), s.sem(f"{tag}_b"), s.sem(f"{tag}_c"), s.sem(f"{tag}_d")
            low_out, least_in = s.sem(f"{tag}_e"), s.sem(f"{tag}_f")
            row_in, row_used = s.sems(f"{tag}_row_in", 3), s.sem(f"{tag}_row_used")
            far_in = s.sems(f"{tag}_far_in", 2)
            junked, v_chain, low_scaled = s.sem(f"{tag}_junked"), s.sem(f"{tag}_vc"), s.sem(f"{tag}_low_scaled")
            block = s.block()

            @block.tensor
            def _(pe):
                for t in range(NT):
                    last = pe.transpose(turn_ps[:, t // 4, (t % 4) * TP:(t % 4 + 1) * TP], ks[:, t, :],
                                        g.ident[0:TP, 0:TP])
                last.then_inc(turned, 1)

            @block.scalar
            def _(act):
                act.activation(ks_low[:, :, :], ks[:, :, :], ACT.Copy, scale=0.2).then_inc(low_scaled, 1)
                act.wait_ge(turned, 1)
                act.activation(rowsT[:, 0:8 * TP].rearrange("p (a b) -> p a b", a=2), turn_ps[:, 0:2, 0:4 * TP],
                               ACT.Copy).then_inc(copied, 1)
                act.activation(rowsT[:, 8 * TP:N], turn_ps[:, 2, 0:2 * TP], ACT.Copy).then_inc(copied, 1)
                act.wait_ge(low_scaled, 1)

            @block.sync
            def _(sp):
                sp.wait_ge(copied, 2)
                sp.dma_start(g.rows_dram[0:CH, :], rowsT[:, :]).then_inc(out_done, 16)
                if rels > 1:
                    for r in range(2):
                        sp.dma_start(far[r][:, :, :], far_of(r)).then_inc(far_in[r], 16)
                sp.wait_ge(out_done, 16)
                for c in range(CH):
                    if c >= 3:
                        sp.wait_ge(row_used, c - 2)
                    sp.dma_start(row[c % 3][:, :], rows_of(g.rows_dram, TP, c * N, N)).then_inc(row_in[c % 3], 16)
                    if c == 0:
                        sp.wait_ge(low_done, 1)
                        sp.dma_start(g.low_dram[0:CH, :], low[:, :]).then_inc(low_out, 16)
                        sp.wait_ge(low_out, 16)
                        sp.dma_start(least[:, :], rows_of(g.low_dram, TP, 0, CH)).then_inc(least_in, 16)
                    if rels > 1 and c // heads == 1 and c % heads == 0:
                        sp.wait_ge(row_used, heads)
                        sp.dma_start(far[0][:, :, :], far_of(2)).then_inc(far_in[0], 16)

            @block.vector
            def _(dve):
                link = chain(dve, v_chain)
                dve.wait_ge(copied, 2)
                dve.tensor_reduce(out=low[:, :], in_=rowsT[:, :], op=ALU.min, axis=AX_X).then_inc(low_done, 1)
                for c in range(CH):
                    r = c // heads
                    dve.wait_ge(row_in[c % 3], c // 3 * 16 + 16)
                    if rels > 1 and c % heads == 0:
                        dve.wait_ge(far_in[r % 2], r // 2 * 16 + 16)
                    for t in range(NT):
                        n = c * NT + t
                        if n >= 2:
                            dve.wait_ge(junked, n - 1)
                        mask = g.far_u[:, t, :] if rels == 1 else far[r % 2][:, t, :]
                        last = dve.tensor_tensor_reduce(out=junk[n % 2][:, :], in0=mask, in1=row[c % 3][:, :],
                                                        scale=1.0, scalar=3 * FAR, op0=ALU.add, op1=ALU.max,
                                                        accum_out=most[:, t, c:c + 1])
                        last.then_inc(junked, 1)
                    dve.wait_ge(junked, (c + 1) * NT)
                    dve.nop().then_inc(row_used, 1)
                dve.wait_ge(least_in, 16)
                all_tiles = least[:, :].unsqueeze(1).to_broadcast([TP, NT, CH])
                link(dve.tensor_tensor(most[:, :, :], most[:, :, :], all_tiles, op=ALU.max))
                link(dve.tensor_tensor(most[:, :, :], most[:, :, :], qd[:, :, :], op=ALU.add))
                link(dve.scalar_tensor_tensor(out=leaky[:, :, :], in0=most[:, :, :], scalar=0.2, in1=most[:, :, :],
                                              op0=ALU.mult, op1=ALU.max))
                link(dve.tensor_copy(top[:, :, :], leaky[:, :, 0:heads]))
                for r in range(1, rels):
                    link(dve.tensor_tensor(top[:, :, :], top[:, :, :], leaky[:, :, r * heads:(r + 1) * heads],
                                           op=ALU.max))
                for r in range(rels):
                    at = slice(r * heads, (r + 1) * heads)
                    link(dve.tensor_tensor(shifted[:, :, 0, at], qd[:, :, at], top[:, :, :], op=ALU.subtract))
                    link(dve.scalar_tensor_tensor(out=shifted[:, :, 1, at], in0=qd[:, :, at], scalar=0.2,
                                                  in1=top[:, :, :], op0=ALU.mult, op1=ALU.subtract))

        units = [(h, d) for h in range(heads) for d in range(0, NT, span)]
        per_bank = max(1, 512 // (width + 1))
        banks_of = -(-(width + 1) // 512)
        nbanks = -(-span // per_bank) if banks_of == 1 else span * banks_of
        W = span * TP
        steps = [(u, r, t) for u in range(len(units)) for t in range(NT) for r in range(rels)]
        per_unit = NT * rels
        with ExitStack() as ctx:
            s = Scope(g, ctx)
            rows = [s.sb(f"{tag}_rows{i}", [TP, rels, 2, W]) for i in range(2)]
            shiftedT = rows[1][0:2 * CH, :, :, :].rearrange("p r i w -> p (r i w)")[:, 0:N]
            high = [s.sb(f"{tag}_high{i}", [TP, W]) for i in range(3)]
            lowb = [s.sb(f"{tag}_lowb{i}", [TP, W]) for i in range(3)]
            wts = [s.sb(f"{tag}_wts{i}", [TP, W]) for i in range(3)]
            recip = s.sb(f"{tag}_recip", [TP, 2, span])
            stream = None if value_of else [s.sb(f"{tag}_values{i}", [TP, width + 1]) for i in range(4)]
            acc = [s.ps(f"{tag}_acc{i}", [TP, nbanks, 512]) for i in range(2)]
            turned, copied, out_done = s.sem(f"{tag}_g"), s.sem(f"{tag}_h"), s.sem(f"{tag}_i")
            rows_in, rows_used = s.sems(f"{tag}_rows_in", 2), s.sem(f"{tag}_rows_used")
            exp_done, max_done, wts_done, wts_used = (s.sem(f"{tag}_{n}") for n in ("exp", "max", "wts", "wts_used"))
            value_in, acc_done, acc_out = s.sems(f"{tag}_value_in", 4), s.sem(f"{tag}_acc_done"), s.sem(f"{tag}_acc_out")
            v_chain, ones = s.sem(f"{tag}_vc2"), s.sem(f"{tag}_ones")
            counts = s.sb(f"{tag}_counts", [TP, NT, KEYS], U16) if rels > 1 else g.counts_u
            counts_in = s.sem(f"{tag}_counts_in")
            turn_ps2 = acc[1][0:2 * CH, :, :] if nbanks >= 3 else s.ps(f"{tag}_turn2", [2 * CH, 3, 512])
            block = s.block()

            def counts_of(r, t, at, w):
                if rels == 1:
                    return counts[:, t, at:at + w]
                return counts[:, t, :].rearrange("p (d r) -> p r d", r=R)[:, r, at:at + w]

            def tile_of(u, d):
                if banks_of == 1:
                    o = (d % per_bank) * (width + 1)
                    return [(acc[u % 2][:, d // per_bank, o:o + width + 1], 0, width + 1)]
                return [(acc[u % 2][:, d * banks_of + b, 0:min(512, width + 1 - 512 * b)], 512 * b,
                         min(512 * b + 512, width + 1)) for b in range(banks_of)]

            @block.tensor
            def _(pe):
                for t in range(NT):
                    last = pe.transpose(turn_ps2[:, t // 4, (t % 4) * TP:(t % 4 + 1) * TP],
                                        shifted[:, t, :, :].rearrange("p a c -> p (a c)"), g.ident[0:TP, 0:TP])
                last.then_inc(turned, 1)
                pe.wait_ge(copied, 2)
                for i, (u, r, t) in enumerate(steps):
                    h, d0 = units[u]
                    n_tiles = min(span, NT - d0)
                    first, final = i % per_unit == 0, i % per_unit == per_unit - 1
                    if first and u >= 2:
                        pe.wait_ge(acc_out, u - 1)
                    if value_of:
                        v = value_of(h, t)
                    else:
                        pe.wait_ge(value_in[i % 4], i // 4 * 16 + 16)
                        v = stream[i % 4][:, :]
                        if i == 0:
                            pe.wait_ge(ones, 4)
                    pe.wait_ge(wts_done, i + 1)
                    for d in range(n_tiles):
                        for o, c0, c1 in tile_of(u, d):
                            opens = first and (banks_of > 1 or d % per_bank == 0)
                            last = pe.matmul(o, wts[i % 3][:, d * TP:(d + 1) * TP], v[:, c0:c1],
                                             start=opens, stop=final, skip_group_check=True)
                    last.then_inc(wts_used, 1)

            @block.scalar
            def _(act):
                act.wait_ge(turned, 1)
                act.activation(shiftedT[:, 0:8 * TP].rearrange("p (a b) -> p a b", a=2), turn_ps2[:, 0:2, 0:4 * TP],
                               ACT.Copy).then_inc(copied, 1)
                act.activation(shiftedT[:, 8 * TP:N], turn_ps2[:, 2, 0:2 * TP], ACT.Copy).then_inc(copied, 1)
                for i, (u, r, t) in enumerate(steps):
                    h, d0 = units[u]
                    w = min(span, NT - d0) * TP
                    c = r * heads + h
                    if i % per_unit == 0:
                        act.wait_ge(rows_in[u % 2], u // 2 * 16 * rels + 16 * rels)
                    if i >= 3:
                        act.wait_ge(max_done, i - 2)
                        act.wait_ge(wts_done, i - 2)
                    act.activation(high[i % 3][:, 0:w], rows[u % 2][:, r, 0, 0:w], ACT.Exp, bias=ks[:, t, c:c + 1])
                    act.activation(lowb[i % 3][:, 0:w], rows[u % 2][:, r, 1, 0:w], ACT.Exp,
                                   bias=ks_low[:, t, c:c + 1]).then_inc(exp_done, 1)

            def take_out(dve, link, u):
                h, d0 = units[u]
                n_tiles = min(span, NT - d0)
                dve.wait_ge(wts_used, (u + 1) * per_unit)
                for d in range(n_tiles):
                    o, c0, c1 = tile_of(u, d)[-1]
                    last = dve.tensor_scalar(recip[:, u % 2, d:d + 1], o[:, width - c0:width - c0 + 1], 1e-16, None,
                                             op0=ALU.add)
                link(last)
                link(dve.reciprocal(recip[:, u % 2, 0:n_tiles], recip[:, u % 2, 0:n_tiles]))
                for d in range(n_tiles):
                    for o, c0, c1 in tile_of(u, d):
                        c1 = min(c1, width)
                        last = finish(dve, h, d0 + d, c0, c1, o[:, 0:c1 - c0], recip[:, u % 2, d:d + 1])
                last.then_inc(acc_out, 1)

            @block.vector
            def _(dve):
                link = chain(dve, v_chain)

                def larger(i):
                    u, r, t = steps[i]
                    w = min(span, NT - units[u][1]) * TP
                    dve.wait_ge(exp_done, i + 1)
                    dve.tensor_tensor(high[i % 3][:, 0:w], high[i % 3][:, 0:w], lowb[i % 3][:, 0:w],
                                      op=ALU.max).then_inc(max_done, 1)

                larger(0)
                if rels > 1:
                    dve.wait_ge(counts_in, 16)
                for i, (u, r, t) in enumerate(steps):
                    h, d0 = units[u]
                    w = min(span, NT - d0) * TP
                    if i + 1 < len(steps):
                        larger(i + 1)
                    dve.wait_ge(max_done, i + 1)
                    if i >= 3:
                        dve.wait_ge(wts_used, i - 2)
                    dve.scalar_tensor_tensor(out=wts[i % 3][:, 0:w], in0=high[i % 3][:, 0:w], scalar=1.0,
                                             in1=counts_of(r, t, d0 * TP, w), op0=ALU.min,
                                             op1=ALU.mult).then_inc(wts_done, 1)
                    if i % per_unit == 2 and u >= 1:
                        take_out(dve, link, u - 1)
                take_out(dve, link, len(units) - 1)

            @block.sync
            def _(sp):
                if rels > 1:
                    sp.dma_start(counts[:, :, :], g.counts_dram).then_inc(counts_in, 16)
                sp.wait_ge(copied, 2)
                sp.dma_start(g.rows_dram[0:2 * CH, :], shiftedT).then_inc(out_done, 16)
                sp.wait_ge(out_done, 16)

                def load_rows(u):
                    h, d0 = units[u]
                    w = min(span, NT - d0) * TP
                    for r in range(rels):
                        src = bass.AP(tensor=g.rows_dram.tensor, offset=(r * heads + h) * N + d0 * TP,
                                      ap=[[0, TP], [CH * N, 2], [1, w]])
                        sp.dma_start(rows[u % 2][:, r, :, 0:w], src).then_inc(rows_in[u % 2], 16)

                load_rows(0)
                if len(units) > 1:
                    load_rows(1)
                for i, (u, r, t) in enumerate(steps):
                    if not value_of:
                        if i >= 4:
                            sp.wait_ge(wts_used, i - 3)
                        h, d0 = units[u]
                        sp.dma_start(stream[i % 4][:, 0:width],
                                     g.values_dram[r, t * TP:(t + 1) * TP, h * width:(h + 1) * width])\
                            .then_inc(value_in[i % 4], 16)
                    if i % per_unit == 4 and u >= 1 and u + 1 < len(units):
                        sp.wait_ge(exp_done, u * per_unit)
                        load_rows(u + 1)

            @block.gpsimd
            def _(pool):
                if not value_of:
                    for i in range(4):
                        pool.memset(stream[i][:, width:width + 1], 1.0).then_inc(ones, 1)


def gat_layer(g, src, dst, etype, w_fc, w_res, attn_l, attn_r):
    nc = g.nc
    H, DH = 12, 64
    with ExitStack() as ctx:
        g.counts = Scope(g, ctx).sb("counts", [TP, NT, KEYS], U16)
        count_edges(g, src, dst, etype)
        save_counts(g)
        merge_edges(g)
    with ExitStack() as ctx:
        s = Scope(g, ctx)
        ks = s.sb("gat_ks", [TP, NT, H])
        qd = s.sb("gat_qd", [TP, NT, H])
        res = s.sb("gat_res", [TP, NT, D])
        with ExitStack() as inner:
            si = Scope(g, inner)
            ft = si.sb("gat_ft", [TP, NT, H, DH + 1])
            with ExitStack() as inmost:
                hT = Scope(g, inmost).sb("gat_hT", [128, KC, N])
                normalize(g, "gat_ln", g.x, res, hT)
                project_gat(g, hT, w_fc, w_res, attn_l, attn_r, ft, res, ks, qd)

            def finish(dve, h, d, c0, c1, sums, recip):
                at = slice(h * DH, (h + 1) * DH)
                return dve.scalar_tensor_tensor(out=res[:, d, at], in0=sums, scalar=recip, in1=res[:, d, at],
                                                op0=ALU.mult, op1=ALU.add)

            attend(g, "gat", H, DH, NT, None, ks, qd,
                   lambda h, t: ft[:, t, h, :], finish)
        added = s.sem("gat_added")
        block = s.block()

        @block.vector
        def _(dve):
            for t in range(NT):
                dve.scalar_tensor_tensor(out=g.x[:, t, :], in0=res[:, t, :], scalar=0.0, in1=g.x[:, t, :],
                                         op0=ALU.max, op1=ALU.add).then_inc(added, 1)
            dve.wait_ge(added, NT)


def scratch(g):
    nc = g.nc
    g.far_dram = nc.dram_tensor("far_dram", (KEYS, N), BF16).ap()
    g.counts_dram = nc.dram_tensor("counts_dram", (TP, NT, KEYS), U16).ap()
    g.span_dram = nc.dram_tensor("span_dram", (2, 2, EH), F32).ap()
    g.range_dram = nc.dram_tensor("range_dram", (KT, 2), I32).ap()
    g.rows_dram = nc.dram_tensor("rows_dram", (24, N), F32).ap()
    g.low_dram = nc.dram_tensor("low_dram", (12, 1), F32).ap()
    g.x_dram = nc.dram_tensor("x_dram", (TP, NT, D), F32).ap()
    g.score_dram = nc.dram_tensor("score_dram", (NT, TP), F32).ap()
    g.values_dram = nc.dram_tensor("values_dram", (R, N, D), F32).ap()


TOKENS = [(0, 417), (417, 834), (834, N)]


def route(g, hT, router_w, gate, gateT):
    X = router_w.shape[0]
    with ExitStack() as ctx:
        s = Scope(g, ctx)
        rw = s.sb("route_w", [X, D])
        rwT = s.sb("route_wT", [128, KC, X])
        logits = s.sb("route_logits", [TP, NT, X])
        pairs = s.sb("route_pairs", [TP, NT, X, X])
        ties = s.sb("route_ties", [TP, NT, X, X])
        before = s.sb("route_before", [TP, X, X])
        rank = s.sb("route_rank", [TP, NT, X])
        top = s.sb("route_top", [TP, NT])
        turn_ps = s.ps("route_turn", [128, 512])
        logit_ps = s.ps("route_ps", [TP, 512])
        gate_ps = s.ps("route_gate", [X, 3, 512])
        w_in, w_turned, w_copied, made = s.sem("route_w_in"), s.sem("route_w_turned"), s.sem("route_w_copied"), s.sem("route_made")
        v_chain, before_done, shifted, exp_done = s.sem("route_vc"), s.sem("route_before_done"), s.sem("route_shifted"), s.sem("route_exp")
        gated, gate_turned, gate_out = s.sem("route_gated"), s.sem("route_gate_turned"), s.sem("route_gate_out")
        block = s.block()

        @block.sync
        def _(sp):
            sp.dma_start(rw[:, :], router_w).then_inc(w_in, 16)

        @block.gpsimd
        def _(pool):
            pool.memset(before[:, :, :], 1.0).then_inc(before_done, 1)
            pool.wait_ge(before_done, 1)
            pool.affine_select(out=before[:, :, :], in_=before[:, :, :], compare_op=ALU.is_gt, fill=0.0,
                               base=0, pattern=[[1, X], [-1, X]], channel_multiplier=0).then_inc(before_done, 1)

        @block.tensor
        def _(pe):
            pe.wait_ge(w_in, 16)
            for c in range(KC):
                last = pe.transpose(turn_ps[:, c * X:(c + 1) * X], rw[:, c * 128:(c + 1) * 128], g.ident[0:X, 0:X])
            last.then_inc(w_turned, 1)
            pe.wait_ge(w_copied, 1)
            for t in range(NT):
                for c in range(KC):
                    last = pe.matmul(logit_ps[:, t * X:(t + 1) * X], hT[:, c, t * TP:(t + 1) * TP], rwT[:, c, :],
                                     start=(c == 0), stop=(c == KC - 1))
            last.then_inc(made, 1)
            pe.wait_ge(gated, 1)
            for t in range(NT):
                last = pe.transpose(gate_ps[:, t // 4, (t % 4) * TP:(t % 4 + 1) * TP], gate[:, t, :],
                                    g.ident[0:TP, 0:TP])
            last.then_inc(gate_turned, 1)

        @block.vector
        def _(dve):
            link = chain(dve, v_chain)
            dve.wait_ge(w_turned, 1)
            dve.tensor_copy(rwT[:, :, :].rearrange("p c e -> p (c e)"), turn_ps[:, 0:KC * X]).then_inc(w_copied, 1)
            dve.wait_ge(made, 1)
            link(dve.tensor_copy(logits[:, :, :].rearrange("p t e -> p (t e)"), logit_ps[:, 0:NT * X]))
            one = logits[:, :, :].unsqueeze(3).to_broadcast([TP, NT, X, X])
            other = logits[:, :, :].unsqueeze(2).to_broadcast([TP, NT, X, X])
            dve.tensor_tensor(pairs[:, :, :, :], other, one, op=ALU.is_gt)
            dve.wait_ge(before_done, 2)
            link(dve.tensor_tensor(ties[:, :, :, :], other, one, op=ALU.is_equal))
            link(dve.tensor_tensor(ties[:, :, :, :], ties[:, :, :, :],
                                   before[:, :, :].unsqueeze(1).to_broadcast([TP, NT, X, X]), op=ALU.mult))
            link(dve.tensor_tensor(pairs[:, :, :, :], pairs[:, :, :, :], ties[:, :, :, :], op=ALU.add))
            link(dve.tensor_reduce(out=rank[:, :, :], in_=pairs[:, :, :, :], op=ALU.add, axis=AX_X))
            link(dve.tensor_reduce(out=top[:, :], in_=logits[:, :, :], op=ALU.max, axis=AX_X))
            dve.tensor_tensor(logits[:, :, :], logits[:, :, :], top[:, :].unsqueeze(2).to_broadcast([TP, NT, X]),
                              op=ALU.subtract).then_inc(shifted, 1)
            dve.wait_ge(exp_done, 1)
            link(dve.scalar_tensor_tensor(out=gate[:, :, :], in0=rank[:, :, :], scalar=1.5, in1=logits[:, :, :],
                                          op0=ALU.is_lt, op1=ALU.mult))
            link(dve.tensor_reduce(out=top[:, :], in_=gate[:, :, :], op=ALU.add, axis=AX_X))
            link(dve.reciprocal(top[:, :], top[:, :]))
            dve.tensor_tensor(gate[:, :, :], gate[:, :, :], top[:, :].unsqueeze(2).to_broadcast([TP, NT, X]),
                              op=ALU.mult).then_inc(gated, 1)
            dve.wait_ge(gate_turned, 1)
            dve.tensor_copy(gateT[:, 0:8 * TP].rearrange("p (a b) -> p a b", a=2),
                            gate_ps[:, 0:2, 0:4 * TP]).then_inc(gate_out, 1)
            dve.tensor_copy(gateT[:, 8 * TP:N], gate_ps[:, 2, 0:2 * TP]).then_inc(gate_out, 1)
            dve.wait_ge(gate_out, 2)

        @block.scalar
        def _(act):
            act.wait_ge(shifted, 1)
            act.activation(logits[:, :, :], logits[:, :, :], ACT.Exp).then_inc(exp_done, 1)


def experts(g, hT, gate, gateT, w1, b1, w2, b2):
    X, F = b1.shape
    FC = F // 128
    with ExitStack() as ctx:
        s = Scope(g, ctx)
        up_w = [s.sb(f"moe_up_w{i}", [128, KC, F]) for i in range(2)]
        down_w = [s.sb(f"moe_down_w{i}", [128, FC, D]) for i in range(2)]
        inner = [s.sb(f"moe_inner{i}", [128, FC, N]) for i in range(2)]
        b1_rows = s.sb("moe_b1_rows", [X * FC, 128])
        b1_cols = s.sb("moe_b1_cols", [128, X * FC])
        b2_sb = s.sb("moe_b2", [X, D])
        up_ps = [s.ps(f"moe_up{i}", [128, 512]) for i in range(4)]
        down_ps = [s.ps(f"moe_down{i}", [TP, 2, 512]) for i in range(2)]
        small_in, turned, copied = s.sem("moe_small_in"), s.sem("moe_turned"), s.sem("moe_copied")
        up_in, down_in = s.sems("moe_up_in", 2), s.sems("moe_down_in", 2)
        up_done, gelu_done, down_done, added = s.sem("moe_up_done"), s.sem("moe_gelu"), s.sem("moe_down_done"), s.sem("moe_added")
        per_up = FC * len(TOKENS)
        block = s.block()

        @block.sync
        def _(sp):
            sp.dma_start(b1_rows[:, :], b1.rearrange("e (c p) -> (e c) p", p=128)).then_inc(small_in, 16)
            sp.dma_start(b2_sb[:, :], b2).then_inc(small_in, 16)
            for e in range(X):
                if e >= 2:
                    sp.wait_ge(up_done, (e - 1) * per_up)
                sp.dma_start(up_w[e % 2][:, :, :], w1[e, :, :].rearrange("(c p) f -> p c f", p=128)).then_inc(up_in[e % 2], 16)
                if e >= 2:
                    sp.wait_ge(down_done, (e - 1) * NT)
                sp.dma_start(down_w[e % 2][:, :, :], w2[e, :, :].rearrange("(c p) f -> p c f", p=128)).then_inc(down_in[e % 2], 16)

        @block.tensor
        def _(pe):
            pe.wait_ge(small_in, 32)
            pe.transpose(up_ps[0][:, 0:X * FC], b1_rows[:, :], g.ident[0:X * FC, 0:X * FC]).then_inc(turned, 1)
            pe.wait_ge(copied, 1)

            def up(e):
                pe.wait_ge(up_in[e % 2], e // 2 * 16 + 16)
                for f in range(FC):
                    for k, (a, b) in enumerate(TOKENS):
                        n = e * per_up + f * len(TOKENS) + k
                        if n >= 4:
                            pe.wait_ge(gelu_done, n - 3)
                        for c in range(KC):
                            last = pe.matmul(up_ps[n % 4][:, 0:b - a], up_w[e % 2][:, c, f * 128:(f + 1) * 128],
                                             hT[:, c, a:b], start=(c == 0), stop=(c == KC - 1))
                        last.then_inc(up_done, 1)

            def down(e):
                pe.wait_ge(down_in[e % 2], e // 2 * 16 + 16)
                pe.wait_ge(gelu_done, (e + 1) * per_up)
                for t in range(NT):
                    n = e * NT + t
                    if n >= 2:
                        pe.wait_ge(added, n - 1)
                    for half in range(2):
                        for f in range(FC):
                            last = pe.matmul(down_ps[n % 2][:, half, 0:384], inner[e % 2][:, f, t * TP:(t + 1) * TP],
                                             down_w[e % 2][:, f, half * 384:(half + 1) * 384],
                                             start=(f == 0), stop=(f == FC - 1))
                    last.then_inc(down_done, 1)

            up(0)
            for e in range(X):
                if e + 1 < X:
                    up(e + 1)
                down(e)
            for t in range(NT):
                n = X * NT + t
                pe.wait_ge(added, n - 1)
                for half in range(2):
                    last = pe.matmul(down_ps[n % 2][:, half, 0:384], gateT[:, t * TP:(t + 1) * TP],
                                     b2_sb[:, half * 384:(half + 1) * 384], start=True, stop=True)
                last.then_inc(down_done, 1)

        @block.scalar
        def _(act):
            act.wait_ge(turned, 1)
            act.activation(b1_cols[:, :], up_ps[0][:, 0:X * FC], ACT.Copy).then_inc(copied, 1)
            act.wait_ge(copied, 1)
            for e in range(X):
                if e >= 2:
                    act.wait_ge(down_done, (e - 1) * NT)
                for f in range(FC):
                    for k, (a, b) in enumerate(TOKENS):
                        n = e * per_up + f * len(TOKENS) + k
                        act.wait_ge(up_done, n + 1)
                        act.activation(inner[e % 2][:, f, a:b], up_ps[n % 4][:, 0:b - a], ACT.Gelu,
                                       bias=b1_cols[:, e * FC + f:e * FC + f + 1]).then_inc(gelu_done, 1)

        @block.vector
        def _(dve):
            for n in range((X + 1) * NT):
                e, t = divmod(n, NT)
                dve.wait_ge(down_done, n + 1)
                if e:
                    dve.wait_ge(added, n - NT + 1)
                x_t = g.x[:, t, :].rearrange("p (a b) -> p a b", a=2)
                y = down_ps[n % 2][:, :, 0:384]
                if e < X:
                    dve.scalar_tensor_tensor(out=x_t, in0=y, scalar=gate[:, t, e:e + 1], in1=x_t,
                                             op0=ALU.mult, op1=ALU.add).then_inc(added, 1)
                else:
                    dve.tensor_tensor(x_t, y, x_t, op=ALU.add).then_inc(added, 1)
            dve.wait_ge(added, (X + 1) * NT)


def moe_layer(g, router_w, w1, b1, w2, b2):
    with ExitStack() as ctx:
        s = Scope(g, ctx)
        hT = s.sb("moe_hT", [128, KC, N])
        gate = s.sb("moe_gate", [TP, NT, router_w.shape[0]])
        gateT = s.sb("moe_gateT", [router_w.shape[0], N])
        with ExitStack() as inner:
            h = Scope(g, inner).sb("moe_h", [TP, NT, D])
            normalize(g, "moe_ln", g.x, h, hT)
            route(g, hT, router_w, gate, gateT)
        experts(g, hT, gate, gateT, w1, b1, w2, b2)


def project_rel(g, tag, hT, w, q, k, ks, qd):
    H = q.shape[1]
    half = (D + 2 * H) // 2
    with ExitStack() as ctx:
        s = Scope(g, ctx)
        w_sb = [s.sb(f"{tag}_w{r}", [128, KC, D + 2 * H]) for r in range(R)]
        qk = s.sb(f"{tag}_qk", [128, KC, 2 * H])
        wT = [s.sb(f"{tag}_wT{i}", [128, KC, 128]) for i in range(2)]
        stage = [s.sb(f"{tag}_stage{i}", [TP, D]) for i in range(3)]
        turn_ps = [s.ps(f"{tag}_wturn{i}", [128, 2, 512]) for i in range(2)]
        out_ps = [s.ps(f"{tag}_out{i}", [128, 2, 512]) for i in range(2)]
        qk_in, w_in, w_turned, w_copied = s.sem(f"{tag}_qk_in"), s.sems(f"{tag}_w_in", R), s.sem(f"{tag}_w_turned"), s.sem(f"{tag}_w_copied")
        qk_made, qk_out, made = s.sem(f"{tag}_qk_made"), s.sem(f"{tag}_qk_out"), s.sem(f"{tag}_made")
        left, right, sent = s.sem(f"{tag}_left"), s.sem(f"{tag}_right"), s.sems(f"{tag}_sent", 3)
        block = s.block()

        @block.sync
        def _(sp):
            for i, v in enumerate((q, k)):
                sp.dma_start(qk[:, :, i * H:(i + 1) * H], v.rearrange("(c p) h -> p c h", p=128),
                             allow_slow_non_contiguous=True).then_inc(qk_in, 16)
            for r in range(R):
                sp.dma_start(w_sb[r][:, :, 0:D], w[r, :, :].rearrange("(c p) f -> p c f", p=128)).then_inc(w_in[r], 16)
            for n in range(R * NT):
                r, t = divmod(n, NT)
                sp.wait_ge(left, n + 1)
                sp.wait_ge(right, n + 1)
                sp.dma_start(g.values_dram[r, t * TP:(t + 1) * TP, :], stage[n % 3][:, :]).then_inc(sent[n % 3], 16)
            for i in range(3):
                sp.wait_ge(sent[i], R * NT // 3 * 16)

        @block.tensor
        def _(pe):
            pe.wait_ge(qk_in, 32)
            for n in range(R * KC + 1):
                if n < R * KC:
                    r, dc = divmod(n, KC)
                    if dc == 0:
                        pe.wait_ge(w_in[r], 16)
                    if n >= 2:
                        pe.wait_ge(w_copied, n - 1)
                    for f in range(KC):
                        last = pe.transpose(turn_ps[n % 2][:, f // 3, (f % 3) * 128:(f % 3 + 1) * 128],
                                            w_sb[r][:, dc, f * 128:(f + 1) * 128], g.ident[:, :])
                    last.then_inc(w_turned, 1)
                if n >= 1:
                    m = n - 1
                    pe.wait_ge(w_copied, m + 1)
                    if m >= 2:
                        pe.wait_ge(qk_out, m - 1)
                    for f in range(KC):
                        last = pe.matmul(out_ps[m % 2][:, 0, 0:2 * H], wT[m % 2][:, f, :], qk[:, f, :],
                                         start=(f == 0), stop=(f == KC - 1))
                    last.then_inc(qk_made, 1)
            pe.wait_ge(qk_out, R * KC)
            for n in range(R * NT):
                r, t = divmod(n, NT)
                if n >= 2:
                    pe.wait_ge(left, n - 1)
                    pe.wait_ge(right, n - 1)
                for a in range(2):
                    for c in range(KC):
                        last = pe.matmul(out_ps[n % 2][0:TP, a, 0:half], hT[:, c, t * TP:(t + 1) * TP],
                                         w_sb[r][:, c, a * half:(a + 1) * half], start=(c == 0), stop=(c == KC - 1))
                last.then_inc(made, 1)

        @block.scalar
        def _(act):
            for n in range(R * KC):
                act.wait_ge(w_turned, n + 1)
                if n >= 2:
                    act.wait_ge(qk_made, n - 1)
                act.activation(wT[n % 2][:, :, :].rearrange("p (a b) d -> p a (b d)", a=2),
                               turn_ps[n % 2][:, :, 0:384], ACT.Copy).then_inc(w_copied, 1)
            for n in range(R * NT):
                act.wait_ge(made, n + 1)
                if n >= 3:
                    act.wait_ge(sent[n % 3], n // 3 * 16)
                act.activation(stage[n % 3][:, 0:half], out_ps[n % 2][0:TP, 0, 0:half], ACT.Copy).then_inc(left, 1)

        @block.vector
        def _(dve):
            for n in range(R * KC):
                r, dc = divmod(n, KC)
                dve.wait_ge(qk_made, n + 1)
                dve.tensor_copy(w_sb[r][:, dc, D:D + 2 * H], out_ps[n % 2][:, 0, 0:2 * H]).then_inc(qk_out, 1)
            for n in range(R * NT):
                r, t = divmod(n, NT)
                dve.wait_ge(made, n + 1)
                if n >= 3:
                    dve.wait_ge(sent[n % 3], n // 3 * 16)
                dve.tensor_copy(stage[n % 3][:, half:D], out_ps[n % 2][0:TP, 1, 0:D - half])
                dve.tensor_copy(qd[:, t, r * H:(r + 1) * H], out_ps[n % 2][0:TP, 1, D - half:D - half + H])
                dve.tensor_copy(ks[:, t, r * H:(r + 1) * H],
                                out_ps[n % 2][0:TP, 1, D - half + H:half]).then_inc(right, 1)
            dve.wait_ge(right, R * NT)


def far_rows(g, r):
    return bass.AP(tensor=g.far_dram.tensor, offset=r * N, ap=[[R * N, TP], [R * N * TP, NT], [1, N]])


def elu_and_turn(g, h, hT):
    with ExitStack() as ctx:
        s = Scope(g, ctx)
        low = [s.sb(f"elu_low{i}", [TP, D]) for i in range(2)]
        banks = [[s.ps(f"elu_turn{i}{j}", [128, 512]) for j in range(2)] for i in range(2)]
        clipped, exp_done, rows_done, v_chain = s.sem("elu_clipped"), s.sem("elu_exp"), s.sem("elu_rows"), s.sem("elu_vc")
        turned, copied = s.sem("elu_turned"), s.sem("elu_copied")
        block = s.block()

        @block.vector
        def _(dve):
            link = chain(dve, v_chain)
            for t in range(NT + 1):
                if t < NT:
                    if t >= 2:
                        dve.wait_ge(rows_done, t - 1)
                    dve.tensor_scalar(low[t % 2][:, :], h[:, t, :], 0.0, None, op0=ALU.min).then_inc(clipped, 1)
                if t >= 1:
                    u = t - 1
                    dve.wait_ge(exp_done, u + 1)
                    link(dve.tensor_scalar(low[u % 2][:, :], low[u % 2][:, :], -1.0, None, op0=ALU.add))
                    dve.scalar_tensor_tensor(out=h[:, u, :], in0=h[:, u, :], scalar=0.0, in1=low[u % 2][:, :],
                                             op0=ALU.max, op1=ALU.add).then_inc(rows_done, 1)
            dve.wait_ge(rows_done, NT)

        def take_turned(act, t):
            act.wait_ge(turned, t + 1)
            for j in range(2):
                act.activation(hT[:, 3 * j:3 * j + 3, t * TP:(t + 1) * TP],
                               banks[t % 2][j][:, 0:3 * TP].rearrange("p (c t) -> p c t", t=TP),
                               ACT.Copy).then_inc(copied, 1)

        @block.scalar
        def _(act):
            for t in range(NT):
                act.wait_ge(clipped, t + 1)
                act.activation(low[t % 2][:, :], low[t % 2][:, :], ACT.Exp).then_inc(exp_done, 1)
                if t >= 1:
                    take_turned(act, t - 1)
            take_turned(act, NT - 1)
            act.wait_ge(copied, 2 * NT)

        @block.tensor
        def _(pe):
            for t in range(NT):
                pe.wait_ge(rows_done, t + 1)
                if t >= 2:
                    pe.wait_ge(copied, 2 * (t - 1))
                turn_tile(pe, g, banks[t % 2], h, t, turned)


def rgat_layers(g, w1, q1, k1, b1, w2, q2, k2, b2):
    with ExitStack() as ctx:
        s = Scope(g, ctx)
        h = s.sb("rgat_h", [TP, NT, D])
        for layer, (tag, w, q, k) in enumerate((("rg1", w1, q1, k1), ("rg2", w2, q2, k2))):
            H = q.shape[1]
            with ExitStack() as inner:
                si = Scope(g, inner)
                ks = si.sb(f"{tag}_ks", [TP, NT, R * H])
                qd = si.sb(f"{tag}_qd", [TP, NT, R * H])
                with ExitStack() as inmost:
                    hT = Scope(g, inmost).sb(f"{tag}_hT", [128, KC, N])
                    if layer == 0:
                        normalize(g, "rg_ln", g.x, h, hT)
                    else:
                        elu_and_turn(g, h, hT)
                    project_rel(g, tag, hT, w, q, k, ks, qd)
                bias = si.sb(f"{tag}_bias", [TP, D])
                load_bias(g, tag, b1 if layer == 0 else b2, bias, add=(layer == 1))

                def finish(dve, hd, d, c0, c1, sums, recip):
                    width = D // H
                    at = slice(hd * width + c0, hd * width + c1)
                    out, plus = (h[:, d, at], bias[:, at]) if layer == 0 else (g.x[:, d, at], g.x[:, d, at])
                    return dve.scalar_tensor_tensor(out=out, in0=sums, scalar=recip, in1=plus,
                                                    op0=ALU.mult, op1=ALU.add)

                attend(g, tag, H, D // H, 5 if layer == 0 else 2, lambda r: far_rows(g, r), ks, qd,
                       None, finish)


def load_bias(g, tag, b, bias, add):
    with ExitStack() as ctx:
        s = Scope(g, ctx)
        loaded, added = s.sem(f"{tag}_bias_in"), s.sem(f"{tag}_bias_added")
        block = s.block()

        @block.sync
        def _(sp):
            sp.dma_start(bias[:, :], rows_of(b, TP, 0, D)).then_inc(loaded, 16)
            sp.wait_ge(loaded, 16)

        if add:
            @block.gpsimd
            def _(pool):
                pool.wait_ge(loaded, 16)
                for t in range(NT):
                    pool.tensor_tensor(g.x[:, t, :], g.x[:, t, :], bias[:, :], op=ALU.add).then_inc(added, 1)
                pool.wait_ge(added, NT)

PICKED = max(1, int(round(0.15 * N)))
QT = PICKED // 2
HEADS = 12
DH = D // HEADS


def pick_tokens(g, n, wr, br, keep, picks, picksT, picked_nT, score_rows, room):
    with ExitStack() as ctx:
        s = Scope(g, ctx)
        wr_rows = s.sb("pick_wr", [TP, D])
        junk = s.sb("pick_junk", [TP, 2, D])
        score = s.sb("pick_score", [TP, NT])
        br_col = s.sb("pick_br", [TP, 1])
        scoreT = s.sb("pick_scoreT", [NT, TP])
        srow, node, tie, less = (room[0:TP, i, :] for i in range(4))
        own = s.sb("pick_own", [TP, NT])
        rank = s.sb("pick_rank", [TP, NT])
        ones = s.sb("pick_ones", [TP, TP])
        total = s.sb("pick_total", [TP, 1])
        ps = s.ps("pick_ps", [128, 512])
        turn_ps = [s.ps(f"pick_turn{i}", [QT, 512]) for i in range(2)]
        picked_ps = s.ps("pick_picked", [128, 3, 512])
        small_in, ready, scored, turned, score_out, srow_in = (s.sem(f"pick_{x}") for x in "abcdef")
        summed, weighed, ranked, v_chain, dots, copied = (s.sem(f"pick_{x}") for x in "ghijkl")
        picksT_turned, picksT_out, gathered, score_saved = (s.sem(f"pick_{x}") for x in "mnop")
        rows_ready = s.sem("pick_q")
        block = s.block()
        j1 = PICKED + 1

        @block.sync
        def _(sp):
            sp.dma_start(wr_rows[:, :], rows_of(wr, TP, 0, D)).then_inc(small_in, 16)
            sp.dma_start(br_col[:, :], rows_of(br, TP, 0, 1)).then_inc(small_in, 16)
            sp.wait_ge(copied, 1)
            sp.dma_start(g.score_dram, scoreT[:, :]).then_inc(score_out, 16)
            sp.wait_ge(score_out, 16)
            sp.dma_start(srow, rows_of(g.score_dram, TP, 0, N)).then_inc(srow_in, 16)
            sp.wait_ge(rows_ready, 1)
            sp.dma_start(score_rows[0:1, :], rows_of(g.score_dram, 1, 0, N)).then_inc(score_saved, 16)
            sp.wait_ge(score_saved, 16)

        @block.gpsimd
        def _(pool):
            pool.iota(node, [[1, N]], base=0, channel_multiplier=0,
                      allow_small_or_imprecise_dtypes=True).then_inc(ready, 1)
            pool.iota(own[:, :], [[TP, NT]], base=0, channel_multiplier=1,
                      allow_small_or_imprecise_dtypes=True).then_inc(ready, 1)
            pool.memset(ones[:, :], 1.0).then_inc(ready, 1)
            pool.memset(score_rows[:, :], 1.0).then_inc(rows_ready, 1)

        @block.scalar
        def _(act):
            act.wait_ge(dots, NT)
            act.wait_ge(small_in, 32)
            act.activation(score[:, :], score[:, :], ACT.Sigmoid, bias=br_col[:, 0:1]).then_inc(scored, 1)
            for i in range(5):
                act.wait_ge(picksT_turned, i + 1)
                act.activation(picksT[:, :, i * 2 * TP:(i + 1) * 2 * TP],
                               turn_ps[i % 2][:, 0:4 * TP].rearrange("p (q k) -> p q k", q=2),
                               ACT.Copy).then_inc(picksT_out, 1)
            act.wait_ge(gathered, 1)
            act.activation(picked_nT[:, :, :].rearrange("p (a b) j -> p a (b j)", b=2),
                           picked_ps[:, :, 0:2 * j1], ACT.Copy).then_inc(gathered, 1)
            act.wait_ge(gathered, 2)

        @block.tensor
        def _(pe):
            pe.wait_ge(scored, 1)
            pe.wait_ge(ready, 3)
            pe.transpose(ps[0:NT, 0:TP], score[:, :], g.ident[0:TP, 0:TP])
            pe.matmul(ps[0:TP, 128:128 + NT], ones[:, :], score[:, :], start=True, stop=True).then_inc(turned, 1)
            for i in range(5):
                if i == 0:
                    pe.wait_ge(ranked, NT)
                if i >= 2:
                    pe.wait_ge(picksT_out, i - 1)
                for q in range(2):
                    for k in range(2):
                        last = pe.transpose(turn_ps[i % 2][:, (2 * q + k) * TP:(2 * q + k + 1) * TP],
                                            picks[:, 2 * i + k, q * QT:(q + 1) * QT], g.ident[0:TP, 0:TP])
                last.then_inc(picksT_turned, 1)
            pe.wait_ge(weighed, 1)
            for c in range(KC):
                for t in range(NT):
                    last = pe.matmul(picked_ps[:, c // 2, (c % 2) * j1:(c % 2 + 1) * j1],
                                     n[:, t, c * 128:(c + 1) * 128], picks[:, t, :],
                                     start=(t == 0), stop=(t == NT - 1))
            last.then_inc(gathered, 1)

        @block.vector
        def _(dve):
            link = chain(dve, v_chain)
            dve.wait_ge(small_in, 32)
            for t in range(NT):
                if t >= 2:
                    dve.wait_ge(dots, t - 1)
                dve.tensor_tensor_reduce(out=junk[:, t % 2, :], in0=n[:, t, :], in1=wr_rows[:, :], scale=1.0,
                                         scalar=0.0, op0=ALU.mult, op1=ALU.add,
                                         accum_out=score[:, t:t + 1]).then_inc(dots, 1)
            dve.wait_ge(turned, 1)
            dve.tensor_copy(scoreT[:, :], ps[0:NT, 0:TP]).then_inc(copied, 1)
            link(dve.tensor_reduce(out=total[:, :], in_=ps[0:TP, 128:128 + NT], op=ALU.add, axis=AX_X))
            link(dve.tensor_scalar(total[:, :], total[:, :], 1e-6, None, op0=ALU.add))
            link(dve.reciprocal(total[:, :], total[:, :]))
            dve.tensor_scalar(picks[:, :, PICKED:j1], score[:, :].unsqueeze(2), total[:, 0:1], None,
                              op0=ALU.mult).then_inc(weighed, 1)
            dve.wait_ge(srow_in, 16)
            for t in range(NT):
                link(dve.tensor_scalar(less, node, own[:, t:t + 1], None, op0=ALU.is_lt))
                link(dve.scalar_tensor_tensor(out=tie, in0=srow, scalar=score[:, t:t + 1],
                                              in1=less, op0=ALU.is_equal, op1=ALU.mult))
                link(dve.scalar_tensor_tensor(out=less, in0=srow, scalar=score[:, t:t + 1],
                                              in1=tie, op0=ALU.is_lt, op1=ALU.add))
                link(dve.tensor_reduce(out=rank[:, t:t + 1], in_=less, op=ALU.add, axis=AX_X))
                dve.tensor_scalar(picks[:, t, 0:PICKED], node[:, 0:PICKED], rank[:, t:t + 1], None,
                                  op0=ALU.is_equal).then_inc(ranked, 1)
            link(dve.tensor_scalar(keep[:, :], rank[:, :], PICKED - 0.5, None, op0=ALU.is_gt))


def columns_of(v, width):
    return v.rearrange("(c p) -> p c", p=128)


def mix_and_project(g, z, nT, picked_nT, score_rows, keep, wm, bm, wk, bk, wv, wq, bq, kT, v, qT):
    with ExitStack() as ctx:
        s = Scope(g, ctx)
        w_sb = [s.sb("mix_w", [128, KC, D]), g.x_all[:, 0:KC, :]]
        mixed = s.sb("mix_rows", [2, D])
        b_cols = s.sb("mix_b", [128, 2, KC])
        row_ps = s.ps("mix_row", [1, 2, 512])
        ps = [s.ps(f"mix_ps{i}", [128, 2, 512]) for i in range(3)]
        w_in, w_used, small_in, row_made, row_out = s.sems("mix_w_in", 2), s.sem("mix_w_used"), s.sem("mix_small"), s.sem("mix_row_made"), s.sem("mix_row_out")
        made, taken = s.sem("mix_made"), s.sem("mix_taken")
        block = s.block()
        jobs = [("mix", t) for t in range(NT)] + [("key", (f, k)) for f in range(KC) for k in range(len(TOKENS))] \
            + [("value", t) for t in range(NT)] + [("query", f) for f in range(KC)]
        weights = {"mix": 0, "key": 1, "value": 2, "query": 3}
        last_of = {kind: max(i for i, j in enumerate(jobs) if j[0] == kind) + 1 for kind in weights}

        @block.sync
        def _(sp):
            sp.dma_start(mixed[1:2, :], rows_of(bm, 1, 0, D)).then_inc(small_in, 16)
            for i, b in enumerate((bk, bq)):
                sp.dma_start(b_cols[:, i, :], columns_of(b, D), allow_slow_non_contiguous=True).then_inc(small_in, 16)
            for i, w in enumerate((wm, wk, wv, wq)):
                if i >= 2:
                    sp.wait_ge(made, last_of["mix" if i == 2 else "key"])
                sp.dma_start(w_sb[i % 2][:, :, :], w.rearrange("(c p) f -> p c f", p=128)).then_inc(w_in[i % 2], 16)

        @block.tensor
        def _(pe):
            pe.wait_ge(w_in[0], 16)
            for a in range(2):
                for c in range(KC):
                    last = pe.matmul(row_ps[:, a, 0:384], picked_nT[:, c, PICKED:PICKED + 1],
                                     w_sb[0][:, c, a * 384:(a + 1) * 384], start=(c == 0), stop=(c == KC - 1))
            last.then_inc(row_made, 1)
            pe.wait_ge(row_out, 1)
            pe.wait_ge(small_in, 48)
            for i, (kind, at) in enumerate(jobs):
                w = w_sb[weights[kind] % 2]
                out = ps[i % 3]
                pe.wait_ge(w_in[weights[kind] % 2], weights[kind] // 2 * 16 + 16)
                if i >= 3:
                    pe.wait_ge(taken, i - 2)
                if kind in ("mix", "value"):
                    rows = slice(at * TP, (at + 1) * TP)
                    for a in range(2):
                        cols = slice(a * 384, (a + 1) * 384)
                        if kind == "mix":
                            pe.matmul(out[0:TP, a, 0:384], score_rows[:, rows], mixed[:, cols],
                                      start=True, stop=False)
                        for c in range(KC):
                            last = pe.matmul(out[0:TP, a, 0:384], nT[:, c, rows], w[:, c, cols],
                                             start=(c == 0 and kind == "value"), stop=(c == KC - 1))
                else:
                    f = at[0] if kind == "key" else at
                    for c in range(KC):
                        if kind == "key":
                            a, b = TOKENS[at[1]]
                            moving = nT[:, c, a:b]
                        else:
                            a, b = 0, PICKED
                            moving = picked_nT[:, c, 0:PICKED]
                        last = pe.matmul(out[:, 0, 0:b - a], w[:, c, f * 128:(f + 1) * 128], moving,
                                         start=(c == 0), stop=(c == KC - 1))
                last.then_inc(made, 1)

        @block.vector
        def _(dve):
            dve.wait_ge(row_made, 1)
            dve.tensor_copy(mixed[0:1, :].rearrange("p (a b) -> p a b", a=2), row_ps[:, :, 0:384]).then_inc(row_out, 1)
            dve.wait_ge(small_in, 48)
            for i, (kind, at) in enumerate(jobs):
                dve.wait_ge(made, i + 1)
                out = ps[i % 3]
                if kind == "mix":
                    z_t = z[:, at, :].rearrange("p (a b) -> p a b", a=2)
                    last = dve.scalar_tensor_tensor(out=z_t, in0=out[0:TP, :, 0:384], scalar=keep[:, at:at + 1],
                                                    in1=z_t, op0=ALU.mult, op1=ALU.add)
                elif kind == "value":
                    last = dve.tensor_copy(v[:, at, :].rearrange("p (a b) -> p a b", a=2), out[0:TP, :, 0:384])
                elif kind == "key":
                    f, k = at
                    a, b = TOKENS[k]
                    last = dve.tensor_scalar(kT[:, f, a:b], out[:, 0, 0:b - a], b_cols[:, 0, f:f + 1], None, op0=ALU.add)
                else:
                    last = dve.tensor_scalar(qT[:, at, :], out[:, 0, 0:PICKED], b_cols[:, 1, at:at + 1], None,
                                             op0=ALU.add)
                last.then_inc(taken, 1)
            dve.wait_ge(taken, len(jobs))


def attend_picked(g, z, kT, v, qT, picksT, bv, wo, bo):
    SCALE = DH ** -0.5
    units = [(q, h) for q in range(2) for h in range(HEADS)]
    with ExitStack() as ctx:
        s = Scope(g, ctx)
        probs = [s.sb(f"att_probs{i}", [QT, N]) for i in range(2)]
        probsT = [s.sb(f"att_probsT{i}", [TP, NT, QT]) for i in range(2)]
        top = s.sb("att_top", [QT, len(units)])
        total = s.sb("att_total", [QT, len(units)])
        ctxT = s.sb("att_ctxT", [128, KC, PICKED])
        bv_cols = s.sb("att_bv", [128, KC])
        wo_sb = s.sb("att_wo", [128, KC, D])
        bo_row = s.sb("att_bo", [1, D])
        ones = s.sb("att_ones", [1, QT])
        out_sb = s.sb("att_out", [QT, 2, D])
        score_ps = [s.ps(f"att_score{i}", [128, 3, 512]) for i in range(2)]
        turn_ps = [s.ps(f"att_turn{i}", [TP, 512]) for i in range(2)]
        flat = [x[0:QT, :, :].rearrange("p a b -> p (a b)") for x in score_ps]
        small_in, wo_in, one_set = s.sem("att_small"), s.sem("att_wo_in"), s.sem("att_one")
        scored, topped, exp_done, scaled, turned, turned_out = (s.sem(f"att_{x}") for x in "abcdef")
        ctx_made, ctx_out, v_chain, out_made, out_taken, spread, added = (s.sem(f"att_{x}") for x in "ghijklm")
        block = s.block()

        @block.sync
        def _(sp):
            sp.dma_start(bv_cols[:, :], columns_of(bv, D), allow_slow_non_contiguous=True).then_inc(small_in, 16)
            sp.dma_start(bo_row[:, :], rows_of(bo, 1, 0, D)).then_inc(small_in, 16)
            sp.dma_start(wo_sb[:, :, :], wo.rearrange("(c p) f -> p c f", p=128)).then_inc(wo_in, 16)

        @block.gpsimd
        def _(pool):
            pool.memset(ones[:, :], 1.0).then_inc(one_set, 1)

        @block.tensor
        def _(pe):
            def scores(i):
                q, h = units[i]
                at = slice(h % 2 * DH, h % 2 * DH + DH)
                if i >= 2:
                    pe.wait_ge(ctx_out, i - 1)
                for k in range(0, N, 512):
                    w = min(512, N - k)
                    last = pe.matmul(flat[i % 2][:, k:k + w], qT[at, h // 2, q * QT:(q + 1) * QT],
                                     kT[at, h // 2, k:k + w], start=True, stop=True)
                last.then_inc(scored, 1)

            def context(i):
                q, h = units[i]
                pe.wait_ge(scaled, i + 1)
                for half in range(2):
                    if i >= 1:
                        pe.wait_ge(turned_out, 2 * (i - 1) + half + 1)
                    for k in range(5):
                        t = half * 5 + k
                        last = pe.transpose(turn_ps[half][:, k * QT:(k + 1) * QT], probs[i % 2][:, t * TP:(t + 1) * TP],
                                            g.ident[0:QT, 0:QT])
                    last.then_inc(turned, 1)
                pe.wait_ge(turned_out, 2 * i + 2)
                at = slice(h % 2 * DH, h % 2 * DH + DH)
                for t in range(NT):
                    last = pe.matmul(score_ps[i % 2][at, 0, 0:QT], v[:, t, h * DH:(h + 1) * DH],
                                     probsT[i % 2][:, t, :], start=(t == 0), stop=(t == NT - 1))
                last.then_inc(ctx_made, 1)

            scores(0)
            for i in range(len(units)):
                if i + 1 < len(units):
                    scores(i + 1)
                context(i)
            pe.wait_ge(ctx_out, len(units))
            pe.wait_ge(wo_in, 16)
            pe.wait_ge(small_in, 32)
            pe.wait_ge(one_set, 1)
            for q in range(2):
                for a in range(2):
                    cols = slice(a * 384, (a + 1) * 384)
                    pe.matmul(score_ps[q][0:QT, a, 0:384], ones[:, :], bo_row[:, cols], start=True, stop=False)
                    for c in range(KC):
                        last = pe.matmul(score_ps[q][0:QT, a, 0:384], ctxT[:, c, q * QT:(q + 1) * QT],
                                         wo_sb[:, c, cols], start=False, stop=(c == KC - 1))
                last.then_inc(out_made, 1)
            pe.wait_ge(out_taken, 2)
            for t in range(NT):
                if t >= 2:
                    pe.wait_ge(added, t - 1)
                for a in range(2):
                    for q in range(2):
                        last = pe.matmul(score_ps[t % 2][0:TP, a, 0:384], picksT[:, q, t * TP:(t + 1) * TP],
                                         out_sb[:, q, a * 384:(a + 1) * 384], start=(q == 0), stop=(q == 1))
                last.then_inc(spread, 1)

        @block.vector
        def _(dve):
            link = chain(dve, v_chain)
            dve.wait_ge(small_in, 32)

            def first_half(i):
                dve.wait_ge(scored, i + 1)
                link(dve.tensor_reduce(out=top[:, i:i + 1], in_=flat[i % 2][:, 0:N], op=ALU.max, axis=AX_X))
                dve.tensor_scalar(top[:, i:i + 1], top[:, i:i + 1], -SCALE, None, op0=ALU.mult).then_inc(topped, 1)

            def second_half(i):
                dve.wait_ge(exp_done, i + 1)
                link(dve.reciprocal(total[:, i:i + 1], total[:, i:i + 1]))
                dve.tensor_scalar(probs[i % 2][:, :], probs[i % 2][:, :], total[:, i:i + 1], None,
                                  op0=ALU.mult).then_inc(scaled, 1)

            def take_context(i):
                q, h = units[i]
                at = slice(h % 2 * DH, h % 2 * DH + DH)
                dve.wait_ge(ctx_made, i + 1)
                dve.tensor_scalar(ctxT[at, h // 2, q * QT:(q + 1) * QT], score_ps[i % 2][at, 0, 0:QT],
                                  bv_cols[at, h // 2:h // 2 + 1], None, op0=ALU.add).then_inc(ctx_out, 1)

            for i in range(len(units)):
                first_half(i)
                if i >= 1:
                    take_context(i - 1)
                second_half(i)
            take_context(len(units) - 1)
            for q in range(2):
                dve.wait_ge(out_made, q + 1)
                dve.tensor_copy(out_sb[:, q, :].rearrange("p (a b) -> p a b", a=2),
                                score_ps[q][0:QT, 0:2, 0:384]).then_inc(out_taken, 1)
            for t in range(NT):
                dve.wait_ge(spread, t + 1)
                z_t = z[:, t, :].rearrange("p (a b) -> p a b", a=2)
                dve.tensor_tensor(z_t, z_t, score_ps[t % 2][0:TP, 0:2, 0:384], op=ALU.add).then_inc(added, 1)
            dve.wait_ge(added, NT)

        @block.scalar
        def _(act):
            for i in range(len(units)):
                act.wait_ge(topped, i + 1)
                if i >= 2:
                    act.wait_ge(turned, 2 * (i - 1))
                act.activation(probs[i % 2][:, :], flat[i % 2][:, 0:N], ACT.Exp, bias=top[:, i:i + 1], scale=SCALE,
                               accum_out=total[:, i:i + 1]).then_inc(exp_done, 1)
                for half in range(2):
                    act.wait_ge(turned, 2 * i + half + 1)
                    if i >= 2:
                        act.wait_ge(ctx_made, i - 1)
                    act.activation(probsT[i % 2][:, half * 5:half * 5 + 5, :].rearrange("p t q -> p (t q)"),
                                   turn_ps[half][:, 0:5 * QT], ACT.Copy).then_inc(turned_out, 1)


def feed_forward(g, z, nT, w1, b1, w2, b2):
    F = w1.shape[1]
    FC = F // 128
    with ExitStack() as ctx:
        s = Scope(g, ctx)
        up_w = s.sb("ff_up_w", [128, KC, F])
        down_w = s.sb("ff_down_w", [128, FC, D])
        inner = s.sb("ff_inner", [128, FC, N])
        b1_cols = s.sb("ff_b1", [128, FC])
        b2_row = s.sb("ff_b2", [1, D])
        ones = s.sb("ff_ones", [1, TP])
        up_ps = [s.ps(f"ff_up{i}", [128, 512]) for i in range(4)]
        down_ps = [s.ps(f"ff_down{i}", [TP, 2, 512]) for i in range(2)]
        w_in, one_set, up_done, gelu_done, down_done, added, plus = (s.sem(f"ff_{x}") for x in "abcdefg")
        x_in = s.sem("ff_x_in")
        block = s.block()
        ups = [(f, k) for f in range(FC) for k in range(len(TOKENS))]

        @block.sync
        def _(sp):
            sp.dma_start(g.x, g.x_dram).then_inc(x_in, 16)
            sp.dma_start(up_w[:, :, :], w1.rearrange("(c p) f -> p c f", p=128)).then_inc(w_in, 16)
            sp.dma_start(down_w[:, :, :], w2.rearrange("(c p) f -> p c f", p=128)).then_inc(w_in, 16)
            sp.dma_start(b1_cols[:, :], columns_of(b1, F), allow_slow_non_contiguous=True).then_inc(w_in, 16)
            sp.dma_start(b2_row[:, :], rows_of(b2, 1, 0, D)).then_inc(w_in, 16)

        @block.gpsimd
        def _(pool):
            pool.memset(ones[:, :], 1.0).then_inc(one_set, 1)
            pool.wait_ge(x_in, 16)
            for t in range(NT):
                pool.tensor_tensor(g.x[:, t, :], g.x[:, t, :], z[:, t, :], op=ALU.add).then_inc(plus, 1)

        @block.tensor
        def _(pe):
            pe.wait_ge(w_in, 64)
            pe.wait_ge(one_set, 1)
            for n, (f, k) in enumerate(ups):
                a, b = TOKENS[k]
                if n >= 4:
                    pe.wait_ge(gelu_done, n - 3)
                for c in range(KC):
                    last = pe.matmul(up_ps[n % 4][:, 0:b - a], up_w[:, c, f * 128:(f + 1) * 128], nT[:, c, a:b],
                                     start=(c == 0), stop=(c == KC - 1))
                last.then_inc(up_done, 1)
            pe.wait_ge(gelu_done, len(ups))
            for t in range(NT):
                if t >= 2:
                    pe.wait_ge(added, t - 1)
                for a in range(2):
                    cols = slice(a * 384, (a + 1) * 384)
                    pe.matmul(down_ps[t % 2][:, a, 0:384], ones[:, :], b2_row[:, cols], start=True, stop=False)
                    for f in range(FC):
                        last = pe.matmul(down_ps[t % 2][:, a, 0:384], inner[:, f, t * TP:(t + 1) * TP],
                                         down_w[:, f, cols], start=False, stop=(f == FC - 1))
                last.then_inc(down_done, 1)

        @block.scalar
        def _(act):
            act.wait_ge(w_in, 64)
            for n, (f, k) in enumerate(ups):
                a, b = TOKENS[k]
                act.wait_ge(up_done, n + 1)
                act.activation(inner[:, f, a:b], up_ps[n % 4][:, 0:b - a], ACT.Gelu,
                               bias=b1_cols[:, f:f + 1]).then_inc(gelu_done, 1)

        @block.vector
        def _(dve):
            for t in range(NT):
                dve.wait_ge(down_done, t + 1)
                dve.wait_ge(plus, t + 1)
                x_t = g.x[:, t, :].rearrange("p (a b) -> p a b", a=2)
                dve.tensor_tensor(x_t, x_t, down_ps[t % 2][:, :, 0:384], op=ALU.add).then_inc(added, 1)
            dve.wait_ge(added, NT)


def save_x(g):
    with ExitStack() as ctx:
        s = Scope(g, ctx)
        saved = s.sem("x_saved")
        block = s.block()

        @block.sync
        def _(sp):
            sp.dma_start(g.x_dram, g.x).then_inc(saved, 16)
            sp.wait_ge(saved, 16)


def mixed_layer(g, g1, b1, g2, b2, wr, br, wq, bq, wk, bk, wv, bv, wo, bo, wm, bm, w1, bf1, w2, bf2):
    with ExitStack() as ctx:
        s = Scope(g, ctx)
        z = s.sb("mixed_z", [TP, NT, D])
        normalize(g, "z_ln", g.x, z, None)
        save_x(g)
        with ExitStack() as attention:
            sa = Scope(g, attention)
            keep = sa.sb("keep", [TP, NT])
            picksT = sa.sb("picksT", [QT, 2, N])
            qT = sa.sb("qT", [128, KC, PICKED])
            kT = sa.sb("kT", [128, KC, N])
            v = sa.sb("v", [TP, NT, D])
            with ExitStack() as inner:
                si = Scope(g, inner)
                nT = si.sb("nT", [128, KC, N])
                picked_nT = si.sb("picked_nT", [128, KC, PICKED + 1])
                score_rows = si.sb("score_rows", [2, N])
                normalize(g, "n_ln", z, v, nT, g1, b1)
                with ExitStack() as inmost:
                    picks = Scope(g, inmost).sb("picks", [TP, NT, PICKED + 1])
                    pick_tokens(g, v, wr, br, keep, picks, picksT, picked_nT, score_rows, kT)
                mix_and_project(g, z, nT, picked_nT, score_rows, keep, wm, bm, wk, bk, wv, wq, bq, kT, v, qT)
            attend_picked(g, z, kT, v, qT, picksT, bv, wo, bo)
        with ExitStack() as inner:
            si = Scope(g, inner)
            nT = si.sb("n2T", [128, KC, N])
            with ExitStack() as inmost:
                n2 = Scope(g, inmost).sb("n2", [TP, NT, D])
                normalize(g, "n2_ln", z, n2, nT, g2, b2)
            feed_forward(g, z, nT, w1, bf1, w2, bf2)


def load_x(g, x):
    with ExitStack() as ctx:
        s = Scope(g, ctx)
        x_in = s.sem("x_in")
        block = s.block()

        @block.sync
        def _(sp):
            sp.dma_start(g.x, x.rearrange("(t p) d -> p t d", p=TP)).then_inc(x_in, 16)
            sp.wait_ge(x_in, 16)


def store_x(g, out):
    with ExitStack() as ctx:
        s = Scope(g, ctx)
        x_out = s.sem("x_out")
        block = s.block()

        @block.sync
        def _(sp):
            sp.dma_start(out.rearrange("(t p) d -> p t d", p=TP), g.x).then_inc(x_out, 16)
            sp.wait_ge(x_out, 16)


def build(nc, io, out):
    g = Shared()
    g.nc = nc
    scratch(g)
    free = sorted(nc.free_semaphores)
    first = min(i for i in free if all(k in free for k in range(i, i + SEMAPHORES)))
    g.semaphore_ids, g.semaphores_used, g.semaphores_live = range(first, first + SEMAPHORES), 0, 0
    with ExitStack() as ctx:
        s = Scope(g, ctx)
        g.ident = s.sb("ident", [128, 128])
        g.x_all = s.sb("x_all", [128, NT, D])
        g.x = g.x_all[0:TP, :, :]
        constants(g)
        load_x(g, io["x"])
        with ExitStack() as first:
            sf = Scope(g, first)
            g.counts_u = sf.sb("counts_u", [TP, NT, N], U16)
            g.far_u = sf.sb("far_u", [TP, NT, N], BF16)
            gat_layer(g, io["src"], io["dst"], io["edge_type_3"],
                      *[io["L0_gnn_" + k] for k in ("W_fc", "W_res", "attn_l", "attn_r")])
        moe_layer(g, *[io["L0_ffn_" + k] for k in ("router_w", "w1", "b1", "w2", "b2")])
        rgat_layers(g, *[io["L1_gnn_" + k] for k in ("W1", "q1", "k1", "b1", "W2", "q2", "k2", "b2")])
        mixed_layer(g, *[io["L1_ffn_" + k] for k in (
            "g1", "b1", "g2", "b2", "Wr", "br", "Wq", "bq", "Wk", "bk", "Wv", "bv", "Wo", "bo", "Wm", "bm",
            "W1", "bf1", "W2", "bf2")])
        store_x(g, out)


def kernel(**inputs):
    import concourse.bacc as bacc
    from concourse.bass_utils import run_bass_kernel_spmd

    nc = bacc.Bacc("TRN2", target_bir_lowering=False, num_devices=1)
    arrays, io = {}, {}
    for name, a in inputs.items():
        a = np.ascontiguousarray(a)
        a = a.reshape(a.shape or (1,))
        arrays[f"in_{name}"] = a
        io[name] = nc.dram_tensor(f"in_{name}", a.shape, mybir.dt.from_np(a.dtype), kind="ExternalInput").ap()
    out = nc.dram_tensor("out", (N, D), F32, kind="ExternalOutput").ap()
    build(nc, io, out)
    return run_bass_kernel_spmd(nc, [arrays], core_ids=[0]).results[0]["out"]
```

```python
from contextlib import ExitStack

import numpy as np

import concourse.bass as bass
from concourse import mybir

F32 = mybir.dt.float32
BF16 = mybir.dt.bfloat16
U16 = mybir.dt.uint16
I32 = mybir.dt.int32
FR = mybir.dt.float32r
ALU = mybir.AluOpType
ACT = mybir.ActivationFunctionType
AX_X = mybir.AxisListType.X

N = 1250
D = 768
E = 20000
R = 3
TP = 125
NT = N // TP
ET = E // TP
EH = ET // 2
KEYS = R * N
KT = KEYS // TP
KC = D // 128
SEMAPHORES = 138
SOFTWARE_SEMAPHORES = 11
FAR = -1.0e30


class Shared:
    pass


class Scope:

    ROOM = 40

    def __init__(self, g, ctx):
        self.g, self.nc, self.ctx = g, g.nc, ctx
        if not g.semaphores_live and g.semaphores_used > len(g.semaphore_ids) - self.ROOM:
            g.nc.all_engine_barrier(sems_to_clear=g.semaphore_ids)
            g.semaphores_used = 0

    def sb(self, name, shape, dt=F32):
        return self.ctx.enter_context(self.nc.sbuf_tensor(name, shape, dt))

    def ps(self, name, shape):
        return self.ctx.enter_context(self.nc.psum_tensor(name, shape, F32))

    def sem(self, name):
        handle = self.nc.alloc_semaphore(name, self.g.semaphore_ids[self.g.semaphores_used])
        self.g.semaphores_used += 1
        self.g.semaphores_live += 1
        self.ctx.callback(self.give_back, handle)
        return handle

    def software_sem(self, name):
        return self.nc.alloc_semaphore(name, self.g.software_ids.pop())

    def give_back(self, handle):
        self.g.semaphores_live -= 1
        self.nc.release_semaphore(handle)

    def sems(self, name, n):
        return [self.sem(f"{name}{i}") for i in range(n)]

    def block(self):
        return self.ctx.enter_context(self.nc.Block())


def rows_of(ap, partitions, offset, width):
    return bass.AP(tensor=ap.tensor, offset=offset, ap=[[0, partitions], [1, width]])


def chain(engine, sem):
    count = [0]

    def link(instruction):
        count[0] += 1
        instruction.then_inc(sem, 1)
        engine.wait_ge(sem, count[0])

    return link


def constants(g):
    with ExitStack() as ctx:
        s = Scope(g, ctx)
        ident_zero, ident_done = s.sem("ident_zero"), s.sem("ident_done")
        block = s.block()

        @block.gpsimd
        def _(pool):
            pool.memset(g.ident[:, :], 0.0).then_inc(ident_zero, 1)
            pool.wait_ge(ident_zero, 1)
            pool.affine_select(out=g.ident[:, :], in_=g.ident[:, :], compare_op=ALU.not_equal, fill=1.0,
                               base=0, pattern=[[-1, 128]], channel_multiplier=1).then_inc(ident_done, 1)
            pool.wait_ge(ident_done, 1)


def count_edges(g, src, dst, etype):
    with ExitStack() as ctx:
        s = Scope(g, ctx)
        sb, sem = s.sb, s.sem

        edges_i = sb("edges_i", [EH, 3, 2, TP], I32)
        edges_f = sb("edges_f", [EH, 3, 2, TP], F32)
        key_f = sb("key_f", [EH, 2, TP], F32)
        span = sb("span", [EH, 2, 2], F32)
        srcT = sb("srcT", [TP, ET + 1], F32)
        keyT = sb("keyT", [TP, ET + 1], F32)
        spans = sb("spans", [KT, 2, ET], F32)
        tile_no = sb("tile_no", [KT, ET], F32)
        first_key = sb("first_key", [KT, 1], F32)
        end_key = sb("end_key", [KT, 1], F32)
        hits = sb("hits", [KT, 2, ET], F32)
        range_f = sb("range_f", [KT, 2], F32)
        range_i = sb("range_i", [KT, 2], I32)
        ranges = sb("ranges", [1, 2 * KT], I32)
        number = sb("number", [TP, KEYS], U16)
        src_hot = [sb(f"src_hot{u}", [TP, N], BF16) for u in range(2)]
        key_hot = [sb(f"key_hot{u}", [TP, TP], BF16) for u in range(2)]
        zeros = sb("zeros", [TP, 512], BF16)
        cnt = [sb(f"cnt{b}", [TP, N], F32) for b in range(2)]
        far = [sb(f"far{b}", [TP, N], BF16) for b in range(2)]
        sums = [s.ps(f"sums{b}", [TP, 3, 512]) for b in range(2)]
        turned = [s.ps(f"turned{b}", [TP, 512]) for b in range(2)]
        sums_flat = [x[:, :, :].rearrange("p a b -> p (a b)") for x in sums]

        loaded = sem("edges_loaded")
        spans_out = sem("spans_out")
        spans_in = sem("spans_in")
        ranges_out = sem("ranges_out")
        ranges_in = sem("ranges_in")
        numbers = sem("numbers")
        v_chain = sem("v_chain")
        keys_done = sem("keys_done")
        edges_turned = sem("edges_turned")
        columns_done = sem("columns_done")
        span_done = sem("span_done")
        range_done = sem("range_done")
        hot_ready = [sem(f"hot_ready{u}") for u in range(2)]
        hot_used = [sem(f"hot_used{u}") for u in range(2)]
        sums_done = sem("sums_done")
        sums_copied = sem("sums_copied")
        far_done = sem("far_done")
        far_out = [sem(f"far_out{b}") for b in range(2)]
        far_free = [sem(f"far_free{b}") for b in range(2)]
        turned_done = [sem(f"turned_done{b}") for b in range(2)]
        turned_copied = [sem(f"turned_copied{b}") for b in range(2)]

        groups = [(0, 4), (4, 8), (8, NT)]
        block = s.block()

        def run_over_keys(engine, count, finish):
            count(0, 0)
            count(0, 1)
            finish(0, 0)
            with engine.Fori(1, KT // 2) as i2:
                count(i2, 0)
                finish(i2 - 1, 1)
                count(i2, 1)
                finish(i2, 0)
            finish(KT // 2 - 1, 1)

        @block.sync
        def _(sp):
            for i, v in enumerate((src, dst, etype)):
                sp.dma_start(edges_i[:, i, :, :], v.rearrange("(c t p) -> t c p", c=2, p=TP)).then_inc(loaded, 16)
            sp.wait_ge(span_done, 2)
            for i in range(2):
                sp.dma_start(g.span_dram[i, :, :].rearrange("c t -> t c"), span[:, i, :],
                             allow_slow_non_contiguous=True).then_inc(spans_out, 16)
            sp.wait_ge(spans_out, 32)
            sp.dma_start(spans[:, :, :].rearrange("k i t -> k (i t)"),
                         rows_of(g.span_dram, KT, 0, 2 * ET)).then_inc(spans_in, 16)
            sp.wait_ge(range_done, 1)
            sp.dma_start(g.range_dram, range_i[:, :]).then_inc(ranges_out, 16)
            sp.wait_ge(ranges_out, 16)
            sp.dma_start(ranges[:, :], rows_of(g.range_dram, 1, 0, 2 * KT)).then_inc(ranges_in, 16)
            for b in range(2):
                sp.nop().then_inc(far_free[b], 1)
            with sp.Fori(0, KT // 2) as i2:
                for b in range(2):
                    sp.wait_ge(far_done, i2 * 2 + (b + 3))
                    sp.dma_start(g.far_dram[bass.ds((i2 * 2 + b) * TP, TP), :], far[b][:, :]).then_inc(far_out[b], 16)
                for b in range(2):
                    sp.wait_ge(far_out[b], i2 * 16 + 16)
                    sp.nop().then_inc(far_free[b], 1)

        @block.gpsimd
        def _(pool):
            pool.iota(number[:, :], [[1, KEYS]], base=0, channel_multiplier=0).then_inc(numbers, 1)
            pool.iota(tile_no[:, :], [[1, ET]], base=-ET, channel_multiplier=0,
                      allow_small_or_imprecise_dtypes=True).then_inc(numbers, 1)
            pool.iota(first_key[:, :], [[0, 1]], base=0, channel_multiplier=TP,
                      allow_small_or_imprecise_dtypes=True).then_inc(numbers, 1)
            pool.iota(end_key[:, :], [[0, 1]], base=TP, channel_multiplier=TP,
                      allow_small_or_imprecise_dtypes=True).then_inc(numbers, 1)
            pool.memset(srcT[:, ET:ET + 1], -1.0).then_inc(numbers, 1)
            pool.memset(keyT[:, ET:ET + 1], -1.0).then_inc(numbers, 1)
            pool.memset(zeros[:, :], 0.0).then_inc(numbers, 1)

        @block.vector
        def _(dve):
            link = chain(dve, v_chain)
            dve.wait_ge(loaded, 48)
            link(dve.tensor_copy(edges_f[:, :, :, :], edges_i[:, :, :, :]))
            link(dve.scalar_tensor_tensor(out=key_f[:, :, :], in0=edges_f[:, 1, :, :], scalar=float(R),
                                          in1=edges_f[:, 2, :, :], op0=ALU.mult, op1=ALU.add))
            dve.tensor_reduce(out=span[:, 0, :], in_=key_f[:, :, :], op=ALU.min, axis=AX_X).then_inc(span_done, 1)
            dve.tensor_reduce(out=span[:, 1, :], in_=key_f[:, :, :], op=ALU.max, axis=AX_X).then_inc(span_done, 1)
            dve.nop().then_inc(keys_done, 1)
            dve.wait_ge(edges_turned, 1)
            dve.tensor_copy(srcT[:, 0:ET], turned[0][:, 0:ET]).then_inc(columns_done, 1)
            dve.tensor_copy(keyT[:, 0:ET], turned[1][:, 0:ET]).then_inc(columns_done, 1)
            dve.wait_ge(spans_in, 16)
            dve.wait_ge(numbers, 7)
            link(dve.scalar_tensor_tensor(out=hits[:, 0, :], in0=spans[:, 1, :], scalar=first_key[:, 0:1],
                                          in1=tile_no[:, :], op0=ALU.is_ge, op1=ALU.mult))
            link(dve.tensor_scalar(tile_no[:, :], tile_no[:, :], float(ET + 1), None, op0=ALU.add))
            link(dve.scalar_tensor_tensor(out=hits[:, 1, :], in0=spans[:, 0, :], scalar=end_key[:, 0:1],
                                          in1=tile_no[:, :], op0=ALU.is_lt, op1=ALU.mult))
            link(dve.tensor_reduce(out=range_f[:, 0:1], in_=hits[:, 0, :], op=ALU.min, axis=AX_X))
            link(dve.tensor_reduce(out=range_f[:, 1:2], in_=hits[:, 1, :], op=ALU.max, axis=AX_X))
            link(dve.tensor_scalar(range_f[:, 0:1], range_f[:, 0:1], float(ET), float(ET - 1),
                                   op0=ALU.add, op1=ALU.min))
            link(dve.scalar_tensor_tensor(out=range_f[:, 1:2], in0=range_f[:, 0:1], scalar=1.0,
                                          in1=range_f[:, 1:2], op0=ALU.add, op1=ALU.max))
            dve.tensor_copy(range_i[:, :], range_f[:, :]).then_inc(range_done, 1)
            dve.wait_ge(columns_done, 2)
            dve.wait_ge(ranges_in, 16)
            for b in range(2):
                dve.nop().then_inc(far_done, 1)
            turn = dve.alloc_register("hot_turn")
            dve.reg_mov(turn, 1)

            def count(i, b):
                lo = dve.value_load(ranges[0:1, bass.ds((i * 2 + b) * 2, 1)], min_val=0, max_val=ET - 1)
                hi = dve.value_load(ranges[0:1, bass.ds((i * 2 + b) * 2 + 1, 1)], min_val=1, max_val=ET)
                with dve.Fori(lo, hi, 2) as t:
                    for u in range(2):
                        dve.wait_ge(hot_used[u], turn)
                        dve.tensor_scalar(src_hot[u][:, :], number[:, 0:N], srcT[:, bass.ds(t + u, 1)], None,
                                          op0=ALU.is_equal)
                        dve.tensor_scalar(key_hot[u][:, :], number[:, bass.ds((i * 2 + b) * TP, TP)],
                                          keyT[:, bass.ds(t + u, 1)], None,
                                          op0=ALU.is_equal).then_inc(hot_ready[u], 1)
                    dve.reg_add(turn, turn, 1)

            def mask(i, b):
                dve.wait_ge(sums_copied, i * 2 + (b + 1))
                dve.wait_ge(far_free[b], i + 1)
                dve.tensor_scalar(far[b][:, :], cnt[b][:, :], 0.5, FAR, op0=ALU.is_lt,
                                  op1=ALU.mult).then_inc(far_done, 1)

            run_over_keys(dve, count, mask)

        @block.tensor
        def _(pe):
            pe.wait_ge(keys_done, 1)
            for c in range(2):
                pe.transpose(turned[0][:, c * EH:(c + 1) * EH], edges_f[:, 0, c, :], g.ident[0:EH, 0:EH])
                last = pe.transpose(turned[1][:, c * EH:(c + 1) * EH], key_f[:, c, :], g.ident[0:EH, 0:EH])
            last.then_inc(edges_turned, 1)
            pe.wait_ge(columns_done, 2)
            pe.wait_ge(numbers, 7)
            pe.wait_ge(ranges_in, 16)
            for b in range(2):
                pe.nop().then_inc(hot_used[b], 1)
                pe.nop().then_inc(turned_copied[b], 1)
            turn = pe.alloc_register("sum_turn")
            pe.reg_mov(turn, 1)

            def count(i, b):
                lo = pe.value_load(ranges[0:1, bass.ds((i * 2 + b) * 2, 1)], min_val=0, max_val=ET - 1)
                hi = pe.value_load(ranges[0:1, bass.ds((i * 2 + b) * 2 + 1, 1)], min_val=1, max_val=ET)
                for k in range(3):
                    w = min(512, N - 512 * k)
                    pe.matmul(sums_flat[b][:, 512 * k:512 * k + w], zeros[:, 0:TP], zeros[:, 0:w],
                              start=True, stop=False, skip_group_check=True)
                with pe.Fori(lo, hi, 2) as t:
                    for u in range(2):
                        pe.wait_ge(hot_ready[u], turn)
                        for k in range(3):
                            w = min(512, N - 512 * k)
                            last = pe.matmul(sums_flat[b][:, 512 * k:512 * k + w], key_hot[u][:, :],
                                             src_hot[u][:, 512 * k:512 * k + w],
                                             start=False, stop=False, skip_group_check=True)
                        last.then_inc(hot_used[u], 1)
                    pe.reg_add(turn, turn, 1)
                pe.matmul(sums_flat[b][:, 0:1], zeros[:, 0:TP], zeros[:, 0:1], start=False, stop=True,
                          skip_group_check=True).then_inc(sums_done, 1)

            def turn_counts(i, b):
                pe.wait_ge(sums_copied, i * 2 + (b + 1))
                for k, (s0, s1) in enumerate(groups):
                    n = 3 * b + k
                    pe.wait_ge(turned_copied[n % 2], i * 3 + (n // 2 + 1))
                    for s in range(s0, s1):
                        last = pe.transpose(turned[n % 2][:, (s - s0) * TP:(s - s0 + 1) * TP],
                                            cnt[b][:, s * TP:(s + 1) * TP], g.ident[0:TP, 0:TP])
                    last.then_inc(turned_done[n % 2], 1)

            run_over_keys(pe, count, turn_counts)

        @block.scalar
        def _(act):
            def copy_counts(i, b):
                act.wait_ge(sums_done, i * 2 + (b + 1))
                act.wait_ge(far_done, i * 2 + (b + 1))
                act.activation(cnt[b][:, :], sums_flat[b][:, 0:N], ACT.Copy).then_inc(sums_copied, 1)

            def keep_turned(i, b):
                for k, (s0, s1) in enumerate(groups):
                    n = 3 * b + k
                    act.wait_ge(turned_done[n % 2], i * 3 + (n // 2 + 1))
                    act.activation(g.counts[:, s0:s1, bass.ds((i * 2 + b) * TP, TP)],
                                   turned[n % 2][:, 0:(s1 - s0) * TP].rearrange("p (s k) -> p s k", k=TP),
                                   ACT.Copy).then_inc(turned_copied[n % 2], 1)

            run_over_keys(act, copy_counts, keep_turned)
            act.nop()


def turn_tile(pe, g, out, rows, t, tiled):
    for c in range(KC):
        last = pe.transpose(out[c // 3][:, (c % 3) * TP:(c % 3 + 1) * TP], rows[:, t, c * 128:(c + 1) * 128],
                            g.ident[0:TP, 0:TP])
    last.then_inc(tiled, 1)


def normalize(g, tag, src, dst, dstT, gamma=None, beta=None, eps=1e-5):
    with ExitStack() as ctx:
        s = Scope(g, ctx)
        parts = s.sb(f"{tag}_parts", [TP, NT, 2, 6])
        mean_var = s.sb(f"{tag}_mean_var", [TP, NT, 2])
        var = s.sb(f"{tag}_var", [TP, NT])
        inv = s.sb(f"{tag}_inv", [TP, NT])
        std_inv = s.sb(f"{tag}_std_inv", [TP, NT])
        square = s.sb(f"{tag}_square", [TP, NT])
        affine = s.sb(f"{tag}_affine", [TP, 2, D]) if gamma is not None else None
        banks = [[s.ps(f"{tag}_turn{i}{j}", [128, 512]) for j in range(2)] for i in range(2)] if dstT is not None else []
        v_chain, inv_done, root_done = s.sem(f"{tag}_chain"), s.sem(f"{tag}_inv_done"), s.sem(f"{tag}_root_done")
        rows_done, turned, copied = s.sem(f"{tag}_rows"), s.sem(f"{tag}_turned"), s.sem(f"{tag}_copied")
        affine_in = s.sem(f"{tag}_affine_in")
        block = s.block()

        if gamma is not None:
            @block.sync
            def _(sp):
                for i, v in enumerate((gamma, beta)):
                    sp.dma_start(affine[:, i, :], rows_of(v, TP, 0, D)).then_inc(affine_in, 16)

        @block.vector
        def _(dve):
            link = chain(dve, v_chain)
            for t in range(NT):
                for i in range(2):
                    last = dve.bn_stats(parts[:, t, i, :], src[:, t, i * 384:(i + 1) * 384])
            link(last)
            for t in range(NT):
                last = dve.bn_aggr(mean_var[:, t, :], parts[:, t, :, :].rearrange("p a b -> p (a b)"))
            link(last)
            link(dve.tensor_scalar(var[:, :], mean_var[:, :, 1], eps, None, op0=ALU.add))
            dve.reciprocal(inv[:, :], var[:, :]).then_inc(inv_done, 1)
            dve.wait_ge(root_done, 1)
            link(dve.tensor_tensor(square[:, :], std_inv[:, :], std_inv[:, :], op=ALU.mult))
            link(dve.tensor_tensor(square[:, :], square[:, :], var[:, :], op=ALU.mult))
            link(dve.tensor_scalar(square[:, :], square[:, :], -0.5, 1.5, op0=ALU.mult, op1=ALU.add))
            link(dve.tensor_tensor(std_inv[:, :], std_inv[:, :], square[:, :], op=ALU.mult))
            if gamma is None:
                for t in range(NT):
                    dve.tensor_scalar(dst[:, t, :], src[:, t, :], mean_var[:, t, 0:1], std_inv[:, t:t + 1],
                                      op0=ALU.subtract, op1=ALU.mult).then_inc(rows_done, 1)
            else:
                dve.wait_ge(affine_in, 32)
                for t in range(NT):
                    link(dve.tensor_scalar(dst[:, t, :], src[:, t, :], mean_var[:, t, 0:1], std_inv[:, t:t + 1],
                                           op0=ALU.subtract, op1=ALU.mult))
                    link(dve.tensor_tensor(dst[:, t, :], dst[:, t, :], affine[:, 0, :], op=ALU.mult))
                    dve.tensor_tensor(dst[:, t, :], dst[:, t, :], affine[:, 1, :], op=ALU.add).then_inc(rows_done, 1)
            dve.wait_ge(rows_done, NT)

        @block.scalar
        def _(act):
            act.wait_ge(inv_done, 1)
            act.activation(std_inv[:, :], inv[:, :], ACT.Sqrt).then_inc(root_done, 1)
            if dstT is not None:
                for t in range(NT):
                    act.wait_ge(turned, t + 1)
                    for j in range(2):
                        act.activation(dstT[:, 3 * j:3 * j + 3, t * TP:(t + 1) * TP],
                                       banks[t % 2][j][:, 0:3 * TP].rearrange("p (c t) -> p c t", t=TP),
                                       ACT.Copy).then_inc(copied, 1)
                act.wait_ge(copied, 2 * NT)

        if dstT is not None:
            @block.tensor
            def _(pe):
                for t in range(NT):
                    pe.wait_ge(rows_done, t + 1)
                    if t >= 2:
                        pe.wait_ge(copied, 2 * (t - 1))
                    turn_tile(pe, g, banks[t % 2], dst, t, turned)


def merge_edges(g):
    with ExitStack() as ctx:
        s = Scope(g, ctx)
        masks = [s.sb(f"masks{i}", [TP, R, N], BF16) for i in range(2)]
        masks_in, merged, summed = s.sems("masks_in", 2), s.sem("masks_merged"), s.sem("counts_summed")
        v_chain, saved = s.sem("merge_vc"), s.sem("counts_saved")
        block = s.block()

        @block.scalar
        def _(act):
            act.dma_start(g.counts_dram, g.counts[:, :, :]).then_inc(saved, 16)
            act.wait_ge(saved, 16)

        @block.sync
        def _(sp):
            for t in range(NT):
                if t >= 2:
                    sp.wait_ge(merged, t - 1)
                sp.dma_start(masks[t % 2][:, :, :], g.far_dram[t * TP * R:(t + 1) * TP * R, :]
                             .rearrange("(d r) s -> d r s", r=R)).then_inc(masks_in[t % 2], 16)

        @block.vector
        def _(dve):
            link = chain(dve, v_chain)
            for t in range(NT):
                dve.wait_ge(masks_in[t % 2], t // 2 * 16 + 16)
                link(dve.tensor_tensor(g.far_u[:, t, :], masks[t % 2][:, 0, :], masks[t % 2][:, 1, :], op=ALU.max))
                dve.tensor_tensor(g.far_u[:, t, :], g.far_u[:, t, :], masks[t % 2][:, 2, :],
                                  op=ALU.max).then_inc(merged, 1)
                by_rel = g.counts[:, t, :].rearrange("p (d r) -> p r d", r=R)
                link(dve.tensor_tensor(g.counts_u[:, t, :], by_rel[:, 0, :], by_rel[:, 1, :], op=ALU.add))
                dve.tensor_tensor(g.counts_u[:, t, :], g.counts_u[:, t, :], by_rel[:, 2, :],
                                  op=ALU.add).then_inc(summed, 1)
            dve.wait_ge(merged, NT)
            dve.wait_ge(summed, NT)


def project_gat(g, hT, w_fc, w_res, attn_l, attn_r, ft, res, ks, qd):
    H, DH = 12, 64
    with ExitStack() as ctx:
        s = Scope(g, ctx)
        w2 = s.sb("gat_w2", [DH, 2, 2 * DH])
        pair = s.sb("gat_pair", [128, 2, 128])
        attn = s.sb("gat_attn", [2 * H, DH])
        attnT = s.sb("gat_attnT", [DH, 2 * H])
        score_w = s.sb("gat_score_w", [128, KC, 2, H])
        score_flat = score_w[:, :, :, :].rearrange("p c l h -> p (c l h)")
        out_ps = [s.ps(f"gat_out{i}", [128, 3, 512]) for i in range(2)]
        chunks = [o[0:TP, :, :].rearrange("p a b -> p (a b)").rearrange("p (c i e) -> p c i e", c=KC, i=2)
                  for o in out_ps]
        score_ps = [s.ps(f"gat_score{i}", [128, 512]) for i in range(2)]
        w_in = s.sem("gat_w_in")
        zeroed, w_turned, w_copied = s.sem("gat_zeroed"), s.sem("gat_w_turned"), s.sem("gat_w_copied")
        s_made, s_copied = s.sem("gat_s_made"), s.sem("gat_s_copied")
        made, values_out, rest_out = s.sem("gat_made"), s.sem("gat_values_out"), s.sem("gat_rest_out")
        block = s.block()

        @block.sync
        def _(sp):
            for i, w in enumerate((w_fc, w_res)):
                for k in range(2):
                    sp.dma_start(w2[:, i, k * DH:(k + 1) * DH], w).then_inc(w_in, 16)
            for i, a in enumerate((attn_l, attn_r)):
                sp.dma_start(attn[i * H:(i + 1) * H, :], a).then_inc(w_in, 16)

        @block.gpsimd
        def _(pool):
            pool.memset(pair[:, :, :], 0.0).then_inc(zeroed, 1)
            pool.memset(score_w[:, :, :, :], 0.0).then_inc(zeroed, 1)
            pool.memset(ft[:, :, :, DH:DH + 1], 1.0).then_inc(zeroed, 1)

        @block.vector
        def _(dve):
            dve.wait_ge(w_turned, 1)
            dve.wait_ge(zeroed, 2)
            for i in range(2):
                for k in range(2):
                    dve.tensor_copy(pair[k * DH:(k + 1) * DH, i, k * DH:(k + 1) * DH],
                                    out_ps[0][k * DH:(k + 1) * DH, i, 0:DH])
            dve.tensor_copy(attnT[:, :], out_ps[0][0:DH, 2, 0:2 * H]).then_inc(w_copied, 1)
            dve.wait_ge(s_made, 1)
            for k in range(2):
                for lr in range(2):
                    first = lr * H + k
                    last = dve.tensor_copy(score_flat[k * DH:(k + 1) * DH, first:first + 26 * (KC - 1) + 1:26],
                                           score_ps[0][k * DH:(k + 1) * DH, lr * H + k:lr * H + H:2])
            last.then_inc(s_copied, 1)
            for t in range(NT):
                dve.wait_ge(made, t + 1)
                dve.tensor_copy(ks[:, t, :], score_ps[t % 2][0:TP, 0:H])
                dve.tensor_copy(qd[:, t, :], score_ps[t % 2][0:TP, H:2 * H]).then_inc(rest_out, 1)

        @block.tensor
        def _(pe):
            pe.wait_ge(w_in, 96)
            for i in range(2):
                pe.transpose(out_ps[0][:, i, 0:DH], w2[:, i, :], g.ident[0:DH, 0:DH])
            pe.transpose(out_ps[0][0:DH, 2, 0:2 * H], attn[:, :], g.ident[0:2 * H, 0:2 * H]).then_inc(w_turned, 1)
            pe.wait_ge(w_copied, 1)
            pe.matmul(score_ps[0][:, 0:2 * H], w2[:, 0, :], attnT[:, :], start=True, stop=True).then_inc(s_made, 1)
            pe.wait_ge(s_copied, 1)
            for t in range(NT):
                if t >= 2:
                    pe.wait_ge(values_out, t - 1)
                    pe.wait_ge(rest_out, t - 1)
                for c in range(KC):
                    x_c = hT[:, c, t * TP:(t + 1) * TP]
                    pe.matmul(out_ps[t % 2][0:TP, c // 2, (c % 2) * 256:(c % 2 + 1) * 256], x_c,
                              pair[:, :, :].rearrange("p i e -> p (i e)"), start=True, stop=True)
                    last = pe.matmul(score_ps[t % 2][0:TP, 0:2 * H], x_c,
                                     score_w[:, c, :, :].rearrange("p l h -> p (l h)"),
                                     start=(c == 0), stop=(c == KC - 1))
                last.then_inc(made, 1)

        @block.scalar
        def _(act):
            for t in range(NT):
                act.wait_ge(made, t + 1)
                act.activation(res[:, t, :].rearrange("p (c e) -> p c e", c=KC), chunks[t % 2][:, :, 1, :], ACT.Copy)
                act.activation(ft[:, t, :, 0:DH].rearrange("p (c k) e -> p c k e", k=2),
                               chunks[t % 2][:, :, 0, :].rearrange("p c (k e) -> p c k e", k=2),
                               ACT.Copy).then_inc(values_out, 1)
            act.wait_ge(values_out, NT)


def greatest(g, tag, heads, group, row, mask_of, ks, qd, ks_low, shifted, score_of=None, beside=None):
    CH = ks.shape[2]
    rels = CH // heads
    NG = CH // group
    RB = len(row)
    MB = 4
    with ExitStack() as ctx:
        s = Scope(g, ctx)
        least = s.sb(f"{tag}_least", [TP, CH])
        most = s.sb(f"{tag}_most", [TP, NT, CH])
        leaky = s.sb(f"{tag}_leaky", [TP, NT, CH])
        top = s.sb(f"{tag}_top", [TP, NT, heads])
        rowsT = s.sb(f"{tag}_rowsT", [CH, N])
        low = s.sb(f"{tag}_low", [CH, 1])
        junk = [s.sb(f"{tag}_junk{i}", [TP, N]) for i in range(2)]
        mask = [s.sb(f"{tag}_mask{i}", [TP, N], BF16) for i in range(MB)] if mask_of else None
        turn_ps = s.ps(f"{tag}_turn", [CH, 3, 512])
        score_ps = s.ps(f"{tag}_score_ps", [TP, 512]) if score_of else None
        scored, scores_out = s.sem(f"{tag}_scored"), s.sem(f"{tag}_scores_out")
        turned, copied, low_done = s.sem(f"{tag}_turned"), s.sem(f"{tag}_copied"), s.sem(f"{tag}_low_done")
        out_done, low_out, least_in = s.sem(f"{tag}_rows_out"), s.sem(f"{tag}_low_out"), s.sem(f"{tag}_least_in")
        row_in, mask_in = s.sems(f"{tag}_row_in", RB), s.sems(f"{tag}_mask_in", MB)
        junked, v_chain, low_scaled = s.sem(f"{tag}_junked"), s.sem(f"{tag}_vc"), s.sem(f"{tag}_low_scaled")
        other = beside(s) if beside else None
        block = s.block()

        @block.tensor
        def _(pe):
            if score_of:
                hT, weights = score_of
                for t in range(NT):
                    for c in range(KC):
                        last = pe.matmul(score_ps[:, t * 2 * CH:(t + 1) * 2 * CH], hT[:, c, t * TP:(t + 1) * TP],
                                         weights[:, c, :, :, :].rearrange("p i r h -> p (i r h)"),
                                         start=(c == 0), stop=(c == KC - 1))
                last.then_inc(scored, 1)
                pe.wait_ge(scores_out, 1)
            for t in range(NT):
                last = pe.transpose(turn_ps[:, t // 4, (t % 4) * TP:(t % 4 + 1) * TP], ks[:, t, :],
                                    g.ident[0:TP, 0:TP])
            last.then_inc(turned, 1)
            if other:
                other.tensor(pe)

        if other:
            @block.gpsimd
            def _(pool):
                other.pool(pool)

        @block.scalar
        def _(act):
            if other:
                other.load(act)
            act.wait_ge(turned, 1)
            act.activation(rowsT[:, 0:8 * TP].rearrange("p (a b) -> p a b", a=2), turn_ps[:, 0:2, 0:4 * TP],
                           ACT.Copy).then_inc(copied, 1)
            act.activation(rowsT[:, 8 * TP:N], turn_ps[:, 2, 0:2 * TP], ACT.Copy).then_inc(copied, 1)
            act.activation(ks_low[:, :, :], ks[:, :, :], ACT.Copy, scale=0.2).then_inc(low_scaled, 1)
            if other:
                other.scalar(act)
            act.wait_ge(low_scaled, 1)

        @block.sync
        def _(sp):
            def load_masks(m):
                if m >= MB:
                    sp.wait_ge(junked, (m - MB + 1) * group)
                sp.dma_start(mask[m % MB][:, :], mask_of(m // NT, m % NT)).then_inc(mask_in[m % MB], 16)

            def load_rows(n):
                if n >= RB:
                    sp.wait_ge(junked, (n - RB + 1) * NT * group)
                src = bass.AP(tensor=g.rows_dram.tensor, offset=n * group * N, ap=[[0, TP], [N, group], [1, N]])
                sp.dma_start(row[n % RB], src).then_inc(row_in[n % RB], 16)

            if mask:
                for m in range(MB):
                    load_masks(m)
            sp.wait_ge(copied, 2)
            sp.dma_start(g.rows_dram[0:CH, :], rowsT[:, :]).then_inc(out_done, 16)
            sp.wait_ge(out_done, 16)
            for n in range(RB - 1):
                load_rows(n)
            sp.wait_ge(low_done, 1)
            sp.dma_start(g.low_dram[0:CH, :], low[:, :]).then_inc(low_out, 16)
            sp.wait_ge(low_out, 16)
            sp.dma_start(least[:, :], rows_of(g.low_dram, TP, 0, CH)).then_inc(least_in, 16)
            for n in range(NG):
                for t in range(NT if mask else 0):
                    if n * NT + t + MB < NG * NT:
                        load_masks(n * NT + t + MB)
                    if t == 0 and n + RB - 1 < NG:
                        load_rows(n + RB - 1)
                if not mask and n + RB - 1 < NG:
                    load_rows(n + RB - 1)

        @block.vector
        def _(dve):
            link = chain(dve, v_chain)
            if score_of:
                dve.wait_ge(scored, 1)
                parts = score_ps[:, 0:NT * 2 * CH].rearrange("p (t i c) -> p t i c", i=2, c=CH)
                dve.tensor_copy(qd[:, :, :], parts[:, :, 0, :])
                dve.tensor_copy(ks[:, :, :], parts[:, :, 1, :]).then_inc(scores_out, 1)
            dve.wait_ge(copied, 2)
            dve.tensor_reduce(out=low[:, :], in_=rowsT[:, :], op=ALU.min, axis=AX_X).then_inc(low_done, 1)
            for n in range(NG):
                dve.wait_ge(row_in[n % RB], n // RB * 16 + 16)
                for t in range(NT):
                    m = n * NT + t
                    if mask:
                        dve.wait_ge(mask_in[m % MB], m // MB * 16 + 16)
                    for k in range(group):
                        i = m * group + k
                        c = n * group + k
                        if i >= 2:
                            dve.wait_ge(junked, i - 1)
                        far = mask[m % MB][:, :] if mask else g.far_u[:, t, :]
                        dve.tensor_tensor_reduce(out=junk[i % 2][:, :], in0=far, in1=row[n % RB][:, k, :],
                                                 scale=1.0, scalar=3 * FAR, op0=ALU.add, op1=ALU.max,
                                                 accum_out=most[:, t, c:c + 1]).then_inc(junked, 1)
            dve.wait_ge(junked, CH * NT)
            dve.wait_ge(least_in, 16)
            all_tiles = least[:, :].unsqueeze(1).to_broadcast([TP, NT, CH])
            link(dve.tensor_tensor(most[:, :, :], most[:, :, :], all_tiles, op=ALU.max))
            link(dve.tensor_tensor(most[:, :, :], most[:, :, :], qd[:, :, :], op=ALU.add))
            link(dve.scalar_tensor_tensor(out=leaky[:, :, :], in0=most[:, :, :], scalar=0.2, in1=most[:, :, :],
                                          op0=ALU.mult, op1=ALU.max))
            link(dve.tensor_copy(top[:, :, :], leaky[:, :, 0:heads]))
            for r in range(1, rels):
                link(dve.tensor_tensor(top[:, :, :], top[:, :, :], leaky[:, :, r * heads:(r + 1) * heads],
                                       op=ALU.max))
            for r in range(rels):
                at = slice(r * heads, (r + 1) * heads)
                link(dve.tensor_tensor(shifted[:, :, 0, at], qd[:, :, at], top[:, :, :], op=ALU.subtract))
                link(dve.scalar_tensor_tensor(out=shifted[:, :, 1, at], in0=qd[:, :, at], scalar=0.2,
                                              in1=top[:, :, :], op0=ALU.mult, op1=ALU.subtract))


class RelationWeights:

    def __init__(self, s, g, layers, weights):
        self.g, self.layers, self.weights = g, layers, weights
        self.qk = [s.sb(f"relw_qk{n}", [128, KC, 2, q.shape[1]]) for n, (w, q, k) in enumerate(layers)]
        self.chunk = [s.sb(f"relw_chunk{i}", [128, D]) for i in range(2)]
        self.wT = [s.sb(f"relw_wT{i}", [128, KC, 128]) for i in range(2)]
        self.turn_ps = [s.ps(f"relw_turn{i}", [128, 2, 512]) for i in range(2)]
        self.out_ps = s.ps("relw_out", [128, 512])
        self.qk_in, self.chunk_in = s.sem("relw_qk_in"), s.sems("relw_chunk_in", 2)
        self.turned, self.copied, self.made = s.sem("relw_turned"), s.sem("relw_copied"), s.sem("relw_made")
        self.taken = s.sem("relw_taken")
        self.steps = [(n, r, c) for n in range(len(layers)) for r in range(R) for c in range(KC)]

    def load_chunk(self, act, i):
        n, r, c = self.steps[i]
        act.dma_start(self.chunk[i % 2][:, :], self.layers[n][0][r, c * 128:(c + 1) * 128, :]
                      ).then_inc(self.chunk_in[i % 2], 16)

    def load(self, act):
        for n, (w, q, k) in enumerate(self.layers):
            for i, v in enumerate((q, k)):
                act.dma_start(self.qk[n][:, :, i, :], v.rearrange("(c p) h -> p c h", p=128),
                              allow_slow_non_contiguous=True).then_inc(self.qk_in, 16)
        self.load_chunk(act, 0)
        self.load_chunk(act, 1)

    def pool(self, pool):
        pass

    def tensor(self, pe):
        pe.wait_ge(self.qk_in, 32 * len(self.layers))
        for i in range(len(self.steps) + 1):
            if i < len(self.steps):
                pe.wait_ge(self.chunk_in[i % 2], i // 2 * 16 + 16)
                if i >= 2:
                    pe.wait_ge(self.copied, i - 1)
                for f in range(KC):
                    last = pe.transpose(self.turn_ps[i % 2][:, f // 3, (f % 3) * 128:(f % 3 + 1) * 128],
                                        self.chunk[i % 2][:, f * 128:(f + 1) * 128], self.g.ident[:, :])
                last.then_inc(self.turned, 1)
            if i >= 1:
                n, r, c = self.steps[i - 1]
                H2 = 2 * self.weights[n].shape[4]
                at = (r * KC + c) * H2
                if n >= 1 and r == 0 and c == 0:
                    pe.wait_ge(self.taken, n)
                pe.wait_ge(self.copied, i)
                for f in range(KC):
                    last = pe.matmul(self.out_ps[:, at:at + H2], self.wT[(i - 1) % 2][:, f, :],
                                     self.qk[n][:, f, :, :].rearrange("p i h -> p (i h)"),
                                     start=(f == 0), stop=(f == KC - 1))
                last.then_inc(self.made, 1)

    def scalar(self, act):
        for i in range(len(self.steps)):
            act.wait_ge(self.turned, i + 1)
            if i + 2 < len(self.steps):
                self.load_chunk(act, i + 2)
            if i >= 2:
                act.wait_ge(self.made, i - 1)
            act.activation(self.wT[i % 2][:, :, :].rearrange("p (a b) d -> p a (b d)", a=2),
                           self.turn_ps[i % 2][:, :, 0:384], ACT.Copy).then_inc(self.copied, 1)
            if (i + 1) % (R * KC) == 0:
                n = i // (R * KC)
                H = self.weights[n].shape[4]
                act.wait_ge(self.made, i + 1)
                for r in range(R):
                    at = r * KC * 2 * H
                    last = act.activation(self.weights[n][:, :, :, r, :],
                                          self.out_ps[:, at:at + KC * 2 * H].rearrange("p (c i h) -> p c i h", i=2, h=H),
                                          ACT.Copy)
                last.then_inc(self.taken, 1)
        act.wait_ge(self.taken, len(self.layers))


class RelationValues:

    def __init__(self, s, g, tag, hT, w, b, bias, add):
        self.g, self.hT, self.w, self.b, self.bias, self.add = g, hT, w, b, bias, add
        self.bias_in, self.bias_added = s.sem(f"{tag}_bias_in"), s.sem(f"{tag}_bias_added")
        self.w_sb = [s.sb(f"{tag}_w{i}", [128, KC, D]) for i in range(2)]
        self.stage = [s.sb(f"{tag}_stage{i}", [TP, D]) for i in range(3)]
        self.out_ps = [s.ps(f"{tag}_out{i}", [TP, 2, 512]) for i in range(2)]
        self.w_in, self.made, self.out = s.sems(f"{tag}_w_in", 2), s.sem(f"{tag}_made"), s.sem(f"{tag}_taken")
        self.sent = s.sems(f"{tag}_sent", 3)

    def load_w(self, act, r):
        act.dma_start(self.w_sb[r % 2][:, :, :], self.w[r, :, :].rearrange("(c p) f -> p c f", p=128)
                      ).then_inc(self.w_in[r % 2], 16)

    def load(self, act):
        self.load_w(act, 0)
        self.load_w(act, 1)
        act.dma_start(self.bias[:, :], rows_of(self.b, TP, 0, D)).then_inc(self.bias_in, 16)

    def pool(self, pool):
        pool.wait_ge(self.bias_in, 16)
        for t in range(NT if self.add else 0):
            x_t = self.g.x[:, t, :]
            pool.tensor_tensor(x_t, x_t, self.bias[:, :], op=ALU.add).then_inc(self.bias_added, 1)
        if self.add:
            pool.wait_ge(self.bias_added, NT)

    def tensor(self, pe):
        for n in range(R * NT):
            r, t = divmod(n, NT)
            if t == 0:
                pe.wait_ge(self.w_in[r % 2], r // 2 * 16 + 16)
            if n >= 2:
                pe.wait_ge(self.out, n - 1)
            for a in range(2):
                for c in range(KC):
                    last = pe.matmul(self.out_ps[n % 2][:, a, 0:384], self.hT[:, c, t * TP:(t + 1) * TP],
                                     self.w_sb[r % 2][:, c, a * 384:(a + 1) * 384], start=(c == 0), stop=(c == KC - 1))
            last.then_inc(self.made, 1)

    def scalar(self, act):
        def send(n):
            r, t = divmod(n, NT)
            act.wait_ge(self.out, n + 1)
            act.dma_start(self.g.values_dram[r, t * TP:(t + 1) * TP, :], self.stage[n % 3][:, :]
                          ).then_inc(self.sent[n % 3], 16)

        for n in range(R * NT):
            r, t = divmod(n, NT)
            act.wait_ge(self.made, n + 1)
            if t == NT - 1 and r + 2 < R:
                self.load_w(act, r + 2)
            if n >= 3:
                act.wait_ge(self.sent[n % 3], n // 3 * 16)
            act.activation(self.stage[n % 3][:, :].rearrange("p (a b) -> p a b", a=2), self.out_ps[n % 2][:, :, 0:384],
                           ACT.Copy).then_inc(self.out, 1)
            if n >= 1:
                send(n - 1)
        send(R * NT - 1)
        for i in range(3):
            act.wait_ge(self.sent[i], R * NT // 3 * 16)


def attend(g, tag, heads, width, span, ks, ks_low, shifted, value_of, finish):
    CH = ks.shape[2]
    rels = CH // heads
    units = [(h, d) for h in range(heads) for d in range(0, NT, span)]
    per_bank = max(1, 512 // (width + 1))
    banks_of = -(-(width + 1) // 512)
    nbanks = -(-span // per_bank) if banks_of == 1 else span * banks_of
    W = span * TP
    steps = [(u, r, t) for u in range(len(units)) for t in range(NT) for r in range(rels)]
    per_unit = NT * rels
    with ExitStack() as ctx:
        s = Scope(g, ctx)
        rows = [s.sb(f"{tag}_rows{i}", [TP, rels, 2, W]) for i in range(2)]
        shiftedT = rows[1][0:2 * CH, :, :, :].rearrange("p r i w -> p (r i w)")[:, 0:N]
        high = [s.sb(f"{tag}_high{i}", [TP, W]) for i in range(3)]
        lowb = [s.sb(f"{tag}_lowb{i}", [TP, W]) for i in range(3)]
        wts = [s.sb(f"{tag}_wts{i}", [TP, W]) for i in range(3)]
        recip = s.sb(f"{tag}_recip", [TP, 2, span])
        stream = None if value_of else [s.sb(f"{tag}_values{i}", [TP, width + 1]) for i in range(4)]
        acc = [s.ps(f"{tag}_acc{i}", [TP, nbanks, 512]) for i in range(2)]
        turned, copied, out_done = s.sem(f"{tag}_g"), s.sem(f"{tag}_h"), s.sem(f"{tag}_i")
        rows_in, rows_used = s.sems(f"{tag}_rows_in", 2), s.sem(f"{tag}_rows_used")
        exp_done, max_done, wts_done, wts_used = (s.sem(f"{tag}_{n}") for n in ("exp", "max", "wts", "wts_used"))
        value_in, acc_done, acc_out = s.sems(f"{tag}_value_in", 4), s.sem(f"{tag}_acc_done"), s.sem(f"{tag}_acc_out")
        v_chain, ones = s.sem(f"{tag}_vc2"), s.sem(f"{tag}_ones")
        counts = s.sb(f"{tag}_counts", [TP, NT, KEYS], U16) if rels > 1 else g.counts_u
        counts_in = s.sems(f"{tag}_counts_in", 2)
        turn_ps2 = acc[1][0:2 * CH, :, :] if nbanks >= 3 else s.ps(f"{tag}_turn2", [2 * CH, 3, 512])
        block = s.block()

        def counts_of(r, t, at, w):
            if rels == 1:
                return counts[:, t, at:at + w]
            return counts[:, t, :].rearrange("p (d r) -> p r d", r=R)[:, r, at:at + w]

        def tile_of(u, d):
            if banks_of == 1:
                o = (d % per_bank) * (width + 1)
                return [(acc[u % 2][:, d // per_bank, o:o + width + 1], 0, width + 1)]
            return [(acc[u % 2][:, d * banks_of + b, 0:min(512, width + 1 - 512 * b)], 512 * b,
                     min(512 * b + 512, width + 1)) for b in range(banks_of)]

        @block.tensor
        def _(pe):
            for t in range(NT):
                last = pe.transpose(turn_ps2[:, t // 4, (t % 4) * TP:(t % 4 + 1) * TP],
                                    shifted[:, t, :, :].rearrange("p a c -> p (a c)"), g.ident[0:TP, 0:TP])
            last.then_inc(turned, 1)
            pe.wait_ge(copied, 2)
            for i, (u, r, t) in enumerate(steps):
                h, d0 = units[u]
                n_tiles = min(span, NT - d0)
                first, final = i % per_unit == 0, i % per_unit == per_unit - 1
                if first and u >= 2:
                    pe.wait_ge(acc_out, u - 1)
                if value_of:
                    v = value_of(h, t)
                else:
                    pe.wait_ge(value_in[i % 4], i // 4 * 16 + 16)
                    v = stream[i % 4][:, :]
                    if i == 0:
                        pe.wait_ge(ones, 4)
                pe.wait_ge(wts_done, i + 1)
                for d in range(n_tiles):
                    for o, c0, c1 in tile_of(u, d):
                        opens = first and (banks_of > 1 or d % per_bank == 0)
                        last = pe.matmul(o, wts[i % 3][:, d * TP:(d + 1) * TP], v[:, c0:c1],
                                         start=opens, stop=final, skip_group_check=True)
                last.then_inc(wts_used, 1)

        @block.scalar
        def _(act):
            act.wait_ge(turned, 1)
            act.activation(shiftedT[:, 0:8 * TP].rearrange("p (a b) -> p a b", a=2), turn_ps2[:, 0:2, 0:4 * TP],
                           ACT.Copy).then_inc(copied, 1)
            act.activation(shiftedT[:, 8 * TP:N], turn_ps2[:, 2, 0:2 * TP], ACT.Copy).then_inc(copied, 1)
            for i, (u, r, t) in enumerate(steps):
                h, d0 = units[u]
                w = min(span, NT - d0) * TP
                c = r * heads + h
                if i % per_unit == 0:
                    act.wait_ge(rows_in[u % 2], u // 2 * 16 * rels + 16 * rels)
                if i >= 3:
                    act.wait_ge(max_done, i - 2)
                    act.wait_ge(wts_done, i - 2)
                act.activation(high[i % 3][:, 0:w], rows[u % 2][:, r, 0, 0:w], ACT.Exp, bias=ks[:, t, c:c + 1])
                act.activation(lowb[i % 3][:, 0:w], rows[u % 2][:, r, 1, 0:w], ACT.Exp,
                               bias=ks_low[:, t, c:c + 1]).then_inc(exp_done, 1)

        def take_out(dve, link, u):
            h, d0 = units[u]
            n_tiles = min(span, NT - d0)
            dve.wait_ge(wts_used, (u + 1) * per_unit)
            for d in range(n_tiles):
                o, c0, c1 = tile_of(u, d)[-1]
                last = dve.tensor_scalar(recip[:, u % 2, d:d + 1], o[:, width - c0:width - c0 + 1], 1e-16, None,
                                         op0=ALU.add)
            link(last)
            link(dve.reciprocal(recip[:, u % 2, 0:n_tiles], recip[:, u % 2, 0:n_tiles]))
            for d in range(n_tiles):
                for o, c0, c1 in tile_of(u, d):
                    c1 = min(c1, width)
                    last = finish(dve, h, d0 + d, c0, c1, o[:, 0:c1 - c0], recip[:, u % 2, d:d + 1])
            last.then_inc(acc_out, 1)

        @block.vector
        def _(dve):
            link = chain(dve, v_chain)

            def larger(i):
                u, r, t = steps[i]
                w = min(span, NT - units[u][1]) * TP
                dve.wait_ge(exp_done, i + 1)
                dve.tensor_tensor(high[i % 3][:, 0:w], high[i % 3][:, 0:w], lowb[i % 3][:, 0:w],
                                  op=ALU.max).then_inc(max_done, 1)

            larger(0)
            if rels > 1:
                dve.wait_ge(counts_in[0], 16)
            for i, (u, r, t) in enumerate(steps):
                if rels > 1 and (r, t) == (0, 2) and u == 0:
                    dve.wait_ge(counts_in[1], 16)
                h, d0 = units[u]
                w = min(span, NT - d0) * TP
                if i + 1 < len(steps):
                    larger(i + 1)
                dve.wait_ge(max_done, i + 1)
                if i >= 3:
                    dve.wait_ge(wts_used, i - 2)
                dve.scalar_tensor_tensor(out=wts[i % 3][:, 0:w], in0=high[i % 3][:, 0:w], scalar=1.0,
                                         in1=counts_of(r, t, d0 * TP, w), op0=ALU.min,
                                         op1=ALU.mult).then_inc(wts_done, 1)
                if i % per_unit == 2 and u >= 1:
                    take_out(dve, link, u - 1)
            take_out(dve, link, len(units) - 1)

        @block.sync
        def _(sp):
            if rels > 1:
                sp.dma_start(counts[:, 0:2, :], g.counts_dram[:, 0:2, :]).then_inc(counts_in[0], 16)
            sp.wait_ge(copied, 2)
            sp.dma_start(g.rows_dram[0:2 * CH, :], shiftedT).then_inc(out_done, 16)
            sp.wait_ge(out_done, 16)

            def load_rows(u):
                h, d0 = units[u]
                w = min(span, NT - d0) * TP
                for r in range(rels):
                    src = bass.AP(tensor=g.rows_dram.tensor, offset=(r * heads + h) * N + d0 * TP,
                                  ap=[[0, TP], [CH * N, 2], [1, w]])
                    sp.dma_start(rows[u % 2][:, r, :, 0:w], src).then_inc(rows_in[u % 2], 16)

            load_rows(0)
            if rels > 1:
                sp.dma_start(counts[:, 2:NT, :], g.counts_dram[:, 2:NT, :]).then_inc(counts_in[1], 16)
            load_rows(1)
            for i, (u, r, t) in enumerate(steps):
                if not value_of:
                    if i >= 4:
                        sp.wait_ge(wts_used, i - 3)
                    h, d0 = units[u]
                    sp.dma_start(stream[i % 4][:, 0:width],
                                 g.values_dram[r, t * TP:(t + 1) * TP, h * width:(h + 1) * width])\
                        .then_inc(value_in[i % 4], 16)
                if i % per_unit == 4 and u >= 1 and u + 1 < len(units):
                    sp.wait_ge(exp_done, u * per_unit)
                    load_rows(u + 1)

        @block.gpsimd
        def _(pool):
            if not value_of:
                for i in range(4):
                    pool.memset(stream[i][:, width:width + 1], 1.0).then_inc(ones, 1)


def attend_wide(g, tag, ks, ks_low, shifted, room, finish):
    CH = ks.shape[2]
    SPAN = 4
    units = [(d, min(d + SPAN, NT)) for d in range(0, NT, SPAN)]
    W = SPAN * TP
    COLS = D + 2
    pieces = [(0, 512), (512, COLS)]
    steps = [(u, r, t) for u in range(len(units)) for t in range(NT) for r in range(CH)]
    per_unit = NT * CH
    with ExitStack() as ctx:
        s = Scope(g, ctx)
        flat = room[:, :, :].rearrange("p t d -> p (t d)")
        rows = [flat[:, i * 2 * CH * W:(i + 1) * 2 * CH * W].rearrange("p (r i w) -> p r i w", r=CH, i=2)
                for i in range(2)]
        shiftedT = flat[0:2 * CH, 2 * CH * W:2 * CH * W + N]
        high = [s.sb(f"{tag}_high{i}", [TP, W]) for i in range(2)]
        lowb = [s.sb(f"{tag}_lowb{i}", [TP, W]) for i in range(2)]
        wts = [s.sb(f"{tag}_wts{i}", [TP, W]) for i in range(2)]
        wts_parts = [[s.sb(f"{tag}_wts_part{i}{j}", [TP, SPAN, TP + 1], FR) for j in range(2)] for i in range(2)]
        values = [s.sb(f"{tag}_values{i}", [TP, COLS]) for i in range(3)]
        value_parts = [[s.sb(f"{tag}_value_part{i}{j}", [TP, COLS], FR) for j in range(2)] for i in range(2)]
        recip = s.sb(f"{tag}_recip", [TP, SPAN])
        counts = s.sb(f"{tag}_counts", [TP, NT, KEYS], U16)
        acc = s.ps(f"{tag}_acc", [TP, SPAN, 2, 512])
        turn_ps = acc[0:2 * CH, :, :, :].rearrange("p a b c -> p (a b) c")
        turned, copied, rows_out = s.sem(f"{tag}_turned"), s.sem(f"{tag}_copied"), s.sem(f"{tag}_rows_out")
        rows_in, counts_in, value_in = s.sems(f"{tag}_rows_in", 2), s.sems(f"{tag}_counts_in", 2), s.sems(f"{tag}_value_in", 3)
        exp_done, max_done, wts_done = s.sem(f"{tag}_exp"), s.sem(f"{tag}_max"), s.sem(f"{tag}_wts_done")
        value_high, wts_high = s.sem(f"{tag}_value_high"), s.sem(f"{tag}_wts_high")
        value_low, wts_low = s.sem(f"{tag}_value_low"), s.sem(f"{tag}_wts_low")
        multiplied, acc_out, v_chain, ends = s.sem(f"{tag}_multiplied"), s.sem(f"{tag}_acc_out"), s.sem(f"{tag}_vc"), s.sem(f"{tag}_ends")
        block = s.block()

        def parts_of(part, w):
            return part[:, 0:w // TP, 0:TP]

        def by_tile(tensor, w):
            return tensor[:, 0:w].rearrange("p (d t) -> p d t", t=TP)

        @block.tensor
        def _(pe):
            for t in range(NT):
                last = pe.transpose(turn_ps[:, t // 4, (t % 4) * TP:(t % 4 + 1) * TP],
                                    shifted[:, t, :, :].rearrange("p a c -> p (a c)"), g.ident[0:TP, 0:TP])
            last.then_inc(turned, 1)
            pe.wait_ge(copied, 2)
            for i, (u, r, t) in enumerate(steps):
                d0, d1 = units[u]
                first, final = i % per_unit == 0, i % per_unit == per_unit - 1
                if first and u >= 1:
                    pe.wait_ge(acc_out, u)
                pe.wait_ge(value_low, i + 1)
                pe.wait_ge(wts_low, i + 1)
                for d in range(d1 - d0):
                    for b, (c0, c1) in enumerate(pieces):
                        last = three(pe, acc[:, d, b, 0:c1 - c0], [w[:, d, 0:TP] for w in wts_parts[i % 2]],
                                     [v[:, c0:c1] for v in value_parts[i % 2]], first, final)
                last.then_inc(multiplied, 1)

        @block.scalar
        def _(act):
            act.wait_ge(turned, 1)
            act.activation(shiftedT[:, 0:8 * TP].rearrange("p (a b) -> p a b", a=2), turn_ps[:, 0:2, 0:4 * TP],
                           ACT.Copy).then_inc(copied, 1)
            act.activation(shiftedT[:, 8 * TP:N], turn_ps[:, 2, 0:2 * TP], ACT.Copy).then_inc(copied, 1)
            act.wait_ge(ends, 3)

            def weigh(i):
                u, r, t = steps[i]
                w = (units[u][1] - units[u][0]) * TP
                if i % per_unit == 0:
                    act.wait_ge(rows_in[u % 2], u // 2 * 16 * CH + 16 * CH)
                if i >= 2:
                    act.wait_ge(wts_done, i - 1)
                act.activation(high[i % 2][:, 0:w], rows[u % 2][:, r, 0, 0:w], ACT.Exp, bias=ks[:, t, r:r + 1])
                act.activation(lowb[i % 2][:, 0:w], rows[u % 2][:, r, 1, 0:w], ACT.Exp,
                               bias=ks_low[:, t, r:r + 1]).then_inc(exp_done, 1)

            weigh(0)
            for i, (u, r, t) in enumerate(steps):
                w = (units[u][1] - units[u][0]) * TP
                if i + 1 < len(steps):
                    weigh(i + 1)
                if i >= 2:
                    act.wait_ge(multiplied, i - 1)
                act.wait_ge(value_in[i % 3], i // 3 * 16 + 16)
                act.activation(value_parts[i % 2][0][:, :], values[i % 3][:, :], ACT.Copy).then_inc(value_high, 1)
                act.wait_ge(wts_done, i + 1)
                act.activation(parts_of(wts_parts[i % 2][0], w), by_tile(wts[i % 2], w), ACT.Copy).then_inc(wts_high, 1)

        @block.vector
        def _(dve):
            link = chain(dve, v_chain)

            def take_out(u):
                d0, d1 = units[u]
                dve.wait_ge(multiplied, (u + 1) * per_unit)
                c0 = pieces[1][0]
                link(dve.tensor_scalar(recip[:, 0:d1 - d0], acc[:, 0:d1 - d0, 1, D - c0], 1e-16, None, op0=ALU.add))
                link(dve.reciprocal(recip[:, 0:d1 - d0], recip[:, 0:d1 - d0]))
                for d in range(d1 - d0):
                    for b, (c0, c1) in enumerate(pieces):
                        c1 = min(c1, D)
                        last = finish(dve, 0, d0 + d, c0, c1, acc[:, d, b, 0:c1 - c0], recip[:, d:d + 1])
                last.then_inc(acc_out, 1)

            def weigh(i):
                u, r, t = steps[i]
                d0, d1 = units[u]
                w = (d1 - d0) * TP
                dve.wait_ge(exp_done, i + 1)
                dve.tensor_tensor(high[i % 2][:, 0:w], high[i % 2][:, 0:w], lowb[i % 2][:, 0:w],
                                  op=ALU.max).then_inc(max_done, 1)
                dve.wait_ge(max_done, i + 1)
                if i >= 2:
                    dve.wait_ge(wts_low, i - 1)
                    dve.wait_ge(wts_high, i - 1)
                by_relation = counts[:, t, :].rearrange("p (d r) -> p r d", r=R)[:, r, d0 * TP:d0 * TP + w]
                dve.scalar_tensor_tensor(out=wts[i % 2][:, 0:w], in0=high[i % 2][:, 0:w], scalar=1.0,
                                         in1=by_relation, op0=ALU.min, op1=ALU.mult).then_inc(wts_done, 1)

            dve.wait_ge(counts_in[0], 16)
            weigh(0)
            for i, (u, r, t) in enumerate(steps):
                if i == 2 * CH - 1:
                    dve.wait_ge(counts_in[1], 16)
                w = (units[u][1] - units[u][0]) * TP
                if i + 1 < len(steps):
                    weigh(i + 1)
                dve.wait_ge(value_high, i + 1)
                dve.tensor_tensor(value_parts[i % 2][1][:, :], values[i % 3][:, :],
                                  value_parts[i % 2][0][:, :].bitcast(F32), op=ALU.subtract).then_inc(value_low, 1)
                dve.wait_ge(wts_high, i + 1)
                dve.tensor_tensor(parts_of(wts_parts[i % 2][1], w), by_tile(wts[i % 2], w),
                                  parts_of(wts_parts[i % 2][0], w).bitcast(F32), op=ALU.subtract).then_inc(wts_low, 1)
                if i % per_unit == 1 and u >= 1:
                    take_out(u - 1)
            take_out(len(units) - 1)

        @block.sync
        def _(sp):
            sp.dma_start(counts[:, 0:2, :], g.counts_dram[:, 0:2, :]).then_inc(counts_in[0], 16)
            sp.wait_ge(copied, 2)
            sp.dma_start(g.rows_dram[0:2 * CH, :], shiftedT).then_inc(rows_out, 16)

            def load_rows(u):
                d0, d1 = units[u]
                w = (d1 - d0) * TP
                for r in range(CH):
                    src = bass.AP(tensor=g.rows_dram.tensor, offset=r * N + d0 * TP, ap=[[0, TP], [CH * N, 2], [1, w]])
                    sp.dma_start(rows[u % 2][:, r, :, 0:w], src).then_inc(rows_in[u % 2], 16)

            sp.wait_ge(rows_out, 16)
            load_rows(0)
            sp.dma_start(counts[:, 2:NT, :], g.counts_dram[:, 2:NT, :]).then_inc(counts_in[1], 16)
            load_rows(1)
            for i, (u, r, t) in enumerate(steps):
                if i >= 3:
                    sp.wait_ge(value_low, i - 2)
                    sp.wait_ge(value_high, i - 2)
                sp.dma_start(values[i % 3][:, 0:D], g.values_dram[r, t * TP:(t + 1) * TP, :]).then_inc(value_in[i % 3], 16)
                if i % per_unit == 4 and u >= 1 and u + 1 < len(units):
                    sp.wait_ge(exp_done, u * per_unit)
                    load_rows(u + 1)

        @block.gpsimd
        def _(pool):
            for v in values:
                pool.memset(v[:, D + 1:D + 2], 0.0)
                pool.memset(v[:, D:D + 1], 1.0).then_inc(ends, 1)


def gat_layer(g, src, dst, etype, w_fc, w_res, attn_l, attn_r, layers, weights):
    nc = g.nc
    H, DH = 12, 64
    with ExitStack() as ctx:
        g.counts = Scope(g, ctx).sb("counts", [TP, NT, KEYS], U16)
        count_edges(g, src, dst, etype)
        merge_edges(g)
    with ExitStack() as ctx:
        s = Scope(g, ctx)
        ks = s.sb("gat_ks", [TP, NT, H])
        qd = s.sb("gat_qd", [TP, NT, H])
        ks_low = s.sb("gat_ks_low", [TP, NT, H])
        shifted = s.sb("gat_shifted", [TP, NT, 2, H])
        res = s.sb("gat_res", [TP, NT, D])
        with ExitStack() as inner:
            si = Scope(g, inner)
            ft = si.sb("gat_ft", [TP, NT, H, DH + 1])
            with ExitStack() as inmost:
                hT = Scope(g, inmost).sb("gat_hT", [128, KC, N])
                normalize(g, "gat_ln", g.x, res, hT)
                project_gat(g, hT, w_fc, w_res, attn_l, attn_r, ft, res, ks, qd)

            def finish(dve, h, d, c0, c1, sums, recip):
                at = slice(h * DH, (h + 1) * DH)
                return dve.scalar_tensor_tensor(out=res[:, d, at], in0=sums, scalar=recip, in1=res[:, d, at],
                                                op0=ALU.mult, op1=ALU.add)

            with ExitStack() as inmost:
                sm = Scope(g, inmost)
                row = [sm.sb(f"gat_row{i}", [TP, 1, N])[:, :, :] for i in range(3)]
                greatest(g, "gat", H, 1, row, None, ks, qd, ks_low, shifted,
                         beside=lambda sc: RelationWeights(sc, g, layers, weights))
            attend(g, "gat2", H, DH, NT, ks, ks_low, shifted, lambda h, t: ft[:, t, h, :], finish)
        added = s.sem("gat_added")
        block = s.block()

        @block.vector
        def _(dve):
            for t in range(NT):
                dve.scalar_tensor_tensor(out=g.x[:, t, :], in0=res[:, t, :], scalar=0.0, in1=g.x[:, t, :],
                                         op0=ALU.max, op1=ALU.add).then_inc(added, 1)
            dve.wait_ge(added, NT)


def scratch(g):
    nc = g.nc
    g.far_dram = nc.dram_tensor("far_dram", (KEYS, N), BF16).ap()
    g.counts_dram = nc.dram_tensor("counts_dram", (TP, NT, KEYS), U16).ap()
    g.span_dram = nc.dram_tensor("span_dram", (2, 2, EH), F32).ap()
    g.range_dram = nc.dram_tensor("range_dram", (KT, 2), I32).ap()
    g.rows_dram = nc.dram_tensor("rows_dram", (24, N), F32).ap()
    g.low_dram = nc.dram_tensor("low_dram", (12, 1), F32).ap()
    g.h_dram = nc.dram_tensor("h_dram", (N, D), F32).ap()
    g.token_dram = nc.dram_tensor("token_dram", ((SLOT_TILES + 2) * TP, 1), I32).ap()
    g.tile_dram = nc.dram_tensor("tile_dram", (1, 2 * SLOT_TILES), I32).ap()
    g.sorted_dram = nc.dram_tensor("sorted_dram", ((SLOT_TILES + 2) * TP, D), F32).ap()
    g.slot_dram = nc.dram_tensor("slot_dram", (SLOT_TILES * TP, D), F32).ap()
    g.x_dram = nc.dram_tensor("x_dram", (TP, NT, D), F32).ap()
    g.score_dram = nc.dram_tensor("score_dram", (NT, TP), F32).ap()
    g.values_dram = nc.dram_tensor("values_dram", (R, N, D), F32).ap()


TOKENS = [(0, 417), (417, 834), (834, N)]


def route(g, hT, router_w, gate, gateT, rank):
    X = router_w.shape[0]
    with ExitStack() as ctx:
        s = Scope(g, ctx)
        rw = s.sb("route_w", [X, D])
        rwT = s.sb("route_wT", [128, KC, X])
        logits = s.sb("route_logits", [TP, NT, X])
        pairs = s.sb("route_pairs", [TP, NT, X, X])
        ties = s.sb("route_ties", [TP, NT, X, X])
        before = s.sb("route_before", [TP, X, X])
        top = s.sb("route_top", [TP, NT])
        turn_ps = s.ps("route_turn", [128, 512])
        logit_ps = s.ps("route_ps", [TP, 512])
        gate_ps = s.ps("route_gate", [X, 3, 512])
        w_in, w_turned, w_copied, made = s.sem("route_w_in"), s.sem("route_w_turned"), s.sem("route_w_copied"), s.sem("route_made")
        v_chain, before_done, shifted, exp_done = s.sem("route_vc"), s.sem("route_before_done"), s.sem("route_shifted"), s.sem("route_exp")
        gated, gate_turned, gate_out = s.sem("route_gated"), s.sem("route_gate_turned"), s.sem("route_gate_out")
        block = s.block()

        @block.sync
        def _(sp):
            sp.dma_start(rw[:, :], router_w).then_inc(w_in, 16)

        @block.gpsimd
        def _(pool):
            pool.memset(before[:, :, :], 1.0).then_inc(before_done, 1)
            pool.wait_ge(before_done, 1)
            pool.affine_select(out=before[:, :, :], in_=before[:, :, :], compare_op=ALU.is_gt, fill=0.0,
                               base=0, pattern=[[1, X], [-1, X]], channel_multiplier=0).then_inc(before_done, 1)

        @block.tensor
        def _(pe):
            pe.wait_ge(w_in, 16)
            for c in range(KC):
                last = pe.transpose(turn_ps[:, c * X:(c + 1) * X], rw[:, c * 128:(c + 1) * 128], g.ident[0:X, 0:X])
            last.then_inc(w_turned, 1)
            pe.wait_ge(w_copied, 1)
            for t in range(NT):
                for c in range(KC):
                    last = pe.matmul(logit_ps[:, t * X:(t + 1) * X], hT[:, c, t * TP:(t + 1) * TP], rwT[:, c, :],
                                     start=(c == 0), stop=(c == KC - 1))
            last.then_inc(made, 1)
            pe.wait_ge(gated, 1)
            for t in range(NT):
                last = pe.transpose(gate_ps[:, t // 4, (t % 4) * TP:(t % 4 + 1) * TP], gate[:, t, :],
                                    g.ident[0:TP, 0:TP])
            last.then_inc(gate_turned, 1)

        @block.vector
        def _(dve):
            link = chain(dve, v_chain)
            dve.wait_ge(w_turned, 1)
            dve.tensor_copy(rwT[:, :, :].rearrange("p c e -> p (c e)"), turn_ps[:, 0:KC * X]).then_inc(w_copied, 1)
            dve.wait_ge(made, 1)
            link(dve.tensor_copy(logits[:, :, :].rearrange("p t e -> p (t e)"), logit_ps[:, 0:NT * X]))
            one = logits[:, :, :].unsqueeze(3).to_broadcast([TP, NT, X, X])
            other = logits[:, :, :].unsqueeze(2).to_broadcast([TP, NT, X, X])
            dve.tensor_tensor(pairs[:, :, :, :], other, one, op=ALU.is_gt)
            dve.wait_ge(before_done, 2)
            link(dve.tensor_tensor(ties[:, :, :, :], other, one, op=ALU.is_equal))
            link(dve.tensor_tensor(ties[:, :, :, :], ties[:, :, :, :],
                                   before[:, :, :].unsqueeze(1).to_broadcast([TP, NT, X, X]), op=ALU.mult))
            link(dve.tensor_tensor(pairs[:, :, :, :], pairs[:, :, :, :], ties[:, :, :, :], op=ALU.add))
            link(dve.tensor_reduce(out=rank[:, :, :], in_=pairs[:, :, :, :], op=ALU.add, axis=AX_X))
            link(dve.tensor_reduce(out=top[:, :], in_=logits[:, :, :], op=ALU.max, axis=AX_X))
            dve.tensor_tensor(logits[:, :, :], logits[:, :, :], top[:, :].unsqueeze(2).to_broadcast([TP, NT, X]),
                              op=ALU.subtract).then_inc(shifted, 1)
            dve.wait_ge(exp_done, 1)
            link(dve.scalar_tensor_tensor(out=gate[:, :, :], in0=rank[:, :, :], scalar=1.5, in1=logits[:, :, :],
                                          op0=ALU.is_lt, op1=ALU.mult))
            link(dve.tensor_reduce(out=top[:, :], in_=gate[:, :, :], op=ALU.add, axis=AX_X))
            link(dve.reciprocal(top[:, :], top[:, :]))
            dve.tensor_tensor(gate[:, :, :], gate[:, :, :], top[:, :].unsqueeze(2).to_broadcast([TP, NT, X]),
                              op=ALU.mult).then_inc(gated, 1)
            dve.wait_ge(gate_turned, 1)
            dve.tensor_copy(gateT[:, 0:8 * TP].rearrange("p (a b) -> p a b", a=2),
                            gate_ps[:, 0:2, 0:4 * TP]).then_inc(gate_out, 1)
            dve.tensor_copy(gateT[:, 8 * TP:N], gate_ps[:, 2, 0:2 * TP]).then_inc(gate_out, 1)
            dve.wait_ge(gate_out, 2)

        @block.scalar
        def _(act):
            act.wait_ge(shifted, 1)
            act.activation(logits[:, :, :], logits[:, :, :], ACT.Exp).then_inc(exp_done, 1)


def three(pe, out, still, moving, first, final):
    pe.matmul(out, still[0], moving[0], start=first, stop=False)
    pe.matmul(out, still[0], moving[1], start=False, stop=False)
    return pe.matmul(out, still[1], moving[0], start=False, stop=final)


SLOT_TILES = (2 * N) // TP + 8


def assign_slots(g, h, rank, gate, x_experts, slots, gates, b2, gateT):
    X = x_experts
    with ExitStack() as ctx:
        s = Scope(g, ctx)
        chosen = s.sb("slot_chosen", [TP, NT, X])
        lower = s.sb("slot_lower", [TP, TP])
        ones = s.sb("slot_ones", [TP, TP])
        place = s.sb("slot_place", [TP, NT, X])
        total = s.sb("slot_total", [TP, NT + 1, X])
        steps = s.sb("slot_steps", [TP, X, NT])
        over = s.sb("slot_over", [TP, X, NT])
        tiles = s.sb("slot_tiles", [TP, X])
        begin = s.sb("slot_begin", [TP, X + 1])
        pick = s.sb("slot_pick", [TP, NT, X])
        slots_f = s.sb("slot_slots_f", [TP, NT, 2])
        token = s.sb("slot_token", [TP, NT], I32)
        number = s.sb("slot_number", [1, SLOT_TILES])
        after = s.sb("slot_after", [1, X - 1, SLOT_TILES])
        even = s.sb("slot_even", [1, SLOT_TILES // 2])
        table = s.sb("slot_table", [1, 2, SLOT_TILES])
        table_i = s.sb("slot_table_i", [1, 2, SLOT_TILES], I32)
        empty = s.sb("slot_empty", [TP, SLOT_TILES + 2], I32)
        b2_sb = s.sb("slot_b2", [X, D])
        zeros = s.sb("slot_zeros", [TP, D])
        ps = [s.ps(f"slot_ps{i}", [TP, 512]) for i in range(2)]
        bias_ps = [s.ps(f"slot_bias{i}", [TP, 2, 512]) for i in range(2)]
        made, counted, v_chain, placed, b2_in = (s.sem(f"slot_{x}") for x in ("made", "counted", "vc", "placed", "b2_in"))
        cleared, h_out, table_out, tabled = (s.sem(f"slot_{x}") for x in ("cleared", "h_out", "table_out", "tabled"))
        scattered = s.software_sem("slot_scattered")
        biased, added, consts, zeroed, tail_out = (s.sem(f"slot_{x}") for x in ("biased", "added", "consts", "zeroed", "tail_out"))
        block = s.block()

        @block.gpsimd
        def _(pool):
            pool.memset(zeros[:, :], 0.0).then_inc(zeroed, 1)
            pool.memset(ones[:, :], 1.0).then_inc(consts, 1)
            pool.memset(lower[:, :], 1.0).then_inc(consts, 1)
            pool.memset(empty[:, :], 0).then_inc(consts, 1)
            pool.iota(token[:, :], [[TP, NT]], base=0, channel_multiplier=1).then_inc(consts, 1)
            pool.iota(steps[:, :, :], [[0, X], [TP, NT]], base=0, channel_multiplier=0,
                      allow_small_or_imprecise_dtypes=True).then_inc(consts, 1)
            pool.iota(number[:, :], [[1, SLOT_TILES]], base=0, channel_multiplier=0,
                      allow_small_or_imprecise_dtypes=True).then_inc(consts, 1)
            pool.wait_ge(consts, 6)
            pool.affine_select(out=lower[:, :], in_=lower[:, :], compare_op=ALU.is_gt, fill=0.0,
                               base=0, pattern=[[1, TP]], channel_multiplier=-1).then_inc(consts, 1)
            pool.wait_ge(cleared, 16)
            pool.wait_ge(placed, 1)
            for t in range(NT):
                for c in range(2):
                    pool.indirect_dma_start(out=g.token_dram, out_offset=bass.IndirectOffsetOnAxis(
                        ap=slots[:, t, c:c + 1], axis=0), in_=token[:, t:t + 1], in_offset=None).then_inc(scattered, 16)
            pool.wait_ge(scattered, 16 * 2 * NT)

        @block.sync
        def _(sp):
            sp.dma_start(b2_sb[:, :], b2).then_inc(b2_in, 16)
            sp.dma_start(g.h_dram.rearrange("(t p) d -> p t d", p=TP), h[:, :, :]).then_inc(h_out, 16)
            sp.wait_ge(consts, 6)
            sp.dma_start(g.token_dram.rearrange("(k p) o -> p (k o)", p=TP), empty[:, :],
                         allow_slow_non_contiguous=True).then_inc(cleared, 16)
            sp.wait_ge(zeroed, 1)
            for k in range(2 * N // TP, SLOT_TILES):
                sp.dma_start(g.slot_dram[k * TP:(k + 1) * TP, :], zeros[:, :]).then_inc(tail_out, 16)
            sp.wait_ge(tabled, 1)
            sp.dma_start(g.tile_dram, table_i[:, :, :].rearrange("p a b -> p (a b)")).then_inc(table_out, 16)
            sp.wait_ge(table_out, 16)
            sp.wait_ge(h_out, 16)
            sp.wait_ge(tail_out, 16 * (SLOT_TILES - 2 * N // TP))

        @block.tensor
        def _(pe):
            pe.wait_ge(made, 1)
            pe.wait_ge(consts, 7)
            flat = chosen[:, :, :].rearrange("p t e -> p (t e)")
            pe.matmul(ps[0][:, 0:NT * X], lower[:, :], flat, start=True, stop=True)
            pe.matmul(ps[1][:, 0:NT * X], ones[:, :], flat, start=True, stop=True).then_inc(counted, 1)
            pe.wait_ge(b2_in, 16)
            for t in range(NT):
                if t >= 2:
                    pe.wait_ge(added, t - 1)
                for a in range(2):
                    last = pe.matmul(bias_ps[t % 2][:, a, 0:384], gateT[:, t * TP:(t + 1) * TP],
                                     b2_sb[:, a * 384:(a + 1) * 384], start=True, stop=True)
                last.then_inc(biased, 1)

        @block.vector
        def _(dve):
            link = chain(dve, v_chain)
            dve.tensor_scalar(chosen[:, :, :], rank[:, :, :], 1.5, None, op0=ALU.is_lt).then_inc(made, 1)
            link(dve.memset(total[:, 0, :], 0.0))
            dve.wait_ge(counted, 1)
            link(dve.tensor_copy(place[:, :, :].rearrange("p t e -> p (t e)"), ps[0][:, 0:NT * X]))
            for t in range(NT):
                link(dve.tensor_tensor(total[:, t + 1, :], total[:, t, :], ps[1][:, t * X:(t + 1) * X], op=ALU.add))
            dve.wait_ge(consts, 7)
            link(dve.tensor_tensor(place[:, :, :], place[:, :, :], total[:, 0:NT, :], op=ALU.add))
            link(dve.tensor_tensor(over[:, :, :], total[:, NT, :].unsqueeze(2).to_broadcast([TP, X, NT]),
                                   steps[:, :, :], op=ALU.is_gt))
            link(dve.tensor_reduce(out=tiles[:, :], in_=over[:, :, :], op=ALU.add, axis=AX_X))
            link(dve.tensor_scalar(tiles[:, :], tiles[:, :], 1.0, None, op0=ALU.max))
            link(dve.memset(begin[:, 0:1], 0.0))
            for e in range(X):
                link(dve.tensor_tensor(begin[:, e + 1:e + 2], begin[:, e:e + 1], tiles[:, e:e + 1], op=ALU.add))
            link(dve.tensor_tensor(after[:, :, :], begin[0:1, 1:X].unsqueeze(2).to_broadcast([1, X - 1, SLOT_TILES]),
                                   number[:, :].unsqueeze(1).to_broadcast([1, X - 1, SLOT_TILES]), op=ALU.is_le))
            link(dve.tensor_reduce(out=table[:, 0, :], in_=after[:, :, :].rearrange("p e k -> p k e"), op=ALU.add,
                                   axis=AX_X))
            link(dve.memset(table[:, 1, :], 0.0))
            link(dve.tensor_copy(table[:, 1, 0:X - 1], begin[0:1, 1:X]))
            link(dve.tensor_scalar(even[:, :], number[:, 0:SLOT_TILES:2], begin[0:1, X:X + 1], None, op0=ALU.is_lt))
            link(dve.tensor_reduce(out=table[:, 1, X - 1:X], in_=even[:, :], op=ALU.add, axis=AX_X))
            dve.tensor_copy(table_i[:, :, :], table[:, :, :]).then_inc(tabled, 1)
            link(dve.tensor_scalar(begin[:, :], begin[:, :], float(TP), None, op0=ALU.mult))
            link(dve.tensor_tensor(place[:, :, :], place[:, :, :],
                                   begin[:, 0:X].unsqueeze(1).to_broadcast([TP, NT, X]), op=ALU.add))
            for c in range(2):
                for src, dst in ((place, slots_f), (gate, gates)):
                    link(dve.scalar_tensor_tensor(out=pick[:, :, :], in0=rank[:, :, :], scalar=float(c),
                                                  in1=src[:, :, :], op0=ALU.is_equal, op1=ALU.mult))
                    link(dve.tensor_reduce(out=dst[:, :, c], in_=pick[:, :, :], op=ALU.add, axis=AX_X))
            dve.tensor_copy(slots[:, :, :], slots_f[:, :, :]).then_inc(placed, 1)
            for t in range(NT):
                dve.wait_ge(biased, t + 1)
                x_t = g.x[:, t, :].rearrange("p (a b) -> p a b", a=2)
                dve.tensor_tensor(x_t, x_t, bias_ps[t % 2][:, :, 0:384], op=ALU.add).then_inc(added, 1)
            dve.wait_ge(placed, 1)
            dve.wait_ge(added, NT)


def sort_rows(g):
    with ExitStack() as ctx:
        s = Scope(g, ctx)
        tokens = s.sb("sort_tokens", [TP, SLOT_TILES + 2], I32)
        rows = [s.sb(f"sort_rows{i}", [TP, D]) for i in range(4)]
        tokens_in, rows_out = s.sem("sort_tokens_in"), s.sems("sort_rows_out", 4)
        rows_in = [s.software_sem(f"sort_rows_in{i}") for i in range(4)]
        block = s.block()

        @block.gpsimd
        def _(pool):
            pool.wait_ge(tokens_in, 16)
            for k in range(SLOT_TILES + 2):
                if k >= 4:
                    pool.wait_ge(rows_out[k % 4], k // 4 * 16)
                pool.indirect_dma_start(out=rows[k % 4][:, :], out_offset=None, in_=g.h_dram,
                                        in_offset=bass.IndirectOffsetOnAxis(ap=tokens[:, k:k + 1], axis=0)
                                        ).then_inc(rows_in[k % 4], 16)

        @block.sync
        def _(sp):
            sp.dma_start(tokens[:, :], g.token_dram.rearrange("(k p) o -> p (k o)", p=TP),
                         allow_slow_non_contiguous=True).then_inc(tokens_in, 16)
            for k in range(SLOT_TILES + 2):
                sp.wait_ge(rows_in[k % 4], k // 4 * 16 + 16)
                sp.dma_start(g.sorted_dram[k * TP:(k + 1) * TP, :], rows[k % 4][:, :]).then_inc(rows_out[k % 4], 16)
            for i in range(4):
                sp.wait_ge(rows_out[i], len(range(i, SLOT_TILES + 2, 4)) * 16)


def experts(g, w1, b1, w2):
    X, F = b1.shape
    FC = F // 128
    with ExitStack() as ctx:
        s = Scope(g, ctx)
        raw_up = s.sb("moe_raw_up", [128, KC * F])
        raw_down = s.sb("moe_raw_down", [128, FC * D])
        up_w = [s.sb(f"moe_up_w{j}", [128, 2 * KC * F], FR) for j in range(2)]
        down_w = [s.sb(f"moe_down_w{j}", [128, 2 * FC * D], FR) for j in range(2)]
        b1_rows = s.sb("moe_b1", [TP, X * F])
        zeros = s.sb("moe_zeros", [128, KC * F])
        rows = [s.sb(f"moe_rows{u}", [TP, D]) for u in range(2)]
        rowsT = [[s.sb(f"moe_rowsT{u}{j}", [128, KC, 126], FR) for j in range(2)] for u in range(2)]
        mid = [s.sb(f"moe_mid{u}", [TP, F]) for u in range(2)]
        midT = [[s.sb(f"moe_midT{u}{j}", [128, FC, 126], FR) for j in range(2)] for u in range(2)]
        out_sb = [s.sb(f"moe_out{u}", [TP, D]) for u in range(2)]
        table = s.sb("moe_table", [1, 2 * SLOT_TILES], I32)
        wide_ps = [s.ps(f"moe_wide{u}", [128, 2, 512]) for u in range(2)]
        mid_ps = [s.ps(f"moe_mid_ps{u}", [128, 512]) for u in range(2)]
        table_in, raw_in, raw_down_in = s.sem("moe_table_in"), s.sem("moe_raw_in"), s.sem("moe_raw_down_in")
        high_done, up_ready, down_ready = s.sem("moe_high_done"), s.sem("moe_up_ready"), s.sem("moe_down_ready")
        rows_in, turned, high_out, low_out = s.sems("moe_rows_in", 2), s.sem("moe_turned"), s.sem("moe_high_out"), s.sem("moe_low_out")
        up_done, bias_done, gelu_done = s.sem("moe_up_done"), s.sem("moe_bias_done"), s.sem("moe_gelu_done")
        mid_turned, mid_high, mid_low = s.sem("moe_mid_turned"), s.sem("moe_mid_high"), s.sem("moe_mid_low")
        down_done, taken, sent = s.sem("moe_down_done"), s.sem("moe_taken"), s.sems("moe_sent", 2)
        expert_free, all_sent, zeroed = s.sem("moe_expert_free"), s.sem("moe_all_sent"), s.sem("moe_zeroed")
        block = s.block()

        def pairs_of(eng):
            return eng.value_load(table[0:1, SLOT_TILES + X - 1:SLOT_TILES + X], min_val=1, max_val=SLOT_TILES // 2)

        def expert_of(eng, tile):
            return eng.value_load(table[0:1, bass.ds(tile, 1)], min_val=0, max_val=X - 1)

        @block.sync
        def _(sp):
            sp.dma_start(table[:, :], g.tile_dram).then_inc(table_in, 16)
            for e in range(X):
                if e >= 1:
                    sp.wait_ge(up_ready, e)
                sp.dma_start(raw_up[:, :].rearrange("p (c f) -> p c f", c=KC),
                             w1[e, :, :].rearrange("(c p) f -> p c f", p=128)).then_inc(raw_in, 16)
                if e >= 1:
                    sp.wait_ge(down_ready, e)
                sp.dma_start(raw_down[:, :].rearrange("p (c f) -> p c f", c=FC),
                             w2[e, :, :].rearrange("(c p) f -> p c f", p=128)).then_inc(raw_down_in, 16)

        @block.gpsimd
        def _(pool):
            pool.wait_ge(table_in, 16)
            for e in range(X):
                if e == 0:
                    pool.memset(zeros[:, :], 0.0).then_inc(zeroed, 1)
                    pool.wait_ge(zeroed, 1)
                if e >= 2:
                    begin = pool.value_load(table[0:1, SLOT_TILES + e - 2:SLOT_TILES + e - 1],
                                            min_val=1, max_val=SLOT_TILES)
                    pool.wait_ge(down_done, begin)
                    pool.nop().then_inc(expert_free, 1)
                for n, (raw, w, loaded, ready) in enumerate(((raw_up, up_w, raw_in, up_ready),
                                                            (raw_down, down_w, raw_down_in, down_ready))):
                    size = KC * F
                    at = slice(e % 2 * size, (e % 2 + 1) * size)
                    pool.wait_ge(loaded, e * 16 + 16)
                    pool.tensor_tensor(w[0][:, at], raw[:, :], zeros[:, :], op=ALU.add).then_inc(high_done, 1)
                    pool.wait_ge(high_done, 2 * e + n + 1)
                    pool.tensor_tensor(w[1][:, at], raw[:, :], w[0][:, at].bitcast(F32),
                                       op=ALU.subtract).then_inc(ready, 1)

        @block.tensor
        def _(pe):
            pe.wait_ge(table_in, 16)
            with pe.Fori(0, pairs_of(pe)) as i:
                for u in range(2):
                    pe.wait_ge(rows_in[u], i * 16 + 16)
                    pe.wait_ge(taken, i * 2 + (u + 1))
                    for c in range(KC):
                        last = pe.transpose(wide_ps[u][:, c // 3, (c % 3) * TP:(c % 3 + 1) * TP],
                                            rows[u][:, c * 128:(c + 1) * 128], g.ident[0:TP, 0:TP])
                    last.then_inc(turned, 1)
                for u in range(2):
                    e = expert_of(pe, i * 2 + u)
                    parity = pe.snap(e % 2)
                    pe.wait_ge(up_ready, e + 1)
                    pe.wait_ge(low_out, i * 2 + (u + 1))
                    pe.wait_ge(mid_low, i * 2 + (u + 1))
                    for c in range(KC):
                        last = three(pe, mid_ps[u][0:TP, 0:F], [rowsT[u][j][:, c, 0:TP] for j in range(2)],
                                     [up_w[j][:, bass.ds(parity * (KC * F) + c * F, F)] for j in range(2)],
                                     c == 0, c == KC - 1)
                    last.then_inc(up_done, 1)
                for u in range(2):
                    e = expert_of(pe, i * 2 + u)
                    parity = pe.snap(e % 2)
                    pe.wait_ge(gelu_done, i * 2 + (u + 1))
                    for c in range(FC):
                        last = pe.transpose(mid_ps[u][:, c * TP:(c + 1) * TP], mid[u][:, c * 128:(c + 1) * 128],
                                            g.ident[0:TP, 0:TP])
                    last.then_inc(mid_turned, 1)
                    pe.wait_ge(down_ready, e + 1)
                    pe.wait_ge(mid_low, i * 2 + (u + 3))
                    for a in range(2):
                        for c in range(FC):
                            last = three(pe, wide_ps[u][0:TP, a, 0:384], [midT[u][j][:, c, 0:TP] for j in range(2)],
                                         [down_w[j][:, bass.ds(parity * (FC * D) + (c * D + a * 384), 384)]
                                          for j in range(2)], c == 0, c == FC - 1)
                    last.then_inc(down_done, 1)

        @block.vector
        def _(dve):
            dve.wait_ge(table_in, 16)
            for u in range(2):
                dve.nop().then_inc(mid_low, 1)
            dve.wait_ge(sent[0], 16)
            dve.wait_ge(sent[1], 16)
            with dve.Fori(0, pairs_of(dve)) as i:
                for u in range(2):
                    dve.wait_ge(high_out, i * 2 + (u + 1))
                    dve.tensor_tensor(rowsT[u][1][:, :, 0:TP].rearrange("p (a b) t -> p a b t", a=2),
                                      wide_ps[u][:, :, 0:3 * TP].rearrange("p a (b t) -> p a b t", t=TP),
                                      rowsT[u][0][:, :, 0:TP].bitcast(F32).rearrange("p (a b) t -> p a b t", a=2),
                                      op=ALU.subtract).then_inc(low_out, 1)
                for u in range(2):
                    e = expert_of(dve, i * 2 + u)
                    dve.wait_ge(up_done, i * 2 + (u + 1))
                    dve.tensor_tensor(mid[u][:, :], mid_ps[u][0:TP, 0:F], b1_rows[:, bass.ds(e * F, F)],
                                      op=ALU.add).then_inc(bias_done, 1)
                for u in range(2):
                    dve.wait_ge(mid_high, i * 2 + (u + 1))
                    dve.tensor_tensor(midT[u][1][:, :, 0:TP], mid_ps[u][:, 0:FC * TP].rearrange("p (c t) -> p c t", t=TP),
                                      midT[u][0][:, :, 0:TP].bitcast(F32), op=ALU.subtract).then_inc(mid_low, 1)

        @block.scalar
        def _(act):
            for u in range(2):
                act.dma_start(rows[u][:, :], g.sorted_dram[u * TP:(u + 1) * TP, :]).then_inc(rows_in[u], 16)
                act.nop().then_inc(taken, 1)
                half = slice(u * (X * F // 2), (u + 1) * (X * F // 2))
                act.dma_start(b1_rows[:, half], rows_of(b1, TP, u * (X * F // 2), X * F // 2)).then_inc(sent[u], 16)
            act.wait_ge(table_in, 16)
            pairs = pairs_of(act)
            with act.Fori(0, pairs) as i:
                for u in range(2):
                    act.wait_ge(turned, i * 2 + (u + 1))
                    act.activation(rowsT[u][0][:, :, 0:TP].rearrange("p (a b) t -> p a b t", a=2),
                                   wide_ps[u][:, :, 0:3 * TP].rearrange("p a (b t) -> p a b t", t=TP),
                                   ACT.Copy).then_inc(high_out, 1)
                    act.dma_start(rows[u][:, :], g.sorted_dram[bass.ds((i * 2 + (u + 2)) * TP, TP), :]
                                  ).then_inc(rows_in[u], 16)
                for u in range(2):
                    act.wait_ge(bias_done, i * 2 + (u + 1))
                    act.activation(mid[u][:, :], mid[u][:, :], ACT.Gelu).then_inc(gelu_done, 1)
                for u in range(2):
                    act.wait_ge(mid_turned, i * 2 + (u + 1))
                    act.activation(midT[u][0][:, :, 0:TP], mid_ps[u][:, 0:FC * TP].rearrange("p (c t) -> p c t", t=TP),
                                   ACT.Copy).then_inc(mid_high, 1)
                for u in range(2):
                    act.wait_ge(down_done, i * 2 + (u + 1))
                    act.wait_ge(sent[u], i * 16 + 16)
                    act.activation(out_sb[u][:, :].rearrange("p (a b) -> p a b", a=2), wide_ps[u][0:TP, :, 0:384],
                                   ACT.Copy).then_inc(taken, 1)
                    act.wait_ge(taken, i * 2 + (u + 3))
                    act.dma_start(g.slot_dram[bass.ds((i * 2 + u) * TP, TP), :], out_sb[u][:, :]).then_inc(sent[u], 16)
            for u in range(2):
                act.wait_ge(sent[u], pairs * 16 + 16)
                act.wait_ge(rows_in[u], pairs * 16 + 16)
            act.nop().then_inc(all_sent, 1)


def combine(g, slots, gates):
    with ExitStack() as ctx:
        s = Scope(g, ctx)
        rows = [s.sb(f"comb_rows{i}", [TP, D]) for i in range(6)]
        rows_in, added = [s.software_sem(f"comb_rows_in{i}") for i in range(6)], s.sem("comb_added")
        block = s.block()
        steps = [(c, t) for c in range(2) for t in range(NT)]

        @block.gpsimd
        def _(pool):
            for i, (c, t) in enumerate(steps):
                if i >= 6:
                    pool.wait_ge(added, i - 5)
                pool.indirect_dma_start(out=rows[i % 6][:, :], out_offset=None, in_=g.slot_dram,
                                        in_offset=bass.IndirectOffsetOnAxis(ap=slots[:, t, c:c + 1], axis=0)
                                        ).then_inc(rows_in[i % 6], 16)

        @block.vector
        def _(dve):
            for i, (c, t) in enumerate(steps):
                dve.wait_ge(rows_in[i % 6], i // 6 * 16 + 16)
                if c:
                    dve.wait_ge(added, i - NT + 1)
                dve.scalar_tensor_tensor(out=g.x[:, t, :], in0=rows[i % 6][:, :], scalar=gates[:, t, c:c + 1],
                                         in1=g.x[:, t, :], op0=ALU.mult, op1=ALU.add).then_inc(added, 1)
            dve.wait_ge(added, len(steps))


def moe_layer(g, router_w, w1, b1, w2, b2):
    X = router_w.shape[0]
    with ExitStack() as ctx:
        s = Scope(g, ctx)
        slots = s.sb("moe_slots", [TP, NT, 2], I32)
        gates = s.sb("moe_gates", [TP, NT, 2])
        with ExitStack() as inner:
            si = Scope(g, inner)
            gate = si.sb("moe_gate", [TP, NT, X])
            rank = si.sb("moe_rank", [TP, NT, X])
            gateT = si.sb("moe_gateT", [X, N])
            hT = si.sb("moe_hT", [128, KC, N])
            h = si.sb("moe_h", [TP, NT, D])
            normalize(g, "moe_ln", g.x, h, hT)
            route(g, hT, router_w, gate, gateT, rank)
            assign_slots(g, h, rank, gate, X, slots, gates, b2, gateT)
        sort_rows(g)
        experts(g, w1, b1, w2)
        combine(g, slots, gates)


def far_tile(g, r, t):
    return bass.AP(tensor=g.far_dram.tensor, offset=r * N + t * TP * R * N, ap=[[R * N, TP], [1, N]])


def elu_and_turn(g, h, hT):
    with ExitStack() as ctx:
        s = Scope(g, ctx)
        low = [s.sb(f"elu_low{i}", [TP, D]) for i in range(2)]
        banks = [[s.ps(f"elu_turn{i}{j}", [128, 512]) for j in range(2)] for i in range(2)]
        clipped, exp_done, rows_done, v_chain = s.sem("elu_clipped"), s.sem("elu_exp"), s.sem("elu_rows"), s.sem("elu_vc")
        turned, copied = s.sem("elu_turned"), s.sem("elu_copied")
        block = s.block()

        @block.vector
        def _(dve):
            link = chain(dve, v_chain)
            for t in range(NT + 1):
                if t < NT:
                    if t >= 2:
                        dve.wait_ge(rows_done, t - 1)
                    dve.tensor_scalar(low[t % 2][:, :], h[:, t, :], 0.0, None, op0=ALU.min).then_inc(clipped, 1)
                if t >= 1:
                    u = t - 1
                    dve.wait_ge(exp_done, u + 1)
                    link(dve.tensor_scalar(low[u % 2][:, :], low[u % 2][:, :], -1.0, None, op0=ALU.add))
                    dve.scalar_tensor_tensor(out=h[:, u, :], in0=h[:, u, :], scalar=0.0, in1=low[u % 2][:, :],
                                             op0=ALU.max, op1=ALU.add).then_inc(rows_done, 1)
            dve.wait_ge(rows_done, NT)

        def take_turned(act, t):
            act.wait_ge(turned, t + 1)
            for j in range(2):
                act.activation(hT[:, 3 * j:3 * j + 3, t * TP:(t + 1) * TP],
                               banks[t % 2][j][:, 0:3 * TP].rearrange("p (c t) -> p c t", t=TP),
                               ACT.Copy).then_inc(copied, 1)

        @block.scalar
        def _(act):
            for t in range(NT):
                act.wait_ge(clipped, t + 1)
                act.activation(low[t % 2][:, :], low[t % 2][:, :], ACT.Exp).then_inc(exp_done, 1)
                if t >= 1:
                    take_turned(act, t - 1)
            take_turned(act, NT - 1)
            act.wait_ge(copied, 2 * NT)

        @block.tensor
        def _(pe):
            for t in range(NT):
                pe.wait_ge(rows_done, t + 1)
                if t >= 2:
                    pe.wait_ge(copied, 2 * (t - 1))
                turn_tile(pe, g, banks[t % 2], h, t, turned)


def rgat_layers(g, w1, b1, w2, b2, weights):
    with ExitStack() as ctx:
        s = Scope(g, ctx)
        h = s.sb("rgat_h", [TP, NT, D])
        for layer, (tag, w) in enumerate((("rg1", w1), ("rg2", w2))):
            H = weights[layer].shape[4]
            with ExitStack() as inner:
                si = Scope(g, inner)
                ks = si.sb(f"{tag}_ks", [TP, NT, R * H])
                qd = si.sb(f"{tag}_qd", [TP, NT, R * H])
                ks_low = si.sb(f"{tag}_ks_low", [TP, NT, R * H])
                shifted = si.sb(f"{tag}_shifted", [TP, NT, 2, R * H])
                bias = si.sb(f"{tag}_bias", [TP, D])
                with ExitStack() as inmost:
                    sm = Scope(g, inmost)
                    hT = sm.sb(f"{tag}_hT", [128, KC, N])
                    if layer == 0:
                        normalize(g, "rg_ln", g.x, h, hT)
                    else:
                        elu_and_turn(g, h, hT)
                    row = [h[:, :, :].rearrange("p t d -> p (t d)")[:, 0:H * N].rearrange("p (h n) -> p h n", h=H),
                           sm.sb(f"{tag}_row", [TP, H, N])[:, :, :]]
                    greatest(g, tag, H, H, row, lambda r, t: far_tile(g, r, t), ks, qd, ks_low, shifted,
                             (hT, weights[layer]),
                             lambda sc: RelationValues(sc, g, tag, hT, w, b1 if layer == 0 else b2, bias, layer == 1))
                def finish(dve, hd, d, c0, c1, sums, recip):
                    width = D // H
                    at = slice(hd * width + c0, hd * width + c1)
                    out, plus = (h[:, d, at], bias[:, at]) if layer == 0 else (g.x[:, d, at], g.x[:, d, at])
                    return dve.scalar_tensor_tensor(out=out, in0=sums, scalar=recip, in1=plus,
                                                    op0=ALU.mult, op1=ALU.add)

                if H > 1:
                    attend(g, tag + "a", H, D // H, 5, ks, ks_low, shifted, None, finish)
                else:
                    attend_wide(g, tag + "a", ks, ks_low, shifted, h, finish)


PICKED = max(1, int(round(0.15 * N)))
QT = PICKED // 2
HEADS = 12
DH = D // HEADS


def pick_tokens(g, n, wr, br, keep, picks, picksT, picked_nT, score_rows, room):
    with ExitStack() as ctx:
        s = Scope(g, ctx)
        wr_rows = s.sb("pick_wr", [TP, D])
        junk = s.sb("pick_junk", [TP, 2, D])
        score = s.sb("pick_score", [TP, NT])
        br_col = s.sb("pick_br", [TP, 1])
        scoreT = s.sb("pick_scoreT", [NT, TP])
        srow, node, tie, less = (room[0:TP, i, :] for i in range(4))
        own = s.sb("pick_own", [TP, NT])
        rank = s.sb("pick_rank", [TP, NT])
        ones = s.sb("pick_ones", [TP, TP])
        total = s.sb("pick_total", [TP, 1])
        ps = s.ps("pick_ps", [128, 512])
        turn_ps = [s.ps(f"pick_turn{i}", [QT, 512]) for i in range(2)]
        picked_ps = s.ps("pick_picked", [128, 3, 512])
        small_in, ready, scored, turned, score_out, srow_in = (s.sem(f"pick_{x}") for x in "abcdef")
        summed, weighed, ranked, v_chain, dots, copied = (s.sem(f"pick_{x}") for x in "ghijkl")
        picksT_turned, picksT_out, gathered, score_saved = (s.sem(f"pick_{x}") for x in "mnop")
        rows_ready = s.sem("pick_q")
        block = s.block()
        j1 = PICKED + 1

        @block.sync
        def _(sp):
            sp.dma_start(wr_rows[:, :], rows_of(wr, TP, 0, D)).then_inc(small_in, 16)
            sp.dma_start(br_col[:, :], rows_of(br, TP, 0, 1)).then_inc(small_in, 16)
            sp.wait_ge(copied, 1)
            sp.dma_start(g.score_dram, scoreT[:, :]).then_inc(score_out, 16)
            sp.wait_ge(score_out, 16)
            sp.dma_start(srow, rows_of(g.score_dram, TP, 0, N)).then_inc(srow_in, 16)
            sp.wait_ge(rows_ready, 1)
            sp.dma_start(score_rows[0:1, :], rows_of(g.score_dram, 1, 0, N)).then_inc(score_saved, 16)
            sp.wait_ge(score_saved, 16)

        @block.gpsimd
        def _(pool):
            pool.iota(node, [[1, N]], base=0, channel_multiplier=0,
                      allow_small_or_imprecise_dtypes=True).then_inc(ready, 1)
            pool.iota(own[:, :], [[TP, NT]], base=0, channel_multiplier=1,
                      allow_small_or_imprecise_dtypes=True).then_inc(ready, 1)
            pool.memset(ones[:, :], 1.0).then_inc(ready, 1)
            pool.memset(score_rows[:, :], 1.0).then_inc(rows_ready, 1)

        @block.scalar
        def _(act):
            act.wait_ge(dots, NT)
            act.wait_ge(small_in, 32)
            act.activation(score[:, :], score[:, :], ACT.Sigmoid, bias=br_col[:, 0:1]).then_inc(scored, 1)
            for i in range(5):
                act.wait_ge(picksT_turned, i + 1)
                act.activation(picksT[:, :, i * 2 * TP:(i + 1) * 2 * TP],
                               turn_ps[i % 2][:, 0:4 * TP].rearrange("p (q k) -> p q k", q=2),
                               ACT.Copy).then_inc(picksT_out, 1)
            act.wait_ge(gathered, 1)
            act.activation(picked_nT[:, :, :].rearrange("p (a b) j -> p a (b j)", b=2),
                           picked_ps[:, :, 0:2 * j1], ACT.Copy).then_inc(gathered, 1)
            act.wait_ge(gathered, 2)

        @block.tensor
        def _(pe):
            pe.wait_ge(scored, 1)
            pe.wait_ge(ready, 3)
            pe.transpose(ps[0:NT, 0:TP], score[:, :], g.ident[0:TP, 0:TP])
            pe.matmul(ps[0:TP, 128:128 + NT], ones[:, :], score[:, :], start=True, stop=True).then_inc(turned, 1)
            for i in range(5):
                if i == 0:
                    pe.wait_ge(ranked, NT)
                if i >= 2:
                    pe.wait_ge(picksT_out, i - 1)
                for q in range(2):
                    for k in range(2):
                        last = pe.transpose(turn_ps[i % 2][:, (2 * q + k) * TP:(2 * q + k + 1) * TP],
                                            picks[:, 2 * i + k, q * QT:(q + 1) * QT], g.ident[0:TP, 0:TP])
                last.then_inc(picksT_turned, 1)
            pe.wait_ge(weighed, 1)
            for c in range(KC):
                for t in range(NT):
                    last = pe.matmul(picked_ps[:, c // 2, (c % 2) * j1:(c % 2 + 1) * j1],
                                     n[:, t, c * 128:(c + 1) * 128], picks[:, t, :],
                                     start=(t == 0), stop=(t == NT - 1))
            last.then_inc(gathered, 1)

        @block.vector
        def _(dve):
            link = chain(dve, v_chain)
            dve.wait_ge(small_in, 32)
            for t in range(NT):
                if t >= 2:
                    dve.wait_ge(dots, t - 1)
                dve.tensor_tensor_reduce(out=junk[:, t % 2, :], in0=n[:, t, :], in1=wr_rows[:, :], scale=1.0,
                                         scalar=0.0, op0=ALU.mult, op1=ALU.add,
                                         accum_out=score[:, t:t + 1]).then_inc(dots, 1)
            dve.wait_ge(turned, 1)
            dve.tensor_copy(scoreT[:, :], ps[0:NT, 0:TP]).then_inc(copied, 1)
            link(dve.tensor_reduce(out=total[:, :], in_=ps[0:TP, 128:128 + NT], op=ALU.add, axis=AX_X))
            link(dve.tensor_scalar(total[:, :], total[:, :], 1e-6, None, op0=ALU.add))
            link(dve.reciprocal(total[:, :], total[:, :]))
            dve.tensor_scalar(picks[:, :, PICKED:j1], score[:, :].unsqueeze(2), total[:, 0:1], None,
                              op0=ALU.mult).then_inc(weighed, 1)
            dve.wait_ge(srow_in, 16)
            for t in range(NT):
                link(dve.tensor_scalar(less, node, own[:, t:t + 1], None, op0=ALU.is_lt))
                link(dve.scalar_tensor_tensor(out=tie, in0=srow, scalar=score[:, t:t + 1],
                                              in1=less, op0=ALU.is_equal, op1=ALU.mult))
                link(dve.scalar_tensor_tensor(out=less, in0=srow, scalar=score[:, t:t + 1],
                                              in1=tie, op0=ALU.is_lt, op1=ALU.add))
                link(dve.tensor_reduce(out=rank[:, t:t + 1], in_=less, op=ALU.add, axis=AX_X))
                dve.tensor_scalar(picks[:, t, 0:PICKED], node[:, 0:PICKED], rank[:, t:t + 1], None,
                                  op0=ALU.is_equal).then_inc(ranked, 1)
            link(dve.tensor_scalar(keep[:, :], rank[:, :], PICKED - 0.5, None, op0=ALU.is_gt))


def columns_of(v, width):
    return v.rearrange("(c p) -> p c", p=128)


def mix_and_project(g, z, nT, picked_nT, score_rows, keep, wm, bm, wk, bk, wv, wq, bq, kT, v, qT):
    with ExitStack() as ctx:
        s = Scope(g, ctx)
        w_sb = [s.sb("mix_w", [128, KC, D]), g.x_all[:, 0:KC, :]]
        mixed = s.sb("mix_rows", [2, D])
        b_cols = s.sb("mix_b", [128, 2, KC])
        row_ps = s.ps("mix_row", [1, 2, 512])
        ps = [s.ps(f"mix_ps{i}", [128, 2, 512]) for i in range(3)]
        w_in, w_used, small_in, row_made, row_out = s.sems("mix_w_in", 2), s.sem("mix_w_used"), s.sem("mix_small"), s.sem("mix_row_made"), s.sem("mix_row_out")
        made, taken = s.sem("mix_made"), s.sem("mix_taken")
        block = s.block()
        jobs = [("mix", t) for t in range(NT)] + [("key", (f, k)) for f in range(KC) for k in range(len(TOKENS))] \
            + [("value", t) for t in range(NT)] + [("query", f) for f in range(KC)]
        weights = {"mix": 0, "key": 1, "value": 2, "query": 3}
        last_of = {kind: max(i for i, j in enumerate(jobs) if j[0] == kind) + 1 for kind in weights}

        @block.sync
        def _(sp):
            sp.dma_start(mixed[1:2, :], rows_of(bm, 1, 0, D)).then_inc(small_in, 16)
            for i, b in enumerate((bk, bq)):
                sp.dma_start(b_cols[:, i, :], columns_of(b, D), allow_slow_non_contiguous=True).then_inc(small_in, 16)
            for i, w in enumerate((wm, wk, wv, wq)):
                if i >= 2:
                    sp.wait_ge(made, last_of["mix" if i == 2 else "key"])
                sp.dma_start(w_sb[i % 2][:, :, :], w.rearrange("(c p) f -> p c f", p=128)).then_inc(w_in[i % 2], 16)

        @block.tensor
        def _(pe):
            pe.wait_ge(w_in[0], 16)
            for a in range(2):
                for c in range(KC):
                    last = pe.matmul(row_ps[:, a, 0:384], picked_nT[:, c, PICKED:PICKED + 1],
                                     w_sb[0][:, c, a * 384:(a + 1) * 384], start=(c == 0), stop=(c == KC - 1))
            last.then_inc(row_made, 1)
            pe.wait_ge(row_out, 1)
            pe.wait_ge(small_in, 48)
            for i, (kind, at) in enumerate(jobs):
                w = w_sb[weights[kind] % 2]
                out = ps[i % 3]
                pe.wait_ge(w_in[weights[kind] % 2], weights[kind] // 2 * 16 + 16)
                if i >= 3:
                    pe.wait_ge(taken, i - 2)
                if kind in ("mix", "value"):
                    rows = slice(at * TP, (at + 1) * TP)
                    for a in range(2):
                        cols = slice(a * 384, (a + 1) * 384)
                        if kind == "mix":
                            pe.matmul(out[0:TP, a, 0:384], score_rows[:, rows], mixed[:, cols],
                                      start=True, stop=False)
                        for c in range(KC):
                            last = pe.matmul(out[0:TP, a, 0:384], nT[:, c, rows], w[:, c, cols],
                                             start=(c == 0 and kind == "value"), stop=(c == KC - 1))
                else:
                    f = at[0] if kind == "key" else at
                    for c in range(KC):
                        if kind == "key":
                            a, b = TOKENS[at[1]]
                            moving = nT[:, c, a:b]
                        else:
                            a, b = 0, PICKED
                            moving = picked_nT[:, c, 0:PICKED]
                        last = pe.matmul(out[:, 0, 0:b - a], w[:, c, f * 128:(f + 1) * 128], moving,
                                         start=(c == 0), stop=(c == KC - 1))
                last.then_inc(made, 1)

        @block.vector
        def _(dve):
            dve.wait_ge(row_made, 1)
            dve.tensor_copy(mixed[0:1, :].rearrange("p (a b) -> p a b", a=2), row_ps[:, :, 0:384]).then_inc(row_out, 1)
            dve.wait_ge(small_in, 48)
            for i, (kind, at) in enumerate(jobs):
                dve.wait_ge(made, i + 1)
                out = ps[i % 3]
                if kind == "mix":
                    z_t = z[:, at, :].rearrange("p (a b) -> p a b", a=2)
                    last = dve.scalar_tensor_tensor(out=z_t, in0=out[0:TP, :, 0:384], scalar=keep[:, at:at + 1],
                                                    in1=z_t, op0=ALU.mult, op1=ALU.add)
                elif kind == "value":
                    last = dve.tensor_copy(v[:, at, :].rearrange("p (a b) -> p a b", a=2), out[0:TP, :, 0:384])
                elif kind == "key":
                    f, k = at
                    a, b = TOKENS[k]
                    last = dve.tensor_scalar(kT[:, f, a:b], out[:, 0, 0:b - a], b_cols[:, 0, f:f + 1], None, op0=ALU.add)
                else:
                    last = dve.tensor_scalar(qT[:, at, :], out[:, 0, 0:PICKED], b_cols[:, 1, at:at + 1], None,
                                             op0=ALU.add)
                last.then_inc(taken, 1)
            dve.wait_ge(taken, len(jobs))


def attend_picked(g, z, kT, v, qT, picksT, bv, wo, bo):
    SCALE = DH ** -0.5
    units = [(q, h) for q in range(2) for h in range(HEADS)]
    with ExitStack() as ctx:
        s = Scope(g, ctx)
        probs = [s.sb(f"att_probs{i}", [QT, N]) for i in range(2)]
        probsT = [s.sb(f"att_probsT{i}", [TP, NT, QT]) for i in range(2)]
        top = s.sb("att_top", [QT, len(units)])
        total = s.sb("att_total", [QT, len(units)])
        ctxT = s.sb("att_ctxT", [128, KC, PICKED])
        bv_cols = s.sb("att_bv", [128, KC])
        wo_sb = s.sb("att_wo", [128, KC, D])
        bo_row = s.sb("att_bo", [1, D])
        ones = s.sb("att_ones", [1, QT])
        out_sb = s.sb("att_out", [QT, 2, D])
        score_ps = [s.ps(f"att_score{i}", [128, 3, 512]) for i in range(2)]
        turn_ps = [s.ps(f"att_turn{i}", [TP, 512]) for i in range(2)]
        flat = [x[0:QT, :, :].rearrange("p a b -> p (a b)") for x in score_ps]
        small_in, wo_in, one_set = s.sem("att_small"), s.sem("att_wo_in"), s.sem("att_one")
        scored, topped, exp_done, scaled, turned, turned_out = (s.sem(f"att_{x}") for x in "abcdef")
        ctx_made, ctx_out, v_chain, out_made, out_taken, spread, added = (s.sem(f"att_{x}") for x in "ghijklm")
        block = s.block()

        @block.sync
        def _(sp):
            sp.dma_start(bv_cols[:, :], columns_of(bv, D), allow_slow_non_contiguous=True).then_inc(small_in, 16)
            sp.dma_start(bo_row[:, :], rows_of(bo, 1, 0, D)).then_inc(small_in, 16)
            sp.dma_start(wo_sb[:, :, :], wo.rearrange("(c p) f -> p c f", p=128)).then_inc(wo_in, 16)

        @block.gpsimd
        def _(pool):
            pool.memset(ones[:, :], 1.0).then_inc(one_set, 1)

        @block.tensor
        def _(pe):
            def scores(i):
                q, h = units[i]
                at = slice(h % 2 * DH, h % 2 * DH + DH)
                if i >= 2:
                    pe.wait_ge(ctx_out, i - 1)
                for k in range(0, N, 512):
                    w = min(512, N - k)
                    last = pe.matmul(flat[i % 2][:, k:k + w], qT[at, h // 2, q * QT:(q + 1) * QT],
                                     kT[at, h // 2, k:k + w], start=True, stop=True)
                last.then_inc(scored, 1)

            def context(i):
                q, h = units[i]
                pe.wait_ge(scaled, i + 1)
                for half in range(2):
                    if i >= 1:
                        pe.wait_ge(turned_out, 2 * (i - 1) + half + 1)
                    for k in range(5):
                        t = half * 5 + k
                        last = pe.transpose(turn_ps[half][:, k * QT:(k + 1) * QT], probs[i % 2][:, t * TP:(t + 1) * TP],
                                            g.ident[0:QT, 0:QT])
                    last.then_inc(turned, 1)
                pe.wait_ge(turned_out, 2 * i + 2)
                at = slice(h % 2 * DH, h % 2 * DH + DH)
                for t in range(NT):
                    last = pe.matmul(score_ps[i % 2][at, 0, 0:QT], v[:, t, h * DH:(h + 1) * DH],
                                     probsT[i % 2][:, t, :], start=(t == 0), stop=(t == NT - 1))
                last.then_inc(ctx_made, 1)

            scores(0)
            for i in range(len(units)):
                if i + 1 < len(units):
                    scores(i + 1)
                context(i)
            pe.wait_ge(ctx_out, len(units))
            pe.wait_ge(wo_in, 16)
            pe.wait_ge(small_in, 32)
            pe.wait_ge(one_set, 1)
            for q in range(2):
                for a in range(2):
                    cols = slice(a * 384, (a + 1) * 384)
                    pe.matmul(score_ps[q][0:QT, a, 0:384], ones[:, :], bo_row[:, cols], start=True, stop=False)
                    for c in range(KC):
                        last = pe.matmul(score_ps[q][0:QT, a, 0:384], ctxT[:, c, q * QT:(q + 1) * QT],
                                         wo_sb[:, c, cols], start=False, stop=(c == KC - 1))
                last.then_inc(out_made, 1)
            pe.wait_ge(out_taken, 2)
            for t in range(NT):
                if t >= 2:
                    pe.wait_ge(added, t - 1)
                for a in range(2):
                    for q in range(2):
                        last = pe.matmul(score_ps[t % 2][0:TP, a, 0:384], picksT[:, q, t * TP:(t + 1) * TP],
                                         out_sb[:, q, a * 384:(a + 1) * 384], start=(q == 0), stop=(q == 1))
                last.then_inc(spread, 1)

        @block.vector
        def _(dve):
            link = chain(dve, v_chain)
            dve.wait_ge(small_in, 32)

            def first_half(i):
                dve.wait_ge(scored, i + 1)
                link(dve.tensor_reduce(out=top[:, i:i + 1], in_=flat[i % 2][:, 0:N], op=ALU.max, axis=AX_X))
                dve.tensor_scalar(top[:, i:i + 1], top[:, i:i + 1], -SCALE, None, op0=ALU.mult).then_inc(topped, 1)

            def second_half(i):
                dve.wait_ge(exp_done, i + 1)
                link(dve.reciprocal(total[:, i:i + 1], total[:, i:i + 1]))
                dve.tensor_scalar(probs[i % 2][:, :], probs[i % 2][:, :], total[:, i:i + 1], None,
                                  op0=ALU.mult).then_inc(scaled, 1)

            def take_context(i):
                q, h = units[i]
                at = slice(h % 2 * DH, h % 2 * DH + DH)
                dve.wait_ge(ctx_made, i + 1)
                dve.tensor_scalar(ctxT[at, h // 2, q * QT:(q + 1) * QT], score_ps[i % 2][at, 0, 0:QT],
                                  bv_cols[at, h // 2:h // 2 + 1], None, op0=ALU.add).then_inc(ctx_out, 1)

            for i in range(len(units)):
                first_half(i)
                if i >= 1:
                    take_context(i - 1)
                second_half(i)
            take_context(len(units) - 1)
            for q in range(2):
                dve.wait_ge(out_made, q + 1)
                dve.tensor_copy(out_sb[:, q, :].rearrange("p (a b) -> p a b", a=2),
                                score_ps[q][0:QT, 0:2, 0:384]).then_inc(out_taken, 1)
            for t in range(NT):
                dve.wait_ge(spread, t + 1)
                z_t = z[:, t, :].rearrange("p (a b) -> p a b", a=2)
                dve.tensor_tensor(z_t, z_t, score_ps[t % 2][0:TP, 0:2, 0:384], op=ALU.add).then_inc(added, 1)
            dve.wait_ge(added, NT)

        @block.scalar
        def _(act):
            for i in range(len(units)):
                act.wait_ge(topped, i + 1)
                if i >= 2:
                    act.wait_ge(turned, 2 * (i - 1))
                act.activation(probs[i % 2][:, :], flat[i % 2][:, 0:N], ACT.Exp, bias=top[:, i:i + 1], scale=SCALE,
                               accum_out=total[:, i:i + 1]).then_inc(exp_done, 1)
                for half in range(2):
                    act.wait_ge(turned, 2 * i + half + 1)
                    if i >= 2:
                        act.wait_ge(ctx_made, i - 1)
                    act.activation(probsT[i % 2][:, half * 5:half * 5 + 5, :].rearrange("p t q -> p (t q)"),
                                   turn_ps[half][:, 0:5 * QT], ACT.Copy).then_inc(turned_out, 1)


def feed_forward(g, z, nT, w1, b1, w2, b2):
    F = w1.shape[1]
    FC = F // 128
    with ExitStack() as ctx:
        s = Scope(g, ctx)
        up_w = s.sb("ff_up_w", [128, KC, F])
        down_w = s.sb("ff_down_w", [128, FC, D])
        inner = s.sb("ff_inner", [128, FC, N])
        b1_cols = s.sb("ff_b1", [128, FC])
        b2_row = s.sb("ff_b2", [1, D])
        ones = s.sb("ff_ones", [1, TP])
        up_ps = [s.ps(f"ff_up{i}", [128, 512]) for i in range(4)]
        down_ps = [s.ps(f"ff_down{i}", [TP, 2, 512]) for i in range(2)]
        w_in, one_set, up_done, gelu_done, down_done, added, plus = (s.sem(f"ff_{x}") for x in "abcdefg")
        x_in = s.sem("ff_x_in")
        block = s.block()
        ups = [(f, k) for f in range(FC) for k in range(len(TOKENS))]

        @block.sync
        def _(sp):
            sp.dma_start(g.x, g.x_dram).then_inc(x_in, 16)
            sp.dma_start(up_w[:, :, :], w1.rearrange("(c p) f -> p c f", p=128)).then_inc(w_in, 16)
            sp.dma_start(down_w[:, :, :], w2.rearrange("(c p) f -> p c f", p=128)).then_inc(w_in, 16)
            sp.dma_start(b1_cols[:, :], columns_of(b1, F), allow_slow_non_contiguous=True).then_inc(w_in, 16)
            sp.dma_start(b2_row[:, :], rows_of(b2, 1, 0, D)).then_inc(w_in, 16)

        @block.gpsimd
        def _(pool):
            pool.memset(ones[:, :], 1.0).then_inc(one_set, 1)
            pool.wait_ge(x_in, 16)
            for t in range(NT):
                pool.tensor_tensor(g.x[:, t, :], g.x[:, t, :], z[:, t, :], op=ALU.add).then_inc(plus, 1)

        @block.tensor
        def _(pe):
            pe.wait_ge(w_in, 64)
            pe.wait_ge(one_set, 1)
            for n, (f, k) in enumerate(ups):
                a, b = TOKENS[k]
                if n >= 4:
                    pe.wait_ge(gelu_done, n - 3)
                for c in range(KC):
                    last = pe.matmul(up_ps[n % 4][:, 0:b - a], up_w[:, c, f * 128:(f + 1) * 128], nT[:, c, a:b],
                                     start=(c == 0), stop=(c == KC - 1))
                last.then_inc(up_done, 1)
            pe.wait_ge(gelu_done, len(ups))
            for t in range(NT):
                if t >= 2:
                    pe.wait_ge(added, t - 1)
                for a in range(2):
                    cols = slice(a * 384, (a + 1) * 384)
                    pe.matmul(down_ps[t % 2][:, a, 0:384], ones[:, :], b2_row[:, cols], start=True, stop=False)
                    for f in range(FC):
                        last = pe.matmul(down_ps[t % 2][:, a, 0:384], inner[:, f, t * TP:(t + 1) * TP],
                                         down_w[:, f, cols], start=False, stop=(f == FC - 1))
                last.then_inc(down_done, 1)

        @block.scalar
        def _(act):
            act.wait_ge(w_in, 64)
            for n, (f, k) in enumerate(ups):
                a, b = TOKENS[k]
                act.wait_ge(up_done, n + 1)
                act.activation(inner[:, f, a:b], up_ps[n % 4][:, 0:b - a], ACT.Gelu,
                               bias=b1_cols[:, f:f + 1]).then_inc(gelu_done, 1)

        @block.vector
        def _(dve):
            for t in range(NT):
                dve.wait_ge(down_done, t + 1)
                dve.wait_ge(plus, t + 1)
                x_t = g.x[:, t, :].rearrange("p (a b) -> p a b", a=2)
                dve.tensor_tensor(x_t, x_t, down_ps[t % 2][:, :, 0:384], op=ALU.add).then_inc(added, 1)
            dve.wait_ge(added, NT)


def save_x(g):
    with ExitStack() as ctx:
        s = Scope(g, ctx)
        saved = s.sem("x_saved")
        block = s.block()

        @block.sync
        def _(sp):
            sp.dma_start(g.x_dram, g.x).then_inc(saved, 16)
            sp.wait_ge(saved, 16)


def mixed_layer(g, g1, b1, g2, b2, wr, br, wq, bq, wk, bk, wv, bv, wo, bo, wm, bm, w1, bf1, w2, bf2):
    with ExitStack() as ctx:
        s = Scope(g, ctx)
        z = s.sb("mixed_z", [TP, NT, D])
        normalize(g, "z_ln", g.x, z, None)
        save_x(g)
        with ExitStack() as attention:
            sa = Scope(g, attention)
            keep = sa.sb("keep", [TP, NT])
            picksT = sa.sb("picksT", [QT, 2, N])
            qT = sa.sb("qT", [128, KC, PICKED])
            kT = sa.sb("kT", [128, KC, N])
            v = sa.sb("v", [TP, NT, D])
            with ExitStack() as inner:
                si = Scope(g, inner)
                nT = si.sb("nT", [128, KC, N])
                picked_nT = si.sb("picked_nT", [128, KC, PICKED + 1])
                score_rows = si.sb("score_rows", [2, N])
                normalize(g, "n_ln", z, v, nT, g1, b1)
                with ExitStack() as inmost:
                    picks = Scope(g, inmost).sb("picks", [TP, NT, PICKED + 1])
                    pick_tokens(g, v, wr, br, keep, picks, picksT, picked_nT, score_rows, kT)
                mix_and_project(g, z, nT, picked_nT, score_rows, keep, wm, bm, wk, bk, wv, wq, bq, kT, v, qT)
            attend_picked(g, z, kT, v, qT, picksT, bv, wo, bo)
        with ExitStack() as inner:
            si = Scope(g, inner)
            nT = si.sb("n2T", [128, KC, N])
            with ExitStack() as inmost:
                n2 = Scope(g, inmost).sb("n2", [TP, NT, D])
                normalize(g, "n2_ln", z, n2, nT, g2, b2)
            feed_forward(g, z, nT, w1, bf1, w2, bf2)


def load_x(g, x):
    with ExitStack() as ctx:
        s = Scope(g, ctx)
        x_in = s.sem("x_in")
        block = s.block()

        @block.sync
        def _(sp):
            sp.dma_start(g.x, x.rearrange("(t p) d -> p t d", p=TP)).then_inc(x_in, 16)
            sp.wait_ge(x_in, 16)


def store_x(g, out):
    with ExitStack() as ctx:
        s = Scope(g, ctx)
        x_out = s.sem("x_out")
        block = s.block()

        @block.sync
        def _(sp):
            sp.dma_start(out.rearrange("(t p) d -> p t d", p=TP), g.x).then_inc(x_out, 16)
            sp.wait_ge(x_out, 16)


def build(nc, io, out):
    g = Shared()
    g.nc = nc
    scratch(g)
    free = sorted(nc.free_semaphores)
    total = SEMAPHORES + SOFTWARE_SEMAPHORES
    first = min(i for i in free if all(k in free for k in range(i, i + total)))
    g.semaphore_ids, g.semaphores_used, g.semaphores_live = range(first, first + SEMAPHORES), 0, 0
    g.software_ids = list(range(first + SEMAPHORES, first + total))
    with ExitStack() as ctx:
        s = Scope(g, ctx)
        g.ident = s.sb("ident", [128, 128])
        g.x_all = s.sb("x_all", [128, NT, D])
        g.x = g.x_all[0:TP, :, :]
        constants(g)
        load_x(g, io["x"])
        relations = [[io[f"L1_gnn_{k}{n}"] for k in "Wqk"] for n in (1, 2)]
        score_weights = [s.sb(f"score_weights{n}", [128, KC, 2, R, q.shape[1]])
                         for n, (w, q, k) in enumerate(relations)]
        with ExitStack() as first:
            sf = Scope(g, first)
            g.counts_u = sf.sb("counts_u", [TP, NT, N], U16)
            g.far_u = sf.sb("far_u", [TP, NT, N], BF16)
            gat_layer(g, io["src"], io["dst"], io["edge_type_3"],
                      *[io["L0_gnn_" + k] for k in ("W_fc", "W_res", "attn_l", "attn_r")], relations, score_weights)
        moe_layer(g, *[io["L0_ffn_" + k] for k in ("router_w", "w1", "b1", "w2", "b2")])
        rgat_layers(g, *[io["L1_gnn_" + k] for k in ("W1", "b1", "W2", "b2")], score_weights)
        mixed_layer(g, *[io["L1_ffn_" + k] for k in (
            "g1", "b1", "g2", "b2", "Wr", "br", "Wq", "bq", "Wk", "bk", "Wv", "bv", "Wo", "bo", "Wm", "bm",
            "W1", "bf1", "W2", "bf2")])
        store_x(g, out)


def kernel(**inputs):
    import concourse.bacc as bacc
    from concourse.bass_utils import run_bass_kernel_spmd

    nc = bacc.Bacc("TRN2", target_bir_lowering=False, num_devices=1)
    arrays, io = {}, {}
    for name, a in inputs.items():
        a = np.ascontiguousarray(a)
        a = a.reshape(a.shape or (1,))
        arrays[f"in_{name}"] = a
        io[name] = nc.dram_tensor(f"in_{name}", a.shape, mybir.dt.from_np(a.dtype), kind="ExternalInput").ap()
    out = nc.dram_tensor("out", (N, D), F32, kind="ExternalOutput").ap()
    build(nc, io, out)
    return run_bass_kernel_spmd(nc, [arrays], core_ids=[0]).results[0]["out"]
```

```python
from contextlib import ExitStack

import numpy as np

import concourse.bass as bass
from concourse import mybir

F32 = mybir.dt.float32
BF16 = mybir.dt.bfloat16
U16 = mybir.dt.uint16
I32 = mybir.dt.int32
FR = mybir.dt.float32r
ALU = mybir.AluOpType
ACT = mybir.ActivationFunctionType
AX_X = mybir.AxisListType.X

N = 1250
D = 768
E = 20000
R = 3
TP = 125
NT = N // TP
ET = E // TP
EH = ET // 2
KEYS = R * N
KT = KEYS // TP
KC = D // 128
SEMAPHORES = 138
SOFTWARE_SEMAPHORES = 11
FAR = -1.0e30


class Shared:
    pass


class Scope:

    ROOM = 40

    def __init__(self, g, ctx):
        self.g, self.nc, self.ctx = g, g.nc, ctx
        if not g.semaphores_live and g.semaphores_used > len(g.semaphore_ids) - self.ROOM:
            g.nc.all_engine_barrier(sems_to_clear=g.semaphore_ids)
            g.semaphores_used = 0

    def sb(self, name, shape, dt=F32):
        return self.ctx.enter_context(self.nc.sbuf_tensor(name, shape, dt))

    def ps(self, name, shape):
        return self.ctx.enter_context(self.nc.psum_tensor(name, shape, F32))

    def sem(self, name):
        handle = self.nc.alloc_semaphore(name, self.g.semaphore_ids[self.g.semaphores_used])
        self.g.semaphores_used += 1
        self.g.semaphores_live += 1
        self.ctx.callback(self.give_back, handle)
        return handle

    def software_sem(self, name):
        return self.nc.alloc_semaphore(name, self.g.software_ids.pop())

    def give_back(self, handle):
        self.g.semaphores_live -= 1
        self.nc.release_semaphore(handle)

    def sems(self, name, n):
        return [self.sem(f"{name}{i}") for i in range(n)]

    def block(self):
        return self.ctx.enter_context(self.nc.Block())


def rows_of(ap, partitions, offset, width):
    return bass.AP(tensor=ap.tensor, offset=offset, ap=[[0, partitions], [1, width]])


def chain(engine, sem):
    count = [0]

    def link(instruction):
        count[0] += 1
        instruction.then_inc(sem, 1)
        engine.wait_ge(sem, count[0])

    return link


def constants(g):
    with ExitStack() as ctx:
        s = Scope(g, ctx)
        ident_zero, ident_done = s.sem("ident_zero"), s.sem("ident_done")
        block = s.block()

        @block.gpsimd
        def _(pool):
            pool.memset(g.ident[:, :], 0.0).then_inc(ident_zero, 1)
            pool.wait_ge(ident_zero, 1)
            pool.affine_select(out=g.ident[:, :], in_=g.ident[:, :], compare_op=ALU.not_equal, fill=1.0,
                               base=0, pattern=[[-1, 128]], channel_multiplier=1).then_inc(ident_done, 1)
            pool.wait_ge(ident_done, 1)


def count_edges(g, src, dst, etype):
    with ExitStack() as ctx:
        s = Scope(g, ctx)
        sb, sem = s.sb, s.sem

        edges_i = sb("edges_i", [EH, 3, 2, TP], I32)
        edges_f = sb("edges_f", [EH, 3, 2, TP], F32)
        key_f = sb("key_f", [EH, 2, TP], F32)
        span = sb("span", [EH, 2, 2], F32)
        srcT = sb("srcT", [TP, ET + 1], F32)
        keyT = sb("keyT", [TP, ET + 1], F32)
        spans = sb("spans", [KT, 2, ET], F32)
        tile_no = sb("tile_no", [KT, ET], F32)
        first_key = sb("first_key", [KT, 1], F32)
        end_key = sb("end_key", [KT, 1], F32)
        hits = sb("hits", [KT, 2, ET], F32)
        range_f = sb("range_f", [KT, 2], F32)
        range_i = sb("range_i", [KT, 2], I32)
        ranges = sb("ranges", [1, 2 * KT + 2], I32)
        number = sb("number", [TP, KEYS], U16)
        src_hot = [sb(f"src_hot{u}", [TP, N], BF16) for u in range(2)]
        key_hot = [sb(f"key_hot{u}", [TP, TP], BF16) for u in range(2)]
        zeros = sb("zeros", [TP, 512], BF16)
        cnt = [sb(f"cnt{b}", [TP, N], F32) for b in range(2)]
        far = [sb(f"far{b}", [TP, N], BF16) for b in range(2)]
        sums = [s.ps(f"sums{b}", [TP, 3, 512]) for b in range(2)]
        turned = [s.ps(f"turned{b}", [TP, 512]) for b in range(2)]
        sums_flat = [x[:, :, :].rearrange("p a b -> p (a b)") for x in sums]

        loaded = sem("edges_loaded")
        spans_out = sem("spans_out")
        spans_in = sem("spans_in")
        ranges_out = sem("ranges_out")
        ranges_in = sem("ranges_in")
        numbers = sem("numbers")
        v_chain = sem("v_chain")
        keys_done = sem("keys_done")
        edges_turned = sem("edges_turned")
        columns_done = sem("columns_done")
        span_done = sem("span_done")
        range_done = sem("range_done")
        hot_ready = [sem(f"hot_ready{u}") for u in range(2)]
        hot_used = [sem(f"hot_used{u}") for u in range(2)]
        sums_done = sem("sums_done")
        sums_copied = sem("sums_copied")
        far_done = sem("far_done")
        far_out = [sem(f"far_out{b}") for b in range(2)]
        far_free = [sem(f"far_free{b}") for b in range(2)]
        turned_done = [sem(f"turned_done{b}") for b in range(2)]
        turned_copied = [sem(f"turned_copied{b}") for b in range(2)]

        groups = [(0, 4), (4, 8), (8, NT)]
        block = s.block()

        def run_over_keys(engine, count, finish, ahead=True):
            def step(i, b, before):
                for part, at in ((count, (i, b)), (finish, before))[::1 if ahead else -1]:
                    part(*at)

            count(0, 0)
            step(0, 1, (0, 0))
            with engine.Fori(1, KT // 2) as i2:
                step(i2, 0, (i2 - 1, 1))
                step(i2, 1, (i2, 0))
            finish(KT // 2 - 1, 1)

        def bounds_of(engine):
            lo, hi = engine.alloc_register("first_edges"), engine.alloc_register("end_edges")

            def load(k):
                engine.reg_mov(lo, engine.value_load(ranges[0:1, bass.ds(k * 2, 1)], min_val=0, max_val=ET - 1))
                engine.reg_mov(hi, engine.value_load(ranges[0:1, bass.ds(k * 2 + 1, 1)], min_val=1, max_val=ET))

            load(0)
            return lo, hi, load

        @block.sync
        def _(sp):
            for i, v in enumerate((src, dst, etype)):
                sp.dma_start(edges_i[:, i, :, :], v.rearrange("(c t p) -> t c p", c=2, p=TP)).then_inc(loaded, 16)
            sp.wait_ge(span_done, 2)
            for i in range(2):
                sp.dma_start(g.span_dram[i, :, :].rearrange("c t -> t c"), span[:, i, :],
                             allow_slow_non_contiguous=True).then_inc(spans_out, 16)
            sp.wait_ge(spans_out, 32)
            sp.dma_start(spans[:, :, :].rearrange("k i t -> k (i t)"),
                         rows_of(g.span_dram, KT, 0, 2 * ET)).then_inc(spans_in, 16)
            sp.wait_ge(range_done, 1)
            sp.dma_start(g.range_dram, range_i[:, :]).then_inc(ranges_out, 16)
            sp.wait_ge(ranges_out, 16)
            sp.dma_start(ranges[:, 0:2 * KT], rows_of(g.range_dram, 1, 0, 2 * KT)).then_inc(ranges_in, 16)
            for b in range(2):
                sp.nop().then_inc(far_free[b], 1)
            with sp.Fori(0, KT // 2) as i2:
                for b in range(2):
                    sp.wait_ge(far_done, i2 * 2 + (b + 3))
                    sp.dma_start(g.far_dram[bass.ds((i2 * 2 + b) * TP, TP), :], far[b][:, :]).then_inc(far_out[b], 16)
                for b in range(2):
                    sp.wait_ge(far_out[b], i2 * 16 + 16)
                    sp.nop().then_inc(far_free[b], 1)

        @block.gpsimd
        def _(pool):
            pool.iota(number[:, :], [[1, KEYS]], base=0, channel_multiplier=0).then_inc(numbers, 1)
            pool.iota(tile_no[:, :], [[1, ET]], base=-ET, channel_multiplier=0,
                      allow_small_or_imprecise_dtypes=True).then_inc(numbers, 1)
            pool.iota(first_key[:, :], [[0, 1]], base=0, channel_multiplier=TP,
                      allow_small_or_imprecise_dtypes=True).then_inc(numbers, 1)
            pool.iota(end_key[:, :], [[0, 1]], base=TP, channel_multiplier=TP,
                      allow_small_or_imprecise_dtypes=True).then_inc(numbers, 1)
            pool.memset(srcT[:, ET:ET + 1], -1.0).then_inc(numbers, 1)
            pool.memset(keyT[:, ET:ET + 1], -1.0).then_inc(numbers, 1)
            pool.memset(zeros[:, :], 0.0).then_inc(numbers, 1)
            pool.memset(ranges[:, 2 * KT:2 * KT + 2], 1).then_inc(numbers, 1)

        @block.vector
        def _(dve):
            link = chain(dve, v_chain)
            dve.wait_ge(loaded, 48)
            link(dve.tensor_copy(edges_f[:, :, :, :], edges_i[:, :, :, :]))
            link(dve.scalar_tensor_tensor(out=key_f[:, :, :], in0=edges_f[:, 1, :, :], scalar=float(R),
                                          in1=edges_f[:, 2, :, :], op0=ALU.mult, op1=ALU.add))
            dve.tensor_reduce(out=span[:, 0, :], in_=key_f[:, :, :], op=ALU.min, axis=AX_X).then_inc(span_done, 1)
            dve.tensor_reduce(out=span[:, 1, :], in_=key_f[:, :, :], op=ALU.max, axis=AX_X).then_inc(span_done, 1)
            dve.nop().then_inc(keys_done, 1)
            dve.wait_ge(edges_turned, 1)
            dve.tensor_copy(srcT[:, 0:ET], turned[0][:, 0:ET]).then_inc(columns_done, 1)
            dve.tensor_copy(keyT[:, 0:ET], turned[1][:, 0:ET]).then_inc(columns_done, 1)
            dve.wait_ge(spans_in, 16)
            dve.wait_ge(numbers, 8)
            link(dve.scalar_tensor_tensor(out=hits[:, 0, :], in0=spans[:, 1, :], scalar=first_key[:, 0:1],
                                          in1=tile_no[:, :], op0=ALU.is_ge, op1=ALU.mult))
            link(dve.tensor_scalar(tile_no[:, :], tile_no[:, :], float(ET + 1), None, op0=ALU.add))
            link(dve.scalar_tensor_tensor(out=hits[:, 1, :], in0=spans[:, 0, :], scalar=end_key[:, 0:1],
                                          in1=tile_no[:, :], op0=ALU.is_lt, op1=ALU.mult))
            link(dve.tensor_reduce(out=range_f[:, 0:1], in_=hits[:, 0, :], op=ALU.min, axis=AX_X))
            link(dve.tensor_reduce(out=range_f[:, 1:2], in_=hits[:, 1, :], op=ALU.max, axis=AX_X))
            link(dve.tensor_scalar(range_f[:, 0:1], range_f[:, 0:1], float(ET), float(ET - 1),
                                   op0=ALU.add, op1=ALU.min))
            link(dve.scalar_tensor_tensor(out=range_f[:, 1:2], in0=range_f[:, 0:1], scalar=1.0,
                                          in1=range_f[:, 1:2], op0=ALU.add, op1=ALU.max))
            dve.tensor_copy(range_i[:, :], range_f[:, :]).then_inc(range_done, 1)
            dve.wait_ge(columns_done, 2)
            dve.wait_ge(ranges_in, 16)
            for b in range(2):
                dve.nop().then_inc(far_done, 1)
            turn = dve.alloc_register("hot_turn")
            dve.reg_mov(turn, 1)


            def count(i, b):
                lo = dve.value_load(ranges[0:1, bass.ds((i * 2 + b) * 2, 1)], min_val=0, max_val=ET - 1)
                hi = dve.value_load(ranges[0:1, bass.ds((i * 2 + b) * 2 + 1, 1)], min_val=1, max_val=ET)
                with dve.Fori(lo, hi, 2) as t:
                    for u in range(2):
                        dve.wait_ge(hot_used[u], turn)
                        dve.tensor_scalar(src_hot[u][:, :], number[:, 0:N], srcT[:, bass.ds(t + u, 1)], None,
                                          op0=ALU.is_equal)
                        dve.tensor_scalar(key_hot[u][:, :], number[:, bass.ds((i * 2 + b) * TP, TP)],
                                          keyT[:, bass.ds(t + u, 1)], None,
                                          op0=ALU.is_equal).then_inc(hot_ready[u], 1)
                    dve.reg_add(turn, turn, 1)

            def mask(i, b):
                dve.wait_ge(sums_copied, i * 2 + (b + 1))
                dve.wait_ge(far_free[b], i + 1)
                dve.tensor_scalar(far[b][:, :], cnt[b][:, :], 0.5, FAR, op0=ALU.is_lt,
                                  op1=ALU.mult).then_inc(far_done, 1)

            run_over_keys(dve, count, mask)

        @block.tensor
        def _(pe):
            pe.wait_ge(keys_done, 1)
            for c in range(2):
                pe.transpose(turned[0][:, c * EH:(c + 1) * EH], edges_f[:, 0, c, :], g.ident[0:EH, 0:EH])
                last = pe.transpose(turned[1][:, c * EH:(c + 1) * EH], key_f[:, c, :], g.ident[0:EH, 0:EH])
            last.then_inc(edges_turned, 1)
            pe.wait_ge(columns_done, 2)
            pe.wait_ge(numbers, 8)
            pe.wait_ge(ranges_in, 16)
            for b in range(2):
                pe.nop().then_inc(hot_used[b], 1)
                pe.nop().then_inc(turned_copied[b], 1)
            turn = pe.alloc_register("sum_turn")
            pe.reg_mov(turn, 1)

            lo, hi, load_bounds = bounds_of(pe)

            def count(i, b):
                for k in range(3):
                    w = min(512, N - 512 * k)
                    pe.matmul(sums_flat[b][:, 512 * k:512 * k + w], zeros[:, 0:TP], zeros[:, 0:w],
                              start=True, stop=False, skip_group_check=True)
                with pe.Fori(lo, hi, 2) as t:
                    for u in range(2):
                        pe.wait_ge(hot_ready[u], turn)
                        for k in range(3):
                            w = min(512, N - 512 * k)
                            last = pe.matmul(sums_flat[b][:, 512 * k:512 * k + w], key_hot[u][:, :],
                                             src_hot[u][:, 512 * k:512 * k + w],
                                             start=False, stop=False, skip_group_check=True)
                        last.then_inc(hot_used[u], 1)
                    pe.reg_add(turn, turn, 1)
                pe.matmul(sums_flat[b][:, 0:1], zeros[:, 0:TP], zeros[:, 0:1], start=False, stop=True,
                          skip_group_check=True).then_inc(sums_done, 1)
                load_bounds(i * 2 + (b + 1))

            def turn_counts(i, b):
                pe.wait_ge(sums_copied, i * 2 + (b + 1))
                for k, (s0, s1) in enumerate(groups):
                    n = 3 * b + k
                    pe.wait_ge(turned_copied[n % 2], i * 3 + (n // 2 + 1))
                    for s in range(s0, s1):
                        last = pe.transpose(turned[n % 2][:, (s - s0) * TP:(s - s0 + 1) * TP],
                                            cnt[b][:, s * TP:(s + 1) * TP], g.ident[0:TP, 0:TP])
                    last.then_inc(turned_done[n % 2], 1)

            run_over_keys(pe, count, turn_counts)

        @block.scalar
        def _(act):
            def copy_counts(i, b):
                act.wait_ge(sums_done, i * 2 + (b + 1))
                act.wait_ge(far_done, i * 2 + (b + 1))
                act.activation(cnt[b][:, :], sums_flat[b][:, 0:N], ACT.Copy).then_inc(sums_copied, 1)

            def keep_turned(i, b):
                for k, (s0, s1) in enumerate(groups):
                    n = 3 * b + k
                    act.wait_ge(turned_done[n % 2], i * 3 + (n // 2 + 1))
                    act.activation(g.counts[:, s0:s1, bass.ds((i * 2 + b) * TP, TP)],
                                   turned[n % 2][:, 0:(s1 - s0) * TP].rearrange("p (s k) -> p s k", k=TP),
                                   ACT.Copy).then_inc(turned_copied[n % 2], 1)

            run_over_keys(act, copy_counts, keep_turned, ahead=False)
            act.nop()


def turn_tile(pe, g, out, rows, t, tiled):
    for c in range(KC):
        last = pe.transpose(out[c // 3][:, (c % 3) * TP:(c % 3 + 1) * TP], rows[:, t, c * 128:(c + 1) * 128],
                            g.ident[0:TP, 0:TP])
    last.then_inc(tiled, 1)


def normalize(g, tag, src, dst, dstT, gamma=None, beta=None, eps=1e-5, keep_in=None):
    with ExitStack() as ctx:
        s = Scope(g, ctx)
        parts = s.sb(f"{tag}_parts", [TP, NT, 2, 6])
        mean_var = s.sb(f"{tag}_mean_var", [TP, NT, 2])
        var = s.sb(f"{tag}_var", [TP, NT])
        inv = s.sb(f"{tag}_inv", [TP, NT])
        std_inv = s.sb(f"{tag}_std_inv", [TP, NT])
        square = s.sb(f"{tag}_square", [TP, NT])
        affine = s.sb(f"{tag}_affine", [TP, 2, D]) if gamma is not None else None
        banks = [[s.ps(f"{tag}_turn{i}{j}", [128, 512]) for j in range(2)] for i in range(2)] if dstT is not None else []
        v_chain, inv_done, root_done = s.sem(f"{tag}_chain"), s.sem(f"{tag}_inv_done"), s.sem(f"{tag}_root_done")
        rows_done, turned, copied = s.sem(f"{tag}_rows"), s.sem(f"{tag}_turned"), s.sem(f"{tag}_copied")
        affine_in, kept = s.sem(f"{tag}_affine_in"), s.sem(f"{tag}_kept")
        block = s.block()

        @block.sync
        def _(sp):
            if gamma is not None:
                for i, v in enumerate((gamma, beta)):
                    sp.dma_start(affine[:, i, :], rows_of(v, TP, 0, D)).then_inc(affine_in, 16)
            if keep_in is not None:
                sp.dma_start(keep_in, src).then_inc(kept, 16)
                sp.wait_ge(kept, 16)

        @block.vector
        def _(dve):
            link = chain(dve, v_chain)
            for t in range(NT):
                for i in range(2):
                    last = dve.bn_stats(parts[:, t, i, :], src[:, t, i * 384:(i + 1) * 384])
            link(last)
            for t in range(NT):
                last = dve.bn_aggr(mean_var[:, t, :], parts[:, t, :, :].rearrange("p a b -> p (a b)"))
            link(last)
            link(dve.tensor_scalar(var[:, :], mean_var[:, :, 1], eps, None, op0=ALU.add))
            dve.reciprocal(inv[:, :], var[:, :]).then_inc(inv_done, 1)
            dve.wait_ge(root_done, 1)
            link(dve.tensor_tensor(square[:, :], std_inv[:, :], std_inv[:, :], op=ALU.mult))
            link(dve.tensor_tensor(square[:, :], square[:, :], var[:, :], op=ALU.mult))
            link(dve.tensor_scalar(square[:, :], square[:, :], -0.5, 1.5, op0=ALU.mult, op1=ALU.add))
            link(dve.tensor_tensor(std_inv[:, :], std_inv[:, :], square[:, :], op=ALU.mult))
            if gamma is None:
                for t in range(NT):
                    dve.tensor_scalar(dst[:, t, :], src[:, t, :], mean_var[:, t, 0:1], std_inv[:, t:t + 1],
                                      op0=ALU.subtract, op1=ALU.mult).then_inc(rows_done, 1)
            else:
                dve.wait_ge(affine_in, 32)
                for t in range(NT):
                    link(dve.tensor_scalar(dst[:, t, :], src[:, t, :], mean_var[:, t, 0:1], std_inv[:, t:t + 1],
                                           op0=ALU.subtract, op1=ALU.mult))
                    link(dve.tensor_tensor(dst[:, t, :], dst[:, t, :], affine[:, 0, :], op=ALU.mult))
                    dve.tensor_tensor(dst[:, t, :], dst[:, t, :], affine[:, 1, :], op=ALU.add).then_inc(rows_done, 1)
            dve.wait_ge(rows_done, NT)

        @block.scalar
        def _(act):
            act.wait_ge(inv_done, 1)
            act.activation(std_inv[:, :], inv[:, :], ACT.Sqrt).then_inc(root_done, 1)
            if dstT is not None:
                for t in range(NT):
                    act.wait_ge(turned, t + 1)
                    for j in range(2):
                        act.activation(dstT[:, 3 * j:3 * j + 3, t * TP:(t + 1) * TP],
                                       banks[t % 2][j][:, 0:3 * TP].rearrange("p (c t) -> p c t", t=TP),
                                       ACT.Copy).then_inc(copied, 1)
                act.wait_ge(copied, 2 * NT)

        if dstT is not None:
            @block.tensor
            def _(pe):
                for t in range(NT):
                    pe.wait_ge(rows_done, t + 1)
                    if t >= 2:
                        pe.wait_ge(copied, 2 * (t - 1))
                    turn_tile(pe, g, banks[t % 2], dst, t, turned)


def merge_edges(g):
    with ExitStack() as ctx:
        s = Scope(g, ctx)
        masks = [s.sb(f"masks{i}", [TP, R, N], BF16) for i in range(4)]
        masks_in, merged, summed = s.sems("masks_in", 4), s.sem("masks_merged"), s.sem("counts_summed")
        v_chain, saved = s.sem("merge_vc"), s.sem("counts_saved")
        block = s.block()

        @block.scalar
        def _(act):
            for t in range(NT):
                act.wait_ge(summed, t + 1)
                act.dma_start(g.counts_dram[:, t, :], g.counts[:, t, :]).then_inc(saved, 16)
            act.wait_ge(saved, 16 * NT)

        @block.sync
        def _(sp):
            for t in range(NT):
                if t >= 4:
                    sp.wait_ge(merged, t - 3)
                sp.dma_start(masks[t % 4][:, :, :], g.far_dram[t * TP * R:(t + 1) * TP * R, :]
                             .rearrange("(d r) s -> d r s", r=R)).then_inc(masks_in[t % 4], 16)

        @block.vector
        def _(dve):
            link = chain(dve, v_chain)
            for t in range(NT):
                dve.wait_ge(masks_in[t % 4], t // 4 * 16 + 16)
                link(dve.tensor_tensor(g.far_u[:, t, :], masks[t % 4][:, 0, :], masks[t % 4][:, 1, :], op=ALU.max))
                dve.tensor_tensor(g.far_u[:, t, :], g.far_u[:, t, :], masks[t % 4][:, 2, :],
                                  op=ALU.max).then_inc(merged, 1)
                by_rel = g.counts[:, t, :].rearrange("p (d r) -> p r d", r=R)
                link(dve.tensor_tensor(g.counts_u[:, t, :], by_rel[:, 0, :], by_rel[:, 1, :], op=ALU.add))
                dve.tensor_tensor(g.counts_u[:, t, :], g.counts_u[:, t, :], by_rel[:, 2, :],
                                  op=ALU.add).then_inc(summed, 1)
            dve.wait_ge(merged, NT)
            dve.wait_ge(summed, NT)


def project_gat(g, hT, w_fc, w_res, attn_l, attn_r, ft, res, ks, qd):
    H, DH = 12, 64
    with ExitStack() as ctx:
        s = Scope(g, ctx)
        w2 = s.sb("gat_w2", [DH, 2, 2 * DH])
        pair = s.sb("gat_pair", [128, 2, 128])
        attn = s.sb("gat_attn", [2 * H, DH])
        attnT = s.sb("gat_attnT", [DH, 2 * H])
        score_w = s.sb("gat_score_w", [128, KC, 2, H])
        score_flat = score_w[:, :, :, :].rearrange("p c l h -> p (c l h)")
        out_ps = [s.ps(f"gat_out{i}", [128, 3, 512]) for i in range(2)]
        chunks = [o[0:TP, :, :].rearrange("p a b -> p (a b)").rearrange("p (c i e) -> p c i e", c=KC, i=2)
                  for o in out_ps]
        score_ps = [s.ps(f"gat_score{i}", [128, 512]) for i in range(2)]
        w_in = s.sem("gat_w_in")
        zeroed, w_turned, w_copied = s.sem("gat_zeroed"), s.sem("gat_w_turned"), s.sem("gat_w_copied")
        s_made, s_copied = s.sem("gat_s_made"), s.sem("gat_s_copied")
        made, values_out, rest_out = s.sem("gat_made"), s.sem("gat_values_out"), s.sem("gat_rest_out")
        block = s.block()

        @block.sync
        def _(sp):
            for i, w in enumerate((w_fc, w_res)):
                for k in range(2):
                    sp.dma_start(w2[:, i, k * DH:(k + 1) * DH], w).then_inc(w_in, 16)
            for i, a in enumerate((attn_l, attn_r)):
                sp.dma_start(attn[i * H:(i + 1) * H, :], a).then_inc(w_in, 16)

        @block.gpsimd
        def _(pool):
            pool.memset(pair[:, :, :], 0.0).then_inc(zeroed, 1)
            pool.memset(score_w[:, :, :, :], 0.0).then_inc(zeroed, 1)
            pool.memset(ft[:, :, :, DH:DH + 1], 1.0).then_inc(zeroed, 1)

        @block.vector
        def _(dve):
            dve.wait_ge(w_turned, 1)
            dve.wait_ge(zeroed, 2)
            for i in range(2):
                for k in range(2):
                    dve.tensor_copy(pair[k * DH:(k + 1) * DH, i, k * DH:(k + 1) * DH],
                                    out_ps[0][k * DH:(k + 1) * DH, i, 0:DH])
            dve.tensor_copy(attnT[:, :], out_ps[0][0:DH, 2, 0:2 * H]).then_inc(w_copied, 1)
            dve.wait_ge(s_made, 1)
            for k in range(2):
                for lr in range(2):
                    first = lr * H + k
                    last = dve.tensor_copy(score_flat[k * DH:(k + 1) * DH, first:first + 26 * (KC - 1) + 1:26],
                                           score_ps[0][k * DH:(k + 1) * DH, lr * H + k:lr * H + H:2])
            last.then_inc(s_copied, 1)
            for t in range(NT):
                dve.wait_ge(made, t + 1)
                dve.tensor_copy(ks[:, t, :], score_ps[t % 2][0:TP, 0:H])
                dve.tensor_copy(qd[:, t, :], score_ps[t % 2][0:TP, H:2 * H]).then_inc(rest_out, 1)

        @block.tensor
        def _(pe):
            pe.wait_ge(w_in, 96)
            for i in range(2):
                pe.transpose(out_ps[0][:, i, 0:DH], w2[:, i, :], g.ident[0:DH, 0:DH])
            pe.transpose(out_ps[0][0:DH, 2, 0:2 * H], attn[:, :], g.ident[0:2 * H, 0:2 * H]).then_inc(w_turned, 1)
            pe.wait_ge(w_copied, 1)
            pe.matmul(score_ps[0][:, 0:2 * H], w2[:, 0, :], attnT[:, :], start=True, stop=True).then_inc(s_made, 1)
            pe.wait_ge(s_copied, 1)
            for t in range(NT):
                if t >= 2:
                    pe.wait_ge(values_out, t - 1)
                    pe.wait_ge(rest_out, t - 1)
                for c in range(KC):
                    x_c = hT[:, c, t * TP:(t + 1) * TP]
                    pe.matmul(out_ps[t % 2][0:TP, c // 2, (c % 2) * 256:(c % 2 + 1) * 256], x_c,
                              pair[:, :, :].rearrange("p i e -> p (i e)"), start=True, stop=True)
                    last = pe.matmul(score_ps[t % 2][0:TP, 0:2 * H], x_c,
                                     score_w[:, c, :, :].rearrange("p l h -> p (l h)"),
                                     start=(c == 0), stop=(c == KC - 1))
                last.then_inc(made, 1)

        @block.scalar
        def _(act):
            for t in range(NT):
                act.wait_ge(made, t + 1)
                act.activation(res[:, t, :].rearrange("p (c e) -> p c e", c=KC), chunks[t % 2][:, :, 1, :], ACT.Copy)
                act.activation(ft[:, t, :, 0:DH].rearrange("p (c k) e -> p c k e", k=2),
                               chunks[t % 2][:, :, 0, :].rearrange("p c (k e) -> p c k e", k=2),
                               ACT.Copy).then_inc(values_out, 1)
            act.wait_ge(values_out, NT)


def greatest(g, tag, heads, group, row, mask_of, ks, qd, ks_low, shifted, score_of=None, beside=None,
             junk=None):
    CH = ks.shape[2]
    rels = CH // heads
    NG = CH // group
    RB = len(row)
    MB = 4
    with ExitStack() as ctx:
        s = Scope(g, ctx)
        least = s.sb(f"{tag}_least", [TP, CH])
        most = s.sb(f"{tag}_most", [TP, NT, CH])
        leaky = s.sb(f"{tag}_leaky", [TP, NT, CH])
        top = s.sb(f"{tag}_top", [TP, NT, heads])
        rowsT = s.sb(f"{tag}_rowsT", [CH, N])
        low = s.sb(f"{tag}_low", [CH, 1])
        junk = junk or [s.sb(f"{tag}_junk{i}", [TP, N])[:, :] for i in range(2)]
        mask = [s.sb(f"{tag}_mask{i}", [TP, N], BF16) for i in range(MB)] if mask_of else None
        turn_ps = s.ps(f"{tag}_turn", [CH, 3, 512])
        score_ps = s.ps(f"{tag}_score_ps", [TP, 512]) if score_of else None
        tile, weights = score_of or (None, None)
        in_parts = bool(score_of) and len(tile(0, 0)) == 2
        weight_parts = [s.sb(f"{tag}_score_w{j}", [128, KC, 2 * CH], FR) for j in range(2)] if in_parts else None
        scored, scores_out, weights_split = s.sem(f"{tag}_scored"), s.sem(f"{tag}_scores_out"), s.sem(f"{tag}_w_split")
        turned, copied, low_done = s.sem(f"{tag}_turned"), s.sem(f"{tag}_copied"), s.sem(f"{tag}_low_done")
        out_done, low_out, least_in = s.sem(f"{tag}_rows_out"), s.sem(f"{tag}_low_out"), s.sem(f"{tag}_least_in")
        row_in, mask_in = s.sems(f"{tag}_row_in", RB), s.sems(f"{tag}_mask_in", MB)
        junked, v_chain, low_scaled = s.sem(f"{tag}_junked"), s.sem(f"{tag}_vc"), s.sem(f"{tag}_low_scaled")
        other = beside(s) if beside else None
        block = s.block()

        @block.tensor
        def _(pe):
            if score_of:
                if in_parts:
                    pe.wait_ge(weights_split, 2)
                for t in range(NT):
                    out = score_ps[:, t * 2 * CH:(t + 1) * 2 * CH]
                    for c in range(KC):
                        if in_parts:
                            last = three(pe, out, tile(c, t), [x[:, c, :] for x in weight_parts], c == 0, c == KC - 1)
                        else:
                            last = pe.matmul(out, tile(c, t)[0], weights[:, c, :, :, :].rearrange("p i r h -> p (i r h)"),
                                             start=(c == 0), stop=(c == KC - 1))
                last.then_inc(scored, 1)
                pe.wait_ge(scores_out, 1)
            for t in range(NT):
                last = pe.transpose(turn_ps[:, t // 4, (t % 4) * TP:(t % 4 + 1) * TP], ks[:, t, :],
                                    g.ident[0:TP, 0:TP])
            last.then_inc(turned, 1)
            if other:
                other.tensor(pe)

        if other:
            @block.gpsimd
            def _(pool):
                other.pool(pool)

        @block.scalar
        def _(act):
            if other:
                other.load(act)
            act.wait_ge(turned, 1)
            act.activation(rowsT[:, 0:8 * TP].rearrange("p (a b) -> p a b", a=2), turn_ps[:, 0:2, 0:4 * TP],
                           ACT.Copy).then_inc(copied, 1)
            act.activation(rowsT[:, 8 * TP:N], turn_ps[:, 2, 0:2 * TP], ACT.Copy).then_inc(copied, 1)
            act.activation(ks_low[:, :, :], ks[:, :, :], ACT.Copy, scale=0.2).then_inc(low_scaled, 1)
            if other:
                other.scalar(act)
            act.wait_ge(low_scaled, 1)

        @block.sync
        def _(sp):
            def load_masks(m):
                if m >= MB:
                    sp.wait_ge(junked, (m - MB + 1) * group)
                sp.dma_start(mask[m % MB][:, :], mask_of(m // NT, m % NT)).then_inc(mask_in[m % MB], 16)

            def load_rows(n):
                if n >= RB:
                    sp.wait_ge(junked, (n - RB + 1) * NT * group)
                src = bass.AP(tensor=g.rows_dram.tensor, offset=n * group * N, ap=[[0, TP], [N, group], [1, N]])
                sp.dma_start(row[n % RB], src).then_inc(row_in[n % RB], 16)

            if mask:
                for m in range(MB):
                    load_masks(m)
            sp.wait_ge(copied, 2)
            sp.dma_start(g.rows_dram[0:CH, :], rowsT[:, :]).then_inc(out_done, 16)
            sp.wait_ge(out_done, 16)
            for n in range(RB - 1):
                load_rows(n)
            sp.wait_ge(low_done, 1)
            sp.dma_start(g.low_dram[0:CH, :], low[:, :]).then_inc(low_out, 16)
            sp.wait_ge(low_out, 16)
            sp.dma_start(least[:, :], rows_of(g.low_dram, TP, 0, CH)).then_inc(least_in, 16)
            for n in range(NG):
                for t in range(NT if mask else 0):
                    if n * NT + t + MB < NG * NT:
                        load_masks(n * NT + t + MB)
                    if t == 0 and n + RB - 1 < NG:
                        load_rows(n + RB - 1)
                if not mask and n + RB - 1 < NG:
                    load_rows(n + RB - 1)

        @block.vector
        def _(dve):
            link = chain(dve, v_chain)
            if in_parts:
                flat = weights[:, :, :, :, :].rearrange("p c i r h -> p c (i r h)")
                dve.tensor_copy(weight_parts[0][:, :, :], flat).then_inc(weights_split, 1)
                dve.wait_ge(weights_split, 1)
                dve.tensor_tensor(weight_parts[1][:, :, :], flat, weight_parts[0][:, :, :].bitcast(F32),
                                  op=ALU.subtract).then_inc(weights_split, 1)
            if score_of:
                dve.wait_ge(scored, 1)
                parts = score_ps[:, 0:NT * 2 * CH].rearrange("p (t i c) -> p t i c", i=2, c=CH)
                dve.tensor_copy(qd[:, :, :], parts[:, :, 0, :])
                dve.tensor_copy(ks[:, :, :], parts[:, :, 1, :]).then_inc(scores_out, 1)
            dve.wait_ge(copied, 2)
            dve.tensor_reduce(out=low[:, :], in_=rowsT[:, :], op=ALU.min, axis=AX_X).then_inc(low_done, 1)
            for n in range(NG):
                dve.wait_ge(row_in[n % RB], n // RB * 16 + 16)
                for t in range(NT):
                    m = n * NT + t
                    if mask:
                        dve.wait_ge(mask_in[m % MB], m // MB * 16 + 16)
                    for k in range(group):
                        i = m * group + k
                        c = n * group + k
                        if i >= 2:
                            dve.wait_ge(junked, i - 1)
                        far = mask[m % MB][:, :] if mask else g.far_u[:, t, :]
                        dve.tensor_tensor_reduce(out=junk[i % 2], in0=far, in1=row[n % RB][:, k, :],
                                                 scale=1.0, scalar=3 * FAR, op0=ALU.add, op1=ALU.max,
                                                 accum_out=most[:, t, c:c + 1]).then_inc(junked, 1)
            dve.wait_ge(junked, CH * NT)
            dve.wait_ge(least_in, 16)
            all_tiles = least[:, :].unsqueeze(1).to_broadcast([TP, NT, CH])
            link(dve.tensor_tensor(most[:, :, :], most[:, :, :], all_tiles, op=ALU.max))
            link(dve.tensor_tensor(most[:, :, :], most[:, :, :], qd[:, :, :], op=ALU.add))
            link(dve.scalar_tensor_tensor(out=leaky[:, :, :], in0=most[:, :, :], scalar=0.2, in1=most[:, :, :],
                                          op0=ALU.mult, op1=ALU.max))
            link(dve.tensor_copy(top[:, :, :], leaky[:, :, 0:heads]))
            for r in range(1, rels):
                link(dve.tensor_tensor(top[:, :, :], top[:, :, :], leaky[:, :, r * heads:(r + 1) * heads],
                                       op=ALU.max))
            for r in range(rels):
                at = slice(r * heads, (r + 1) * heads)
                link(dve.tensor_tensor(shifted[:, :, 0, at], qd[:, :, at], top[:, :, :], op=ALU.subtract))
                link(dve.scalar_tensor_tensor(out=shifted[:, :, 1, at], in0=qd[:, :, at], scalar=0.2,
                                              in1=top[:, :, :], op0=ALU.mult, op1=ALU.subtract))


class RelationWeights:

    def __init__(self, s, g, layers, weights):
        self.g, self.layers, self.weights = g, layers, weights
        self.qk = [s.sb(f"relw_qk{n}", [128, KC, 2, q.shape[1]]) for n, (w, q, k) in enumerate(layers)]
        self.chunk = [s.sb(f"relw_chunk{i}", [128, D]) for i in range(2)]
        self.wT = [s.sb(f"relw_wT{i}", [128, KC, 128]) for i in range(2)]
        self.turn_ps = [s.ps(f"relw_turn{i}", [128, 2, 512]) for i in range(2)]
        self.out_ps = s.ps("relw_out", [128, 512])
        self.qk_in, self.chunk_in = s.sem("relw_qk_in"), s.sems("relw_chunk_in", 2)
        self.turned, self.copied, self.made = s.sem("relw_turned"), s.sem("relw_copied"), s.sem("relw_made")
        self.taken = s.sem("relw_taken")
        self.steps = [(n, r, c) for n in range(len(layers)) for r in range(R) for c in range(KC)]

    def load_chunk(self, act, i):
        n, r, c = self.steps[i]
        act.dma_start(self.chunk[i % 2][:, :], self.layers[n][0][r, c * 128:(c + 1) * 128, :]
                      ).then_inc(self.chunk_in[i % 2], 16)

    def load(self, act):
        for n, (w, q, k) in enumerate(self.layers):
            for i, v in enumerate((q, k)):
                act.dma_start(self.qk[n][:, :, i, :], v.rearrange("(c p) h -> p c h", p=128),
                              allow_slow_non_contiguous=True).then_inc(self.qk_in, 16)
        self.load_chunk(act, 0)
        self.load_chunk(act, 1)

    def pool(self, pool):
        pass

    def tensor(self, pe):
        pe.wait_ge(self.qk_in, 32 * len(self.layers))
        for i in range(len(self.steps) + 1):
            if i < len(self.steps):
                pe.wait_ge(self.chunk_in[i % 2], i // 2 * 16 + 16)
                if i >= 2:
                    pe.wait_ge(self.copied, i - 1)
                for f in range(KC):
                    last = pe.transpose(self.turn_ps[i % 2][:, f // 3, (f % 3) * 128:(f % 3 + 1) * 128],
                                        self.chunk[i % 2][:, f * 128:(f + 1) * 128], self.g.ident[:, :])
                last.then_inc(self.turned, 1)
            if i >= 1:
                n, r, c = self.steps[i - 1]
                H2 = 2 * self.weights[n].shape[4]
                at = (r * KC + c) * H2
                if n >= 1 and r == 0 and c == 0:
                    pe.wait_ge(self.taken, n)
                pe.wait_ge(self.copied, i)
                for f in range(KC):
                    last = pe.matmul(self.out_ps[:, at:at + H2], self.wT[(i - 1) % 2][:, f, :],
                                     self.qk[n][:, f, :, :].rearrange("p i h -> p (i h)"),
                                     start=(f == 0), stop=(f == KC - 1))
                last.then_inc(self.made, 1)

    def scalar(self, act):
        for i in range(len(self.steps)):
            act.wait_ge(self.turned, i + 1)
            if i + 2 < len(self.steps):
                self.load_chunk(act, i + 2)
            if i >= 2:
                act.wait_ge(self.made, i - 1)
            act.activation(self.wT[i % 2][:, :, :].rearrange("p (a b) d -> p a (b d)", a=2),
                           self.turn_ps[i % 2][:, :, 0:384], ACT.Copy).then_inc(self.copied, 1)
            if (i + 1) % (R * KC) == 0:
                n = i // (R * KC)
                H = self.weights[n].shape[4]
                act.wait_ge(self.made, i + 1)
                for r in range(R):
                    at = r * KC * 2 * H
                    last = act.activation(self.weights[n][:, :, :, r, :],
                                          self.out_ps[:, at:at + KC * 2 * H].rearrange("p (c i h) -> p c i h", i=2, h=H),
                                          ACT.Copy)
                last.then_inc(self.taken, 1)
        act.wait_ge(self.taken, len(self.layers))


class RelationValues:

    def __init__(self, s, g, tag, hT, w, b, bias):
        self.g, self.hT, self.w, self.b, self.bias = g, hT, w, b, bias
        self.bias_in = s.sem(f"{tag}_bias_in")
        self.w_sb = [s.sb(f"{tag}_w{i}", [128, KC, D]) for i in range(2)]
        self.stage = [s.sb(f"{tag}_stage{i}", [TP, D]) for i in range(3)]
        self.out_ps = [s.ps(f"{tag}_out{i}", [TP, 2, 512]) for i in range(2)]
        self.w_in, self.made, self.out = s.sems(f"{tag}_w_in", 2), s.sem(f"{tag}_made"), s.sem(f"{tag}_taken")
        self.sent = s.sems(f"{tag}_sent", 3)

    def load_w(self, act, r):
        act.dma_start(self.w_sb[r % 2][:, :, :], self.w[r, :, :].rearrange("(c p) f -> p c f", p=128)
                      ).then_inc(self.w_in[r % 2], 16)

    def load(self, act):
        self.load_w(act, 0)
        self.load_w(act, 1)
        act.dma_start(self.bias[:, :], rows_of(self.b, TP, 0, D)).then_inc(self.bias_in, 16)

    def pool(self, pool):
        pool.wait_ge(self.bias_in, 16)

    def tensor(self, pe):
        for n in range(R * NT):
            r, t = divmod(n, NT)
            if t == 0:
                pe.wait_ge(self.w_in[r % 2], r // 2 * 16 + 16)
            if n >= 2:
                pe.wait_ge(self.out, n - 1)
            for a in range(2):
                for c in range(KC):
                    last = pe.matmul(self.out_ps[n % 2][:, a, 0:384], self.hT[:, c, t * TP:(t + 1) * TP],
                                     self.w_sb[r % 2][:, c, a * 384:(a + 1) * 384], start=(c == 0), stop=(c == KC - 1))
            last.then_inc(self.made, 1)

    def scalar(self, act):
        def send(n):
            r, t = divmod(n, NT)
            act.wait_ge(self.out, n + 1)
            act.dma_start(self.g.values_dram[r, t * TP:(t + 1) * TP, :], self.stage[n % 3][:, :]
                          ).then_inc(self.sent[n % 3], 16)

        for n in range(R * NT):
            r, t = divmod(n, NT)
            act.wait_ge(self.made, n + 1)
            if t == NT - 1 and r + 2 < R:
                self.load_w(act, r + 2)
            if n >= 3:
                act.wait_ge(self.sent[n % 3], n // 3 * 16)
            act.activation(self.stage[n % 3][:, :].rearrange("p (a b) -> p a b", a=2), self.out_ps[n % 2][:, :, 0:384],
                           ACT.Copy).then_inc(self.out, 1)
            if n >= 1:
                send(n - 1)
        send(R * NT - 1)
        for i in range(3):
            act.wait_ge(self.sent[i], R * NT // 3 * 16)


class WideRelationValues:

    HALF = D // 2

    def __init__(self, s, g, tag, parts, w, b, bias, stage):
        self.g, self.parts, self.w, self.b, self.bias, self.stage = g, parts, w, b, bias, stage
        self.raw = [s.sb(f"{tag}_raw{i}", [128, KC, self.HALF]) for i in range(2)]
        self.w_parts = [[s.sb(f"{tag}_w{i}{j}", [128, KC, self.HALF], FR) for j in range(2)] for i in range(2)]
        self.out_ps = [s.ps(f"{tag}_out{i}", [TP, 512]) for i in range(4)]
        self.bias_in, self.bias_added = s.sem(f"{tag}_bias_in"), s.sem(f"{tag}_bias_added")
        self.raw_in, self.high, self.low = s.sems(f"{tag}_raw_in", 2), s.sem(f"{tag}_high"), s.sem(f"{tag}_low")
        self.made, self.out = s.sem(f"{tag}_made"), s.sem(f"{tag}_out_taken")
        self.sent = s.sems(f"{tag}_sent", 4)
        self.halves = [(r, a) for r in range(R) for a in range(2)]

    def load_half(self, act, k):
        r, a = self.halves[k]
        act.dma_start(self.raw[k % 2][:, :, :], self.w[r, :, a * self.HALF:(a + 1) * self.HALF]
                      .rearrange("(c p) f -> p c f", p=128)).then_inc(self.raw_in[k % 2], 16)

    def load(self, act):
        self.load_half(act, 0)
        self.load_half(act, 1)
        act.dma_start(self.bias[:, :], rows_of(self.b, TP, 0, D)).then_inc(self.bias_in, 16)

    def pool(self, pool):
        for k in range(len(self.halves)):
            pool.wait_ge(self.high, k + 1)
            pool.tensor_tensor(self.w_parts[k % 2][1][:, :, :], self.raw[k % 2][:, :, :],
                               self.w_parts[k % 2][0][:, :, :].bitcast(F32), op=ALU.subtract).then_inc(self.low, 1)
            if k == 1:
                pool.wait_ge(self.bias_in, 16)
                for t in range(NT):
                    x_t = self.g.x[:, t, :]
                    pool.tensor_tensor(x_t, x_t, self.bias[:, :], op=ALU.add).then_inc(self.bias_added, 1)
        pool.wait_ge(self.bias_added, NT)

    def tensor(self, pe):
        for n in range(len(self.halves) * NT):
            k, t = divmod(n, NT)
            if t == 0:
                pe.wait_ge(self.high, k + 1)
                pe.wait_ge(self.low, k + 1)
            if n >= 4:
                pe.wait_ge(self.out, n - 3)
            for c in range(KC):
                last = three(pe, self.out_ps[n % 4][:, 0:self.HALF], [x[:, c, t, 0:TP] for x in self.parts],
                             [x[:, c, :] for x in self.w_parts[k % 2]], c == 0, c == KC - 1)
            last.then_inc(self.made, 1)

    def scalar(self, act):
        def make_high(k):
            act.wait_ge(self.raw_in[k % 2], k // 2 * 16 + 16)
            if k >= 2:
                act.wait_ge(self.made, (k - 1) * NT)
            act.activation(self.w_parts[k % 2][0][:, :, :], self.raw[k % 2][:, :, :], ACT.Copy).then_inc(self.high, 1)

        def send(n):
            k, t = divmod(n, NT)
            r, a = self.halves[k]
            act.wait_ge(self.out, n + 1)
            act.dma_start(self.g.values_dram[r, t * TP:(t + 1) * TP, a * self.HALF:(a + 1) * self.HALF],
                          self.stage[n % 4]).then_inc(self.sent[n % 4], 16)

        steps = len(self.halves) * NT
        make_high(0)
        for n in range(steps):
            k, t = divmod(n, NT)
            if t == 1 and k + 1 < len(self.halves):
                make_high(k + 1)
            if t == 5 and k + 2 < len(self.halves):
                act.wait_ge(self.high, k + 1)
                act.wait_ge(self.low, k + 1)
                self.load_half(act, k + 2)
            act.wait_ge(self.made, n + 1)
            if n >= 4:
                act.wait_ge(self.sent[n % 4], n // 4 * 16)
            act.activation(self.stage[n % 4], self.out_ps[n % 4][:, 0:self.HALF], ACT.Copy).then_inc(self.out, 1)
            if n >= 1:
                send(n - 1)
        send(steps - 1)
        for i in range(4):
            act.wait_ge(self.sent[i], len(range(i, steps, 4)) * 16)


def attend(g, tag, heads, width, span, ks, ks_low, shifted, finish):
    CH = ks.shape[2]
    rels = CH // heads
    units = [(h, d) for h in range(heads) for d in range(0, NT, span)]
    per_bank = 512 // (width + 1)
    nbanks = -(-span // per_bank)
    W = span * TP
    steps = [(u, r, t) for u in range(len(units)) for t in range(NT) for r in range(rels)]
    per_unit = NT * rels
    with ExitStack() as ctx:
        s = Scope(g, ctx)
        rows = [s.sb(f"{tag}_rows{i}", [TP, rels, 2, W]) for i in range(2)]
        shiftedT = rows[1][0:2 * CH, :, :, :].rearrange("p r i w -> p (r i w)")[:, 0:N]
        high = [s.sb(f"{tag}_high{i}", [TP, W]) for i in range(5)]
        lowb = [s.sb(f"{tag}_lowb{i}", [TP, W]) for i in range(4)]
        HB, LB = len(high), len(lowb)
        wts = high
        recip = s.sb(f"{tag}_recip", [TP, 2, span])
        stream = [s.sb(f"{tag}_values{i}", [TP, width + 1]) for i in range(4)]
        acc = [s.ps(f"{tag}_acc{i}", [TP, nbanks, 512]) for i in range(2)]
        turned, copied, out_done = s.sem(f"{tag}_turned"), s.sem(f"{tag}_copied"), s.sem(f"{tag}_rows_out")
        rows_in = s.sems(f"{tag}_rows_in", 2)
        exp_done, max_done, wts_done, wts_used = (s.sem(f"{tag}_{n}") for n in ("exp", "max", "wts", "wts_used"))
        value_in, acc_out = s.sems(f"{tag}_value_in", 4), s.sem(f"{tag}_acc_out")
        v_chain, ones = s.sem(f"{tag}_vc2"), s.sem(f"{tag}_ones")
        counts = s.sb(f"{tag}_counts", [TP, NT, KEYS], U16)
        counts_in = s.sems(f"{tag}_counts_in", 2)
        turn_ps2 = acc[1][0:2 * CH, :, :]
        block = s.block()

        def counts_of(r, t, at, w):
            return counts[:, t, :].rearrange("p (d r) -> p r d", r=R)[:, r, at:at + w]

        def tile_of(u, d):
            o = (d % per_bank) * (width + 1)
            return acc[u % 2][:, d // per_bank, o:o + width + 1]

        @block.tensor
        def _(pe):
            for t in range(NT):
                last = pe.transpose(turn_ps2[:, t // 4, (t % 4) * TP:(t % 4 + 1) * TP],
                                    shifted[:, t, :, :].rearrange("p a c -> p (a c)"), g.ident[0:TP, 0:TP])
            last.then_inc(turned, 1)
            pe.wait_ge(copied, 2)
            for i, (u, r, t) in enumerate(steps):
                h, d0 = units[u]
                n_tiles = min(span, NT - d0)
                first, final = i % per_unit == 0, i % per_unit == per_unit - 1
                if first and u >= 2:
                    pe.wait_ge(acc_out, u - 1)
                pe.wait_ge(value_in[i % 4], i // 4 * 16 + 16)
                if i == 0:
                    pe.wait_ge(ones, 4)
                pe.wait_ge(wts_done, i + 1)
                for d in range(n_tiles):
                    last = pe.matmul(tile_of(u, d), wts[i % HB][:, d * TP:(d + 1) * TP], stream[i % 4][:, :],
                                     start=first and d % per_bank == 0, stop=final, skip_group_check=True)
                last.then_inc(wts_used, 1)

        @block.scalar
        def _(act):
            act.wait_ge(turned, 1)
            act.activation(shiftedT[:, 0:8 * TP].rearrange("p (a b) -> p a b", a=2), turn_ps2[:, 0:2, 0:4 * TP],
                           ACT.Copy).then_inc(copied, 1)
            act.activation(shiftedT[:, 8 * TP:N], turn_ps2[:, 2, 0:2 * TP], ACT.Copy).then_inc(copied, 1)
            for i, (u, r, t) in enumerate(steps):
                h, d0 = units[u]
                w = min(span, NT - d0) * TP
                c = r * heads + h
                if i % per_unit == 0:
                    act.wait_ge(rows_in[u % 2], u // 2 * 16 * rels + 16 * rels)
                if i >= HB:
                    act.wait_ge(wts_used, i - HB + 1)
                if i >= LB:
                    act.wait_ge(max_done, i - LB + 1)
                act.activation(high[i % HB][:, 0:w], rows[u % 2][:, r, 0, 0:w], ACT.Exp, bias=ks[:, t, c:c + 1])
                act.activation(lowb[i % LB][:, 0:w], rows[u % 2][:, r, 1, 0:w], ACT.Exp,
                               bias=ks_low[:, t, c:c + 1]).then_inc(exp_done, 1)

        def take_out(dve, link, u):
            h, d0 = units[u]
            n_tiles = min(span, NT - d0)
            dve.wait_ge(wts_used, (u + 1) * per_unit)
            for d in range(n_tiles):
                last = dve.tensor_scalar(recip[:, u % 2, d:d + 1], tile_of(u, d)[:, width:width + 1], 1e-16, None,
                                         op0=ALU.add)
            link(last)
            link(dve.reciprocal(recip[:, u % 2, 0:n_tiles], recip[:, u % 2, 0:n_tiles]))
            for d in range(n_tiles):
                last = finish(dve, h, d0 + d, 0, width, tile_of(u, d)[:, 0:width], recip[:, u % 2, d:d + 1])
            last.then_inc(acc_out, 1)

        @block.vector
        def _(dve):
            link = chain(dve, v_chain)

            def larger(i):
                u, r, t = steps[i]
                w = min(span, NT - units[u][1]) * TP
                dve.wait_ge(exp_done, i + 1)
                dve.tensor_tensor(high[i % HB][:, 0:w], high[i % HB][:, 0:w], lowb[i % LB][:, 0:w],
                                  op=ALU.max).then_inc(max_done, 1)

            larger(0)
            dve.wait_ge(counts_in[0], 16)
            for i, (u, r, t) in enumerate(steps):
                if (u, r, t) == (0, 0, 2):
                    dve.wait_ge(counts_in[1], 16)
                h, d0 = units[u]
                w = min(span, NT - d0) * TP
                if i + 1 < len(steps):
                    larger(i + 1)
                dve.wait_ge(max_done, i + 1)
                dve.scalar_tensor_tensor(out=wts[i % HB][:, 0:w], in0=high[i % HB][:, 0:w], scalar=1.0,
                                         in1=counts_of(r, t, d0 * TP, w), op0=ALU.min,
                                         op1=ALU.mult).then_inc(wts_done, 1)
                if i % per_unit == 2 and u >= 1:
                    take_out(dve, link, u - 1)
            take_out(dve, link, len(units) - 1)

        @block.sync
        def _(sp):
            sp.dma_start(counts[:, 0:2, :], g.counts_dram[:, 0:2, :]).then_inc(counts_in[0], 16)
            sp.wait_ge(copied, 2)
            sp.dma_start(g.rows_dram[0:2 * CH, :], shiftedT).then_inc(out_done, 16)
            sp.wait_ge(out_done, 16)

            def load_rows(u):
                h, d0 = units[u]
                w = min(span, NT - d0) * TP
                for r in range(rels):
                    src = bass.AP(tensor=g.rows_dram.tensor, offset=(r * heads + h) * N + d0 * TP,
                                  ap=[[0, TP], [CH * N, 2], [1, w]])
                    sp.dma_start(rows[u % 2][:, r, :, 0:w], src).then_inc(rows_in[u % 2], 16)

            load_rows(0)
            sp.dma_start(counts[:, 2:NT, :], g.counts_dram[:, 2:NT, :]).then_inc(counts_in[1], 16)
            load_rows(1)
            for i, (u, r, t) in enumerate(steps):
                if i >= 4:
                    sp.wait_ge(wts_used, i - 3)
                h, d0 = units[u]
                sp.dma_start(stream[i % 4][:, 0:width],
                             g.values_dram[r, t * TP:(t + 1) * TP, h * width:(h + 1) * width]
                             ).then_inc(value_in[i % 4], 16)
                if i % per_unit == 4 and u >= 1 and u + 1 < len(units):
                    sp.wait_ge(exp_done, u * per_unit)
                    load_rows(u + 1)

        @block.gpsimd
        def _(pool):
            for i in range(4):
                pool.memset(stream[i][:, width:width + 1], 1.0).then_inc(ones, 1)


def attend_narrow(g, tag, ks, ks_low, shifted, ft, res):
    H = ks.shape[2]
    WIDTH = ft.shape[3]
    DV = WIDTH - 1
    pieces = [(0, 512), (512, 1024), (1024, N)]
    steps = [(h, t) for h in range(H) for t in range(NT)]
    COPY, TURN, TAKE = 3, 5, 7
    HALF = NT // 2
    with ExitStack() as ctx:
        s = Scope(g, ctx)
        rows = [s.sb(f"{tag}_rows{i}", [TP, 2, N]) for i in range(2)]
        shiftedT = rows[1][0:2 * H, 0, :]
        masks = g.far_u[:, :, :].rearrange("p t n -> p (t n)").bitcast(F32)
        high = [masks[:, i * N:(i + 1) * N] for i in range(NT // 2)]
        lowb = [s.sb(f"{tag}_lowb{i}", [TP, N])[:, :] for i in range(4)]
        HB, LB = len(high), len(lowb)
        sumsT = s.sb(f"{tag}_sumsT", [WIDTH, N])
        recip = s.sb(f"{tag}_recip", [TP, NT])
        acc = [s.ps(f"{tag}_acc{i}", [128, 3, 512]) for i in range(2)]
        back = s.ps(f"{tag}_back", [TP, 2, 512])
        turned, copied, rows_out = s.sem(f"{tag}_turned"), s.sem(f"{tag}_copied"), s.sem(f"{tag}_rows_out")
        rows_in = s.sems(f"{tag}_rows_in", 2)
        exp_done, max_done, wts_done = s.sem(f"{tag}_exp"), s.sem(f"{tag}_max"), s.sem(f"{tag}_wts_done")
        multiplied, sums_out, sums_turned = s.sem(f"{tag}_multiplied"), s.sem(f"{tag}_sums_out"), s.sem(f"{tag}_sums_turned")
        taken, v_chain = s.sem(f"{tag}_taken"), s.sem(f"{tag}_vc")
        block = s.block()
        wts = high

        @block.tensor
        def _(pe):
            for t in range(NT):
                last = pe.transpose(acc[1][0:2 * H, t // 4, (t % 4) * TP:(t % 4 + 1) * TP],
                                    shifted[:, t, :, :].rearrange("p a c -> p (a c)"), g.ident[0:TP, 0:TP])
            last.then_inc(turned, 1)
            pe.wait_ge(copied, 2)

            def turn_sums(h):
                pe.wait_ge(sums_out, h + 1)
                if h >= 1:
                    pe.wait_ge(taken, h)
                for d in range(NT):
                    last = pe.transpose(back[:, d // HALF, (d % HALF) * WIDTH:(d % HALF + 1) * WIDTH],
                                        sumsT[:, d * TP:(d + 1) * TP], g.ident[0:WIDTH, 0:WIDTH])
                last.then_inc(sums_turned, 1)

            for i, (h, t) in enumerate(steps):
                if t == 0 and h >= 2:
                    pe.wait_ge(sums_out, h - 1)
                pe.wait_ge(wts_done, i + 1)
                for b, (c0, c1) in enumerate(pieces):
                    last = pe.matmul(acc[h % 2][0:WIDTH, b, 0:c1 - c0], ft[:, t, h, :], wts[i % HB][:, c0:c1],
                                     start=(t == 0), stop=(t == NT - 1))
                last.then_inc(multiplied, 1)
                if t == TURN and h >= 1:
                    turn_sums(h - 1)
            turn_sums(H - 1)

        @block.scalar
        def _(act):
            act.wait_ge(turned, 1)
            act.activation(shiftedT[:, 0:8 * TP].rearrange("p (a b) -> p a b", a=2), acc[1][0:2 * H, 0:2, 0:4 * TP],
                           ACT.Copy).then_inc(copied, 1)
            act.activation(shiftedT[:, 8 * TP:N], acc[1][0:2 * H, 2, 0:2 * TP], ACT.Copy).then_inc(copied, 1)

            def copy_sums(h):
                act.wait_ge(multiplied, (h + 1) * NT)
                if h >= 1:
                    act.wait_ge(sums_turned, h)
                act.activation(sumsT[:, :], acc[h % 2][0:WIDTH, :, :].rearrange("p a b -> p (a b)")[:, 0:N],
                               ACT.Copy).then_inc(sums_out, 1)

            for i, (h, t) in enumerate(steps):
                if t == 0:
                    act.wait_ge(rows_in[h % 2], h // 2 * 16 + 16)
                if i >= HB:
                    act.wait_ge(multiplied, i - HB + 1)
                if i >= LB:
                    act.wait_ge(max_done, i - LB + 1)
                act.activation(high[i % HB], rows[h % 2][:, 0, :], ACT.Exp, bias=ks[:, t, h:h + 1])
                act.activation(lowb[i % LB], rows[h % 2][:, 1, :], ACT.Exp,
                               bias=ks_low[:, t, h:h + 1]).then_inc(exp_done, 1)
                if t == COPY and h >= 1:
                    copy_sums(h - 1)
            copy_sums(H - 1)

        @block.vector
        def _(dve):
            link = chain(dve, v_chain)

            def larger(i):
                dve.wait_ge(exp_done, i + 1)
                dve.tensor_tensor(high[i % HB], high[i % HB], lowb[i % LB],
                                  op=ALU.max).then_inc(max_done, 1)

            def take_out(h):
                dve.wait_ge(sums_turned, h + 1)
                by_tile = back[:, :, 0:HALF * WIDTH].rearrange("p a (d w) -> p a d w", w=WIDTH)
                link(dve.tensor_scalar(recip[:, :].rearrange("p (a d) -> p a d", a=2), by_tile[:, :, :, DV], 1e-16, None,
                                       op0=ALU.add))
                link(dve.reciprocal(recip[:, :], recip[:, :]))
                for d in range(NT):
                    at = slice(h * DV, (h + 1) * DV)
                    last = dve.scalar_tensor_tensor(out=res[:, d, at], in0=by_tile[:, d // HALF, d % HALF, 0:DV],
                                                    scalar=recip[:, d:d + 1], in1=res[:, d, at],
                                                    op0=ALU.mult, op1=ALU.add)
                last.then_inc(taken, 1)

            larger(0)
            for i, (h, t) in enumerate(steps):
                if i + 1 < len(steps):
                    larger(i + 1)
                dve.wait_ge(max_done, i + 1)
                dve.scalar_tensor_tensor(out=wts[i % HB], in0=high[i % HB], scalar=1.0,
                                         in1=g.counts_u[:, t, :], op0=ALU.min, op1=ALU.mult).then_inc(wts_done, 1)
                if t == TAKE and h >= 1:
                    take_out(h - 1)
            take_out(H - 1)
            dve.wait_ge(taken, H)

        @block.sync
        def _(sp):
            sp.wait_ge(copied, 2)
            sp.dma_start(g.rows_dram[0:2 * H, :], shiftedT).then_inc(rows_out, 16)
            sp.wait_ge(rows_out, 16)
            for h in range(H):
                if h >= 2:
                    sp.wait_ge(exp_done, (h - 1) * NT)
                src = bass.AP(tensor=g.rows_dram.tensor, offset=h * N, ap=[[0, TP], [H * N, 2], [1, N]])
                sp.dma_start(rows[h % 2][:, :, :], src).then_inc(rows_in[h % 2], 16)


def attend_wide(g, tag, ks, ks_low, shifted, room, finish):
    CH = ks.shape[2]
    SPAN = 4
    units = [(d, min(d + SPAN, NT)) for d in range(0, NT, SPAN)]
    W = SPAN * TP
    COLS = D + 2
    pieces = [(0, 512), (512, COLS)]
    steps = [(u, r, t) for u in range(len(units)) for t in range(NT) for r in range(CH)]
    per_unit = NT * CH
    with ExitStack() as ctx:
        s = Scope(g, ctx)
        flat = room[:, :, :].rearrange("p t d -> p (t d)")
        rows = [flat[:, i * 2 * CH * W:(i + 1) * 2 * CH * W].rearrange("p (r i w) -> p r i w", r=CH, i=2)
                for i in range(2)]
        shiftedT = flat[0:2 * CH, 2 * CH * W:2 * CH * W + N]
        high = [s.sb(f"{tag}_high{i}", [TP, W]) for i in range(4)]
        lowb = [s.sb(f"{tag}_lowb{i}", [TP, W]) for i in range(3)]
        HB, LB, PB = len(high), len(lowb), 3
        wts = high
        wts_parts = [[s.sb(f"{tag}_wts_part{i}{j}", [TP, SPAN, TP + 1], FR) for j in range(2)] for i in range(PB)]
        values = [s.sb(f"{tag}_values{i}", [TP, COLS]) for i in range(3)]
        value_parts = [[s.sb(f"{tag}_value_part{i}{j}", [TP, COLS], FR) for j in range(2)] for i in range(PB)]
        recip = s.sb(f"{tag}_recip", [TP, SPAN])
        counts = s.sb(f"{tag}_counts", [TP, NT, KEYS], U16)
        acc = s.ps(f"{tag}_acc", [TP, SPAN, 2, 512])
        turn_ps = acc[0:2 * CH, :, :, :].rearrange("p a b c -> p (a b) c")
        turned, copied, rows_out = s.sem(f"{tag}_turned"), s.sem(f"{tag}_copied"), s.sem(f"{tag}_rows_out")
        rows_in, counts_in, value_in = s.sems(f"{tag}_rows_in", 2), s.sems(f"{tag}_counts_in", 2), s.sems(f"{tag}_value_in", 3)
        exp_done, max_done, wts_done = s.sem(f"{tag}_exp"), s.sem(f"{tag}_max"), s.sem(f"{tag}_wts_done")
        value_high, wts_high = s.sem(f"{tag}_value_high"), s.sem(f"{tag}_wts_high")
        value_low, wts_low = s.sem(f"{tag}_value_low"), s.sem(f"{tag}_wts_low")
        multiplied, acc_out, v_chain, ends = s.sem(f"{tag}_multiplied"), s.sem(f"{tag}_acc_out"), s.sem(f"{tag}_vc"), s.sem(f"{tag}_ends")
        block = s.block()

        def parts_of(part, w):
            return part[:, 0:w // TP, 0:TP]

        def by_tile(tensor, w):
            return tensor[:, 0:w].rearrange("p (d t) -> p d t", t=TP)

        @block.tensor
        def _(pe):
            for t in range(NT):
                last = pe.transpose(turn_ps[:, t // 4, (t % 4) * TP:(t % 4 + 1) * TP],
                                    shifted[:, t, :, :].rearrange("p a c -> p (a c)"), g.ident[0:TP, 0:TP])
            last.then_inc(turned, 1)
            pe.wait_ge(copied, 2)
            for i, (u, r, t) in enumerate(steps):
                d0, d1 = units[u]
                first, final = i % per_unit == 0, i % per_unit == per_unit - 1
                if first and u >= 1:
                    pe.wait_ge(acc_out, u)
                pe.wait_ge(value_low, i + 1)
                pe.wait_ge(wts_low, i + 1)
                for d in range(d1 - d0):
                    for b, (c0, c1) in enumerate(pieces):
                        last = three(pe, acc[:, d, b, 0:c1 - c0], [w[:, d, 0:TP] for w in wts_parts[i % PB]],
                                     [v[:, c0:c1] for v in value_parts[i % PB]], first, final)
                last.then_inc(multiplied, 1)

        @block.scalar
        def _(act):
            act.wait_ge(turned, 1)
            act.activation(shiftedT[:, 0:8 * TP].rearrange("p (a b) -> p a b", a=2), turn_ps[:, 0:2, 0:4 * TP],
                           ACT.Copy).then_inc(copied, 1)
            act.activation(shiftedT[:, 8 * TP:N], turn_ps[:, 2, 0:2 * TP], ACT.Copy).then_inc(copied, 1)
            act.wait_ge(ends, 3)

            def weigh(i):
                u, r, t = steps[i]
                w = (units[u][1] - units[u][0]) * TP
                if i % per_unit == 0:
                    act.wait_ge(rows_in[u % 2], u // 2 * 16 * CH + 16 * CH)
                if i >= HB:
                    act.wait_ge(wts_low, i - HB + 1)
                if i >= LB:
                    act.wait_ge(max_done, i - LB + 1)
                act.activation(high[i % HB][:, 0:w], rows[u % 2][:, r, 0, 0:w], ACT.Exp, bias=ks[:, t, r:r + 1])
                act.activation(lowb[i % LB][:, 0:w], rows[u % 2][:, r, 1, 0:w], ACT.Exp,
                               bias=ks_low[:, t, r:r + 1]).then_inc(exp_done, 1)

            weigh(0)
            weigh(1)
            for i, (u, r, t) in enumerate(steps):
                w = (units[u][1] - units[u][0]) * TP
                if i + 2 < len(steps):
                    weigh(i + 2)
                if i >= PB:
                    act.wait_ge(multiplied, i - PB + 1)
                act.wait_ge(value_in[i % 3], i // 3 * 16 + 16)
                act.activation(value_parts[i % PB][0][:, :], values[i % 3][:, :], ACT.Copy).then_inc(value_high, 1)
                act.wait_ge(wts_done, i + 1)
                act.activation(parts_of(wts_parts[i % PB][0], w), by_tile(wts[i % HB], w), ACT.Copy).then_inc(wts_high, 1)

        @block.vector
        def _(dve):
            link = chain(dve, v_chain)

            def take_out(u):
                d0, d1 = units[u]
                dve.wait_ge(multiplied, (u + 1) * per_unit)
                c0 = pieces[1][0]
                link(dve.tensor_scalar(recip[:, 0:d1 - d0], acc[:, 0:d1 - d0, 1, D - c0], 1e-16, None, op0=ALU.add))
                link(dve.reciprocal(recip[:, 0:d1 - d0], recip[:, 0:d1 - d0]))
                for d in range(d1 - d0):
                    for b, (c0, c1) in enumerate(pieces):
                        c1 = min(c1, D)
                        last = finish(dve, 0, d0 + d, c0, c1, acc[:, d, b, 0:c1 - c0], recip[:, d:d + 1])
                last.then_inc(acc_out, 1)

            def weigh(i):
                u, r, t = steps[i]
                d0, d1 = units[u]
                w = (d1 - d0) * TP
                dve.wait_ge(exp_done, i + 1)
                dve.tensor_tensor(high[i % HB][:, 0:w], high[i % HB][:, 0:w], lowb[i % LB][:, 0:w],
                                  op=ALU.max).then_inc(max_done, 1)
                dve.wait_ge(max_done, i + 1)
                by_relation = counts[:, t, :].rearrange("p (d r) -> p r d", r=R)[:, r, d0 * TP:d0 * TP + w]
                dve.scalar_tensor_tensor(out=wts[i % HB][:, 0:w], in0=high[i % HB][:, 0:w], scalar=1.0,
                                         in1=by_relation, op0=ALU.min, op1=ALU.mult).then_inc(wts_done, 1)

            dve.wait_ge(counts_in[0], 16)
            weigh(0)
            for i, (u, r, t) in enumerate(steps):
                if i == 2 * CH - 1:
                    dve.wait_ge(counts_in[1], 16)
                w = (units[u][1] - units[u][0]) * TP
                if i + 1 < len(steps):
                    weigh(i + 1)
                dve.wait_ge(value_high, i + 1)
                dve.tensor_tensor(value_parts[i % PB][1][:, :], values[i % 3][:, :],
                                  value_parts[i % PB][0][:, :].bitcast(F32), op=ALU.subtract).then_inc(value_low, 1)
                dve.wait_ge(wts_high, i + 1)
                dve.tensor_tensor(parts_of(wts_parts[i % PB][1], w), by_tile(wts[i % HB], w),
                                  parts_of(wts_parts[i % PB][0], w).bitcast(F32), op=ALU.subtract).then_inc(wts_low, 1)
                if i % per_unit == 1 and u >= 1:
                    take_out(u - 1)
            take_out(len(units) - 1)

        @block.sync
        def _(sp):
            sp.dma_start(counts[:, 0:2, :], g.counts_dram[:, 0:2, :]).then_inc(counts_in[0], 16)
            sp.wait_ge(copied, 2)
            sp.dma_start(g.rows_dram[0:2 * CH, :], shiftedT).then_inc(rows_out, 16)

            def load_rows(u):
                d0, d1 = units[u]
                w = (d1 - d0) * TP
                for r in range(CH):
                    src = bass.AP(tensor=g.rows_dram.tensor, offset=r * N + d0 * TP, ap=[[0, TP], [CH * N, 2], [1, w]])
                    sp.dma_start(rows[u % 2][:, r, :, 0:w], src).then_inc(rows_in[u % 2], 16)

            sp.wait_ge(rows_out, 16)
            load_rows(0)
            sp.dma_start(counts[:, 2:NT, :], g.counts_dram[:, 2:NT, :]).then_inc(counts_in[1], 16)
            load_rows(1)
            for i, (u, r, t) in enumerate(steps):
                if i >= 3:
                    sp.wait_ge(value_low, i - 2)
                    sp.wait_ge(value_high, i - 2)
                sp.dma_start(values[i % 3][:, 0:D], g.values_dram[r, t * TP:(t + 1) * TP, :]).then_inc(value_in[i % 3], 16)
                if i % per_unit == 4 and u >= 1 and u + 1 < len(units):
                    sp.wait_ge(exp_done, u * per_unit)
                    load_rows(u + 1)

        @block.gpsimd
        def _(pool):
            for v in values:
                pool.memset(v[:, D + 1:D + 2], 0.0)
                pool.memset(v[:, D:D + 1], 1.0).then_inc(ends, 1)


def gat_layer(g, src, dst, etype, w_fc, w_res, attn_l, attn_r, layers, weights):
    nc = g.nc
    H, DH = 12, 64
    with ExitStack() as ctx:
        g.counts = Scope(g, ctx).sb("counts", [TP, NT, KEYS], U16)
        count_edges(g, src, dst, etype)
        merge_edges(g)
    with ExitStack() as ctx:
        s = Scope(g, ctx)
        ks = s.sb("gat_ks", [TP, NT, H])
        qd = s.sb("gat_qd", [TP, NT, H])
        ks_low = s.sb("gat_ks_low", [TP, NT, H])
        shifted = s.sb("gat_shifted", [TP, NT, 2, H])
        res = s.sb("gat_res", [TP, NT, D])
        with ExitStack() as inner:
            si = Scope(g, inner)
            ft = si.sb("gat_ft", [TP, NT, H, DH + 1])
            with ExitStack() as inmost:
                hT = Scope(g, inmost).sb("gat_hT", [128, KC, N])
                normalize(g, "gat_ln", g.x, res, hT)
                project_gat(g, hT, w_fc, w_res, attn_l, attn_r, ft, res, ks, qd)

            with ExitStack() as inmost:
                sm = Scope(g, inmost)
                row = [sm.sb(f"gat_row{i}", [TP, 1, N])[:, :, :] for i in range(3)]
                greatest(g, "gat", H, 1, row, None, ks, qd, ks_low, shifted,
                         beside=lambda sc: RelationWeights(sc, g, layers, weights))
            attend_narrow(g, "gat2", ks, ks_low, shifted, ft, res)
        added = s.sem("gat_added")
        block = s.block()

        @block.vector
        def _(dve):
            for t in range(NT):
                dve.scalar_tensor_tensor(out=g.x[:, t, :], in0=res[:, t, :], scalar=0.0, in1=g.x[:, t, :],
                                         op0=ALU.max, op1=ALU.add).then_inc(added, 1)
            dve.wait_ge(added, NT)


def scratch(g):
    nc = g.nc
    g.far_dram = nc.dram_tensor("far_dram", (KEYS, N), BF16).ap()
    g.counts_dram = nc.dram_tensor("counts_dram", (TP, NT, KEYS), U16).ap()
    g.span_dram = nc.dram_tensor("span_dram", (2, 2, EH), F32).ap()
    g.range_dram = nc.dram_tensor("range_dram", (KT, 2), I32).ap()
    g.rows_dram = nc.dram_tensor("rows_dram", (24, N), F32).ap()
    g.low_dram = nc.dram_tensor("low_dram", (12, 1), F32).ap()
    g.h_dram = nc.dram_tensor("h_dram", (N, D), F32).ap()
    g.token_dram = nc.dram_tensor("token_dram", ((SLOT_TILES + 2) * TP, 1), I32).ap()
    g.tile_dram = nc.dram_tensor("tile_dram", (1, 2 * SLOT_TILES), I32).ap()
    g.sorted_dram = nc.dram_tensor("sorted_dram", ((SLOT_TILES + 2) * TP, D), F32).ap()
    g.slot_dram = nc.dram_tensor("slot_dram", (SLOT_TILES * TP, D), F32).ap()
    g.x_dram = nc.dram_tensor("x_dram", (TP, NT, D), F32).ap()
    g.score_dram = nc.dram_tensor("score_dram", (NT, TP), F32).ap()
    g.values_dram = nc.dram_tensor("values_dram", (R, N, D), F32).ap()


TOKENS = [(0, 417), (417, 834), (834, N)]


class ExpertWeights:

    def __init__(self, s, w1, w2):
        X, rows, F = w1.shape
        self.size = rows // 128 * F
        self.sources = (w1, w2)
        self.raw = [s.sb(f"moe_raw{n}", [128, self.size]) for n in range(2)]
        self.parts = [[s.sb(f"moe_w{n}{j}", [128, 2 * self.size], FR) for j in range(2)] for n in range(2)]
        self.zeros = s.sb("moe_zeros", [128, self.size])

    def load(self, sp, n, e, loaded):
        sp.dma_start(self.raw[n][:, :].rearrange("p (c f) -> p c f", f=self.sources[n].shape[2]),
                     self.sources[n][e, :, :].rearrange("(c p) f -> p c f", p=128)).then_inc(loaded, 16)

    def split(self, pool, n, e, high_done, high_count, ready):
        at = slice(e % 2 * self.size, (e % 2 + 1) * self.size)
        high, low = (x[:, at] for x in self.parts[n])
        pool.tensor_tensor(high, self.raw[n][:, :], self.zeros[:, :], op=ALU.add).then_inc(high_done, 1)
        pool.wait_ge(high_done, high_count)
        pool.tensor_tensor(low, self.raw[n][:, :], high.bitcast(F32), op=ALU.subtract).then_inc(ready, 1)


def route(g, hT, router_w, gate, gateT, rank, expert_weights):
    X = router_w.shape[0]
    with ExitStack() as ctx:
        s = Scope(g, ctx)
        rw = s.sb("route_w", [X, D])
        rwT = s.sb("route_wT", [128, KC, X])
        logits = s.sb("route_logits", [TP, NT, X])
        pairs = s.sb("route_pairs", [TP, NT, X, X])
        ties = s.sb("route_ties", [TP, NT, X, X])
        before = s.sb("route_before", [TP, X, X])
        top = s.sb("route_top", [TP, NT])
        turn_ps = s.ps("route_turn", [128, 512])
        logit_ps = s.ps("route_ps", [TP, 512])
        gate_ps = s.ps("route_gate", [X, 3, 512])
        w_in, w_turned, w_copied, made = s.sem("route_w_in"), s.sem("route_w_turned"), s.sem("route_w_copied"), s.sem("route_made")
        v_chain, before_done, shifted, exp_done = s.sem("route_vc"), s.sem("route_before_done"), s.sem("route_shifted"), s.sem("route_exp")
        gated, gate_turned, gate_out = s.sem("route_gated"), s.sem("route_gate_turned"), s.sem("route_gate_out")
        zeroed, raw_in, high_done, split = (s.sem(f"route_{x}") for x in ("zeroed", "raw_in", "high_done", "split"))
        block = s.block()

        @block.sync
        def _(sp):
            sp.dma_start(rw[:, :], router_w).then_inc(w_in, 16)
            for n in range(2):
                expert_weights.load(sp, n, 0, raw_in)

        @block.gpsimd
        def _(pool):
            pool.memset(before[:, :, :], 1.0).then_inc(before_done, 1)
            pool.wait_ge(before_done, 1)
            pool.affine_select(out=before[:, :, :], in_=before[:, :, :], compare_op=ALU.is_gt, fill=0.0,
                               base=0, pattern=[[1, X], [-1, X]], channel_multiplier=0).then_inc(before_done, 1)
            pool.memset(expert_weights.zeros[:, :], 0.0).then_inc(zeroed, 1)
            pool.wait_ge(zeroed, 1)
            pool.wait_ge(raw_in, 32)
            for n in range(2):
                expert_weights.split(pool, n, 0, high_done, n + 1, split)
            pool.wait_ge(split, 2)

        @block.tensor
        def _(pe):
            pe.wait_ge(w_in, 16)
            for c in range(KC):
                last = pe.transpose(turn_ps[:, c * X:(c + 1) * X], rw[:, c * 128:(c + 1) * 128], g.ident[0:X, 0:X])
            last.then_inc(w_turned, 1)
            pe.wait_ge(w_copied, 1)
            for t in range(NT):
                for c in range(KC):
                    last = pe.matmul(logit_ps[:, t * X:(t + 1) * X], hT[:, c, t * TP:(t + 1) * TP], rwT[:, c, :],
                                     start=(c == 0), stop=(c == KC - 1))
            last.then_inc(made, 1)
            pe.wait_ge(gated, 1)
            for t in range(NT):
                last = pe.transpose(gate_ps[:, t // 4, (t % 4) * TP:(t % 4 + 1) * TP], gate[:, t, :],
                                    g.ident[0:TP, 0:TP])
            last.then_inc(gate_turned, 1)

        @block.vector
        def _(dve):
            link = chain(dve, v_chain)
            dve.wait_ge(w_turned, 1)
            dve.tensor_copy(rwT[:, :, :].rearrange("p c e -> p (c e)"), turn_ps[:, 0:KC * X]).then_inc(w_copied, 1)
            dve.wait_ge(made, 1)
            link(dve.tensor_copy(logits[:, :, :].rearrange("p t e -> p (t e)"), logit_ps[:, 0:NT * X]))
            one = logits[:, :, :].unsqueeze(3).to_broadcast([TP, NT, X, X])
            other = logits[:, :, :].unsqueeze(2).to_broadcast([TP, NT, X, X])
            dve.tensor_tensor(pairs[:, :, :, :], other, one, op=ALU.is_gt)
            dve.wait_ge(before_done, 2)
            link(dve.tensor_tensor(ties[:, :, :, :], other, one, op=ALU.is_equal))
            link(dve.tensor_tensor(ties[:, :, :, :], ties[:, :, :, :],
                                   before[:, :, :].unsqueeze(1).to_broadcast([TP, NT, X, X]), op=ALU.mult))
            link(dve.tensor_tensor(pairs[:, :, :, :], pairs[:, :, :, :], ties[:, :, :, :], op=ALU.add))
            link(dve.tensor_reduce(out=rank[:, :, :], in_=pairs[:, :, :, :], op=ALU.add, axis=AX_X))
            link(dve.tensor_reduce(out=top[:, :], in_=logits[:, :, :], op=ALU.max, axis=AX_X))
            dve.tensor_tensor(logits[:, :, :], logits[:, :, :], top[:, :].unsqueeze(2).to_broadcast([TP, NT, X]),
                              op=ALU.subtract).then_inc(shifted, 1)
            dve.wait_ge(exp_done, 1)
            link(dve.scalar_tensor_tensor(out=gate[:, :, :], in0=rank[:, :, :], scalar=1.5, in1=logits[:, :, :],
                                          op0=ALU.is_lt, op1=ALU.mult))
            link(dve.tensor_reduce(out=top[:, :], in_=gate[:, :, :], op=ALU.add, axis=AX_X))
            link(dve.reciprocal(top[:, :], top[:, :]))
            dve.tensor_tensor(gate[:, :, :], gate[:, :, :], top[:, :].unsqueeze(2).to_broadcast([TP, NT, X]),
                              op=ALU.mult).then_inc(gated, 1)
            dve.wait_ge(gate_turned, 1)
            dve.tensor_copy(gateT[:, 0:8 * TP].rearrange("p (a b) -> p a b", a=2),
                            gate_ps[:, 0:2, 0:4 * TP]).then_inc(gate_out, 1)
            dve.tensor_copy(gateT[:, 8 * TP:N], gate_ps[:, 2, 0:2 * TP]).then_inc(gate_out, 1)
            dve.wait_ge(gate_out, 2)

        @block.scalar
        def _(act):
            act.wait_ge(shifted, 1)
            act.activation(logits[:, :, :], logits[:, :, :], ACT.Exp).then_inc(exp_done, 1)


def three(pe, out, still, moving, first, final):
    pe.matmul(out, still[0], moving[0], start=first, stop=False)
    pe.matmul(out, still[0], moving[1], start=False, stop=False)
    return pe.matmul(out, still[1], moving[0], start=False, stop=final)


SLOT_TILES = (2 * N) // TP + 8


def assign_slots(g, h, rank, gate, x_experts, slots, gates, b2, gateT):
    X = x_experts
    with ExitStack() as ctx:
        s = Scope(g, ctx)
        chosen = s.sb("slot_chosen", [TP, NT, X])
        lower = s.sb("slot_lower", [TP, TP])
        ones = s.sb("slot_ones", [TP, TP])
        place = s.sb("slot_place", [TP, NT, X])
        total = s.sb("slot_total", [TP, NT + 1, X])
        steps = s.sb("slot_steps", [TP, X, NT])
        over = s.sb("slot_over", [TP, X, NT])
        tiles = s.sb("slot_tiles", [TP, X])
        begin = s.sb("slot_begin", [TP, X + 1])
        pick = s.sb("slot_pick", [TP, NT, X])
        slots_f = s.sb("slot_slots_f", [TP, NT, 2])
        token = s.sb("slot_token", [TP, NT], I32)
        number = s.sb("slot_number", [1, SLOT_TILES])
        after = s.sb("slot_after", [1, X - 1, SLOT_TILES])
        even = s.sb("slot_even", [1, SLOT_TILES // 2])
        table = s.sb("slot_table", [1, 2, SLOT_TILES])
        table_i = s.sb("slot_table_i", [1, 2, SLOT_TILES], I32)
        empty = s.sb("slot_empty", [TP, SLOT_TILES + 2], I32)
        b2_sb = s.sb("slot_b2", [X, D])
        zeros = s.sb("slot_zeros", [TP, D])
        ps = [s.ps(f"slot_ps{i}", [TP, 512]) for i in range(2)]
        bias_ps = [s.ps(f"slot_bias{i}", [TP, 2, 512]) for i in range(2)]
        made, counted, v_chain, placed, b2_in = (s.sem(f"slot_{x}") for x in ("made", "counted", "vc", "placed", "b2_in"))
        cleared, h_out, table_out, tabled = (s.sem(f"slot_{x}") for x in ("cleared", "h_out", "table_out", "tabled"))
        scattered = s.software_sem("slot_scattered")
        biased, added, consts, zeroed, tail_out = (s.sem(f"slot_{x}") for x in ("biased", "added", "consts", "zeroed", "tail_out"))
        block = s.block()

        @block.gpsimd
        def _(pool):
            pool.memset(zeros[:, :], 0.0).then_inc(zeroed, 1)
            pool.memset(ones[:, :], 1.0).then_inc(consts, 1)
            pool.memset(lower[:, :], 1.0).then_inc(consts, 1)
            pool.memset(empty[:, :], 0).then_inc(consts, 1)
            pool.iota(token[:, :], [[TP, NT]], base=0, channel_multiplier=1).then_inc(consts, 1)
            pool.iota(steps[:, :, :], [[0, X], [TP, NT]], base=0, channel_multiplier=0,
                      allow_small_or_imprecise_dtypes=True).then_inc(consts, 1)
            pool.iota(number[:, :], [[1, SLOT_TILES]], base=0, channel_multiplier=0,
                      allow_small_or_imprecise_dtypes=True).then_inc(consts, 1)
            pool.wait_ge(consts, 6)
            pool.affine_select(out=lower[:, :], in_=lower[:, :], compare_op=ALU.is_gt, fill=0.0,
                               base=0, pattern=[[1, TP]], channel_multiplier=-1).then_inc(consts, 1)
            pool.wait_ge(cleared, 16)
            pool.wait_ge(placed, 1)
            for t in range(NT):
                for c in range(2):
                    pool.indirect_dma_start(out=g.token_dram, out_offset=bass.IndirectOffsetOnAxis(
                        ap=slots[:, t, c:c + 1], axis=0), in_=token[:, t:t + 1], in_offset=None).then_inc(scattered, 16)
            pool.wait_ge(scattered, 16 * 2 * NT)

        @block.sync
        def _(sp):
            sp.dma_start(b2_sb[:, :], b2).then_inc(b2_in, 16)
            sp.dma_start(g.h_dram.rearrange("(t p) d -> p t d", p=TP), h[:, :, :]).then_inc(h_out, 16)
            sp.wait_ge(consts, 6)
            sp.dma_start(g.token_dram.rearrange("(k p) o -> p (k o)", p=TP), empty[:, :],
                         allow_slow_non_contiguous=True).then_inc(cleared, 16)
            sp.wait_ge(zeroed, 1)
            for k in range(2 * N // TP, SLOT_TILES):
                sp.dma_start(g.slot_dram[k * TP:(k + 1) * TP, :], zeros[:, :]).then_inc(tail_out, 16)
            sp.wait_ge(tabled, 1)
            sp.dma_start(g.tile_dram, table_i[:, :, :].rearrange("p a b -> p (a b)")).then_inc(table_out, 16)
            sp.wait_ge(table_out, 16)
            sp.wait_ge(h_out, 16)
            sp.wait_ge(tail_out, 16 * (SLOT_TILES - 2 * N // TP))

        @block.tensor
        def _(pe):
            pe.wait_ge(made, 1)
            pe.wait_ge(consts, 7)
            flat = chosen[:, :, :].rearrange("p t e -> p (t e)")
            pe.matmul(ps[0][:, 0:NT * X], lower[:, :], flat, start=True, stop=True)
            pe.matmul(ps[1][:, 0:NT * X], ones[:, :], flat, start=True, stop=True).then_inc(counted, 1)
            pe.wait_ge(b2_in, 16)
            for t in range(NT):
                if t >= 2:
                    pe.wait_ge(added, t - 1)
                for a in range(2):
                    last = pe.matmul(bias_ps[t % 2][:, a, 0:384], gateT[:, t * TP:(t + 1) * TP],
                                     b2_sb[:, a * 384:(a + 1) * 384], start=True, stop=True)
                last.then_inc(biased, 1)

        @block.vector
        def _(dve):
            link = chain(dve, v_chain)
            dve.tensor_scalar(chosen[:, :, :], rank[:, :, :], 1.5, None, op0=ALU.is_lt).then_inc(made, 1)
            link(dve.memset(total[:, 0, :], 0.0))
            dve.wait_ge(counted, 1)
            link(dve.tensor_copy(place[:, :, :].rearrange("p t e -> p (t e)"), ps[0][:, 0:NT * X]))
            for t in range(NT):
                link(dve.tensor_tensor(total[:, t + 1, :], total[:, t, :], ps[1][:, t * X:(t + 1) * X], op=ALU.add))
            dve.wait_ge(consts, 7)
            link(dve.tensor_tensor(place[:, :, :], place[:, :, :], total[:, 0:NT, :], op=ALU.add))
            link(dve.tensor_tensor(over[:, :, :], total[:, NT, :].unsqueeze(2).to_broadcast([TP, X, NT]),
                                   steps[:, :, :], op=ALU.is_gt))
            link(dve.tensor_reduce(out=tiles[:, :], in_=over[:, :, :], op=ALU.add, axis=AX_X))
            link(dve.tensor_scalar(tiles[:, :], tiles[:, :], 1.0, None, op0=ALU.max))
            link(dve.memset(begin[:, 0:1], 0.0))
            for e in range(X):
                link(dve.tensor_tensor(begin[:, e + 1:e + 2], begin[:, e:e + 1], tiles[:, e:e + 1], op=ALU.add))
            link(dve.tensor_tensor(after[:, :, :], begin[0:1, 1:X].unsqueeze(2).to_broadcast([1, X - 1, SLOT_TILES]),
                                   number[:, :].unsqueeze(1).to_broadcast([1, X - 1, SLOT_TILES]), op=ALU.is_le))
            link(dve.tensor_reduce(out=table[:, 0, :], in_=after[:, :, :].rearrange("p e k -> p k e"), op=ALU.add,
                                   axis=AX_X))
            link(dve.memset(table[:, 1, :], 0.0))
            link(dve.tensor_copy(table[:, 1, 0:X - 1], begin[0:1, 1:X]))
            link(dve.tensor_scalar(even[:, :], number[:, 0:SLOT_TILES:2], begin[0:1, X:X + 1], None, op0=ALU.is_lt))
            link(dve.tensor_reduce(out=table[:, 1, X - 1:X], in_=even[:, :], op=ALU.add, axis=AX_X))
            dve.tensor_copy(table_i[:, :, :], table[:, :, :]).then_inc(tabled, 1)
            link(dve.tensor_scalar(begin[:, :], begin[:, :], float(TP), None, op0=ALU.mult))
            link(dve.tensor_tensor(place[:, :, :], place[:, :, :],
                                   begin[:, 0:X].unsqueeze(1).to_broadcast([TP, NT, X]), op=ALU.add))
            for c in range(2):
                for src, dst in ((place, slots_f), (gate, gates)):
                    link(dve.scalar_tensor_tensor(out=pick[:, :, :], in0=rank[:, :, :], scalar=float(c),
                                                  in1=src[:, :, :], op0=ALU.is_equal, op1=ALU.mult))
                    link(dve.tensor_reduce(out=dst[:, :, c], in_=pick[:, :, :], op=ALU.add, axis=AX_X))
            dve.tensor_copy(slots[:, :, :], slots_f[:, :, :]).then_inc(placed, 1)
            for t in range(NT):
                dve.wait_ge(biased, t + 1)
                x_t = g.x[:, t, :].rearrange("p (a b) -> p a b", a=2)
                dve.tensor_tensor(x_t, x_t, bias_ps[t % 2][:, :, 0:384], op=ALU.add).then_inc(added, 1)
            dve.wait_ge(placed, 1)
            dve.wait_ge(added, NT)


def experts(g, b1, expert_weights):
    X, F = b1.shape
    FC = F // 128
    with ExitStack() as ctx:
        s = Scope(g, ctx)
        up_w, down_w = expert_weights.parts
        b1_rows = s.sb("moe_b1", [TP, X * F])
        rows = [s.sb(f"moe_rows{u}", [TP, D]) for u in range(2)]
        tokens = s.sb("sort_tokens", [TP, SLOT_TILES + 2], I32)
        gathered = [s.sb(f"sort_rows{i}", [TP, D]) for i in range(4)]
        rowsT = [[s.sb(f"moe_rowsT{u}{j}", [128, KC, 126], FR) for j in range(2)] for u in range(2)]
        mid = [s.sb(f"moe_mid{u}", [TP, F]) for u in range(2)]
        midT = [[s.sb(f"moe_midT{u}{j}", [128, FC, 126], FR) for j in range(2)] for u in range(2)]
        out_sb = [s.sb(f"moe_out{u}", [TP, D]) for u in range(2)]
        table = s.sb("moe_table", [1, 2 * SLOT_TILES], I32)
        wide_ps = [s.ps(f"moe_wide{u}", [128, 2, 512]) for u in range(2)]
        mid_ps = [s.ps(f"moe_mid_ps{u}", [128, 512]) for u in range(2)]
        table_in, raw_in, raw_down_in = s.sem("moe_table_in"), s.sem("moe_raw_in"), s.sem("moe_raw_down_in")
        high_done, up_ready, down_ready = s.sem("moe_high_done"), s.sem("moe_up_ready"), s.sem("moe_down_ready")
        rows_in, turned, high_out, low_out = s.sems("moe_rows_in", 2), s.sem("moe_turned"), s.sem("moe_high_out"), s.sem("moe_low_out")
        up_done, bias_done, gelu_done = s.sem("moe_up_done"), s.sem("moe_bias_done"), s.sem("moe_gelu_done")
        mid_turned, mid_high, mid_low = s.sem("moe_mid_turned"), s.sem("moe_mid_high"), s.sem("moe_mid_low")
        down_done, taken, sent = s.sem("moe_down_done"), s.sem("moe_taken"), s.sems("moe_sent", 2)
        tokens_in, sorted_out, sorted_done = s.sem("sort_tokens_in"), s.sems("sort_out", 4), s.sem("sort_done")
        gathered_in = [s.software_sem(f"sort_in{i}") for i in range(4)]
        expert_free, all_sent = s.sem("moe_expert_free"), s.sem("moe_all_sent")
        block = s.block()

        def pairs_of(eng):
            return eng.value_load(table[0:1, SLOT_TILES + X - 1:SLOT_TILES + X], min_val=1, max_val=SLOT_TILES // 2)

        def expert_of(eng, tile):
            return eng.value_load(table[0:1, bass.ds(tile, 1)], min_val=0, max_val=X - 1)

        TILES = SLOT_TILES + 2
        GATHERS = [range(0, 6), range(6, 18), range(18, TILES)]

        @block.sync
        def _(sp):
            sp.dma_start(tokens[:, :], g.token_dram.rearrange("(k p) o -> p (k o)", p=TP),
                         allow_slow_non_contiguous=True).then_inc(tokens_in, 16)
            sp.dma_start(table[:, :], g.tile_dram).then_inc(table_in, 16)
            for e in range(X):
                if e >= 1:
                    sp.wait_ge(up_ready, e)
                    expert_weights.load(sp, 0, e, raw_in)
                    sp.wait_ge(down_ready, e)
                    expert_weights.load(sp, 1, e, raw_down_in)
                if e < len(GATHERS):
                    for k in GATHERS[e]:
                        sp.wait_ge(gathered_in[k % 4], k // 4 * 16 + 16)
                        sp.dma_start(g.sorted_dram[k * TP:(k + 1) * TP, :], gathered[k % 4][:, :]
                                     ).then_inc(sorted_out[k % 4], 16)
                        if k >= 1:
                            sp.wait_ge(sorted_out[(k - 1) % 4], (k - 1) // 4 * 16 + 16)
                            sp.nop().then_inc(sorted_done, 1)
                if e == len(GATHERS) - 1:
                    sp.wait_ge(sorted_out[(TILES - 1) % 4], (TILES - 1) // 4 * 16 + 16)
                    sp.nop().then_inc(sorted_done, 1)

        @block.gpsimd
        def _(pool):
            pool.wait_ge(table_in, 16)
            pool.wait_ge(tokens_in, 16)
            for e in range(X):
                for k in GATHERS[e] if e < len(GATHERS) else ():
                    if k >= 4:
                        pool.wait_ge(sorted_out[k % 4], k // 4 * 16)
                    pool.indirect_dma_start(out=gathered[k % 4][:, :], out_offset=None, in_=g.h_dram,
                                            in_offset=bass.IndirectOffsetOnAxis(ap=tokens[:, k:k + 1], axis=0)
                                            ).then_inc(gathered_in[k % 4], 16)
                if e >= 2:
                    begin = pool.value_load(table[0:1, SLOT_TILES + e - 2:SLOT_TILES + e - 1],
                                            min_val=1, max_val=SLOT_TILES)
                    pool.wait_ge(down_done, begin)
                    pool.nop().then_inc(expert_free, 1)
                for n, (loaded, ready) in enumerate(((raw_in, up_ready), (raw_down_in, down_ready))):
                    if e == 0:
                        pool.nop().then_inc(ready, 1)
                    else:
                        pool.wait_ge(loaded, e * 16)
                        expert_weights.split(pool, n, e, high_done, 2 * (e - 1) + n + 1, ready)

        @block.tensor
        def _(pe):
            pe.wait_ge(table_in, 16)
            with pe.Fori(0, pairs_of(pe)) as i:
                for u in range(2):
                    pe.wait_ge(rows_in[u], i * 16 + 16)
                    pe.wait_ge(taken, i * 2 + (u + 1))
                    for c in range(KC):
                        last = pe.transpose(wide_ps[u][:, c // 3, (c % 3) * TP:(c % 3 + 1) * TP],
                                            rows[u][:, c * 128:(c + 1) * 128], g.ident[0:TP, 0:TP])
                    last.then_inc(turned, 1)
                for u in range(2):
                    e = expert_of(pe, i * 2 + u)
                    parity = pe.snap(e % 2)
                    pe.wait_ge(up_ready, e + 1)
                    pe.wait_ge(low_out, i * 2 + (u + 1))
                    pe.wait_ge(mid_low, i * 2 + (u + 1))
                    for c in range(KC):
                        last = three(pe, mid_ps[u][0:TP, 0:F], [rowsT[u][j][:, c, 0:TP] for j in range(2)],
                                     [up_w[j][:, bass.ds(parity * (KC * F) + c * F, F)] for j in range(2)],
                                     c == 0, c == KC - 1)
                    last.then_inc(up_done, 1)
                for u in range(2):
                    e = expert_of(pe, i * 2 + u)
                    parity = pe.snap(e % 2)
                    pe.wait_ge(gelu_done, i * 2 + (u + 1))
                    for c in range(FC):
                        last = pe.transpose(mid_ps[u][:, c * TP:(c + 1) * TP], mid[u][:, c * 128:(c + 1) * 128],
                                            g.ident[0:TP, 0:TP])
                    last.then_inc(mid_turned, 1)
                    pe.wait_ge(down_ready, e + 1)
                    pe.wait_ge(mid_low, i * 2 + (u + 3))
                    for a in range(2):
                        for c in range(FC):
                            last = three(pe, wide_ps[u][0:TP, a, 0:384], [midT[u][j][:, c, 0:TP] for j in range(2)],
                                         [down_w[j][:, bass.ds(parity * (FC * D) + (c * D + a * 384), 384)]
                                          for j in range(2)], c == 0, c == FC - 1)
                    last.then_inc(down_done, 1)

        @block.vector
        def _(dve):
            dve.wait_ge(table_in, 16)
            for u in range(2):
                dve.nop().then_inc(mid_low, 1)
            dve.wait_ge(sent[0], 16)
            dve.wait_ge(sent[1], 16)
            with dve.Fori(0, pairs_of(dve)) as i:
                for u in range(2):
                    dve.wait_ge(turned, i * 2 + (u + 1))
                    dve.tensor_copy(rowsT[u][0][:, :, 0:TP].rearrange("p (a b) t -> p a b t", a=2),
                                    wide_ps[u][:, :, 0:3 * TP].rearrange("p a (b t) -> p a b t", t=TP)
                                    ).then_inc(high_out, 1)
                    dve.wait_ge(high_out, i * 2 + (u + 1))
                    dve.tensor_tensor(rowsT[u][1][:, :, 0:TP].rearrange("p (a b) t -> p a b t", a=2),
                                      wide_ps[u][:, :, 0:3 * TP].rearrange("p a (b t) -> p a b t", t=TP),
                                      rowsT[u][0][:, :, 0:TP].bitcast(F32).rearrange("p (a b) t -> p a b t", a=2),
                                      op=ALU.subtract).then_inc(low_out, 1)
                for u in range(2):
                    e = expert_of(dve, i * 2 + u)
                    dve.wait_ge(up_done, i * 2 + (u + 1))
                    dve.tensor_tensor(mid[u][:, :], mid_ps[u][0:TP, 0:F], b1_rows[:, bass.ds(e * F, F)],
                                      op=ALU.add).then_inc(bias_done, 1)
                for u in range(2):
                    dve.wait_ge(mid_turned, i * 2 + (u + 1))
                    dve.tensor_copy(midT[u][0][:, :, 0:TP], mid_ps[u][:, 0:FC * TP].rearrange("p (c t) -> p c t", t=TP)
                                    ).then_inc(mid_high, 1)
                    dve.wait_ge(mid_high, i * 2 + (u + 1))
                    dve.tensor_tensor(midT[u][1][:, :, 0:TP], mid_ps[u][:, 0:FC * TP].rearrange("p (c t) -> p c t", t=TP),
                                      midT[u][0][:, :, 0:TP].bitcast(F32), op=ALU.subtract).then_inc(mid_low, 1)
                for u in range(2):
                    dve.wait_ge(down_done, i * 2 + (u + 1))
                    dve.wait_ge(sent[u], i * 16 + 16)
                    dve.tensor_copy(out_sb[u][:, :].rearrange("p (a b) -> p a b", a=2), wide_ps[u][0:TP, :, 0:384]
                                    ).then_inc(taken, 1)

        @block.scalar
        def _(act):
            for u in range(2):
                act.wait_ge(sorted_done, u + 1)
                act.dma_start(rows[u][:, :], g.sorted_dram[u * TP:(u + 1) * TP, :]).then_inc(rows_in[u], 16)
                act.nop().then_inc(taken, 1)
                half = slice(u * (X * F // 2), (u + 1) * (X * F // 2))
                act.dma_start(b1_rows[:, half], rows_of(b1, TP, u * (X * F // 2), X * F // 2)).then_inc(sent[u], 16)
            act.wait_ge(table_in, 16)
            pairs = pairs_of(act)
            with act.Fori(0, pairs) as i:
                for u in range(2):
                    act.wait_ge(turned, i * 2 + (u + 1))
                    act.wait_ge(sorted_done, i * 2 + (u + 3))
                    act.dma_start(rows[u][:, :], g.sorted_dram[bass.ds((i * 2 + (u + 2)) * TP, TP), :]
                                  ).then_inc(rows_in[u], 16)
                for u in range(2):
                    act.wait_ge(bias_done, i * 2 + (u + 1))
                    act.activation(mid[u][:, :], mid[u][:, :], ACT.Gelu).then_inc(gelu_done, 1)
                for u in range(2):
                    act.wait_ge(taken, i * 2 + (u + 3))
                    act.dma_start(g.slot_dram[bass.ds((i * 2 + u) * TP, TP), :], out_sb[u][:, :]).then_inc(sent[u], 16)
            for u in range(2):
                act.wait_ge(sent[u], pairs * 16 + 16)
                act.wait_ge(rows_in[u], pairs * 16 + 16)
            act.nop().then_inc(all_sent, 1)


def combine(g, slots, gates):
    with ExitStack() as ctx:
        s = Scope(g, ctx)
        rows = [s.sb(f"comb_rows{i}", [TP, D]) for i in range(6)]
        rows_in, added = [s.software_sem(f"comb_rows_in{i}") for i in range(6)], s.sem("comb_added")
        block = s.block()
        steps = [(c, t) for c in range(2) for t in range(NT)]

        @block.gpsimd
        def _(pool):
            for i, (c, t) in enumerate(steps):
                if i >= 6:
                    pool.wait_ge(added, i - 5)
                pool.indirect_dma_start(out=rows[i % 6][:, :], out_offset=None, in_=g.slot_dram,
                                        in_offset=bass.IndirectOffsetOnAxis(ap=slots[:, t, c:c + 1], axis=0)
                                        ).then_inc(rows_in[i % 6], 16)

        @block.vector
        def _(dve):
            for i, (c, t) in enumerate(steps):
                dve.wait_ge(rows_in[i % 6], i // 6 * 16 + 16)
                if c:
                    dve.wait_ge(added, i - NT + 1)
                dve.scalar_tensor_tensor(out=g.x[:, t, :], in0=rows[i % 6][:, :], scalar=gates[:, t, c:c + 1],
                                         in1=g.x[:, t, :], op0=ALU.mult, op1=ALU.add).then_inc(added, 1)
            dve.wait_ge(added, len(steps))


def moe_layer(g, router_w, w1, b1, w2, b2):
    X = router_w.shape[0]
    with ExitStack() as ctx:
        s = Scope(g, ctx)
        slots = s.sb("moe_slots", [TP, NT, 2], I32)
        gates = s.sb("moe_gates", [TP, NT, 2])
        with ExitStack() as both:
            expert_weights = ExpertWeights(Scope(g, both), w1, w2)
            with ExitStack() as inner:
                si = Scope(g, inner)
                gate = si.sb("moe_gate", [TP, NT, X])
                rank = si.sb("moe_rank", [TP, NT, X])
                gateT = si.sb("moe_gateT", [X, N])
                hT = si.sb("moe_hT", [128, KC, N])
                h = si.sb("moe_h", [TP, NT, D])
                normalize(g, "moe_ln", g.x, h, hT)
                route(g, hT, router_w, gate, gateT, rank, expert_weights)
                assign_slots(g, h, rank, gate, X, slots, gates, b2, gateT)
            experts(g, b1, expert_weights)
        combine(g, slots, gates)


def far_tile(g, r, t):
    return bass.AP(tensor=g.far_dram.tensor, offset=r * N + t * TP * R * N, ap=[[R * N, TP], [1, N]])


def elu_and_turn(g, h, parts):
    with ExitStack() as ctx:
        s = Scope(g, ctx)
        low = [s.sb(f"elu_low{i}", [TP, D]) for i in range(2)]
        banks = [[s.ps(f"elu_turn{i}{j}", [128, 512]) for j in range(2)] for i in range(2)]
        clipped, exp_done, rows_done, v_chain = s.sem("elu_clipped"), s.sem("elu_exp"), s.sem("elu_rows"), s.sem("elu_vc")
        turned, copied, low_out = s.sem("elu_turned"), s.sem("elu_copied"), s.sem("elu_low_out")
        block = s.block()

        def turned_rows(t, j):
            return banks[t % 2][j][:, 0:3 * TP].rearrange("p (c t) -> p c t", t=TP)

        def take_low(dve, t):
            dve.wait_ge(copied, 2 * t + 2)
            for j in range(2):
                dve.tensor_tensor(parts[1][:, 3 * j:3 * j + 3, t, 0:TP], turned_rows(t, j),
                                  parts[0][:, 3 * j:3 * j + 3, t, 0:TP].bitcast(F32), op=ALU.subtract
                                  ).then_inc(low_out, 1)

        @block.vector
        def _(dve):
            link = chain(dve, v_chain)
            for t in range(NT + 1):
                if t < NT:
                    if t >= 2:
                        dve.wait_ge(rows_done, t - 1)
                    dve.tensor_scalar(low[t % 2][:, :], h[:, t, :], 0.0, None, op0=ALU.min).then_inc(clipped, 1)
                if t >= 1:
                    u = t - 1
                    dve.wait_ge(exp_done, u + 1)
                    link(dve.tensor_scalar(low[u % 2][:, :], low[u % 2][:, :], -1.0, None, op0=ALU.add))
                    dve.scalar_tensor_tensor(out=h[:, u, :], in0=h[:, u, :], scalar=0.0, in1=low[u % 2][:, :],
                                             op0=ALU.max, op1=ALU.add).then_inc(rows_done, 1)
                if t >= 2:
                    take_low(dve, t - 2)
            take_low(dve, NT - 1)
            dve.wait_ge(rows_done, NT)
            dve.wait_ge(low_out, 2 * NT)

        def take_turned(act, t):
            act.wait_ge(turned, t + 1)
            for j in range(2):
                act.activation(parts[0][:, 3 * j:3 * j + 3, t, 0:TP], turned_rows(t, j), ACT.Copy).then_inc(copied, 1)

        @block.scalar
        def _(act):
            for t in range(NT):
                act.wait_ge(clipped, t + 1)
                act.activation(low[t % 2][:, :], low[t % 2][:, :], ACT.Exp).then_inc(exp_done, 1)
                if t >= 1:
                    take_turned(act, t - 1)
            take_turned(act, NT - 1)
            act.wait_ge(copied, 2 * NT)

        @block.tensor
        def _(pe):
            for t in range(NT):
                pe.wait_ge(rows_done, t + 1)
                if t >= 2:
                    pe.wait_ge(low_out, 2 * (t - 1))
                turn_tile(pe, g, banks[t % 2], h, t, turned)


def rgat_layers(g, w1, b1, w2, b2, weights):
    with ExitStack() as ctx:
        s = Scope(g, ctx)
        h = s.sb("rgat_h", [TP, NT, D])
        for layer, (tag, w) in enumerate((("rg1", w1), ("rg2", w2))):
            H = weights[layer].shape[4]
            with ExitStack() as inner:
                si = Scope(g, inner)
                ks = si.sb(f"{tag}_ks", [TP, NT, R * H])
                qd = si.sb(f"{tag}_qd", [TP, NT, R * H])
                ks_low = si.sb(f"{tag}_ks_low", [TP, NT, R * H])
                shifted = si.sb(f"{tag}_shifted", [TP, NT, 2, R * H])
                bias = si.sb(f"{tag}_bias", [TP, D])
                with ExitStack() as inmost:
                    sm = Scope(g, inmost)
                    free = h[:, :, :].rearrange("p t d -> p (t d)")
                    if layer == 0:
                        hT = sm.sb(f"{tag}_hT", [128, KC, N])
                        normalize(g, "rg_ln", g.x, h, hT)
                        row = [free[:, 0:H * N].rearrange("p (h n) -> p h n", h=H),
                               sm.sb(f"{tag}_row", [TP, H, N])[:, :, :]]
                        greatest(g, tag, H, H, row, lambda r, t: far_tile(g, r, t), ks, qd, ks_low, shifted,
                                 (lambda c, t: [hT[:, c, t * TP:(t + 1) * TP]], weights[layer]),
                                 lambda sc: RelationValues(sc, g, tag, hT, w, b1, bias))
                    else:
                        parts = [sm.sb(f"{tag}_hT{j}", [128, KC, NT, TP + 1], FR) for j in range(2)]
                        elu_and_turn(g, h, parts)
                        row, junk = ([free[:, (i + j) * N:(i + j + 1) * N] for j in range(2)] for i in (0, 2))
                        stage = [free[:, 4 * N + j * D // 2:4 * N + (j + 1) * D // 2] for j in range(4)]
                        greatest(g, tag, H, H, [x.unsqueeze(1) for x in row], lambda r, t: far_tile(g, r, t),
                                 ks, qd, ks_low, shifted,
                                 (lambda c, t: [x[:, c, t, 0:TP] for x in parts], weights[layer]),
                                 lambda sc: WideRelationValues(sc, g, tag, parts, w, b2, bias, stage), junk)

                def finish(dve, hd, d, c0, c1, sums, recip):
                    width = D // H
                    at = slice(hd * width + c0, hd * width + c1)
                    out, plus = (h[:, d, at], bias[:, at]) if layer == 0 else (g.x[:, d, at], g.x[:, d, at])
                    return dve.scalar_tensor_tensor(out=out, in0=sums, scalar=recip, in1=plus,
                                                    op0=ALU.mult, op1=ALU.add)

                if H > 1:
                    attend(g, tag + "a", H, D // H, 5, ks, ks_low, shifted, finish)
                else:
                    attend_wide(g, tag + "a", ks, ks_low, shifted, h, finish)


PICKED = max(1, int(round(0.15 * N)))
QT = PICKED // 2
HEADS = 12
DH = D // HEADS


def pick_tokens(g, n, nT, wr, br, wk, bk, wm, keep, picks, picksT, picked_nT, score_rows, kT, w_sb):
    with ExitStack() as ctx:
        s = Scope(g, ctx)
        free = g.x[:, :, :].rearrange("p t d -> p (t d)")
        srow, node, tie, less = (free[:, i * N:(i + 1) * N] for i in range(4))
        wr_rows = free[:, 4 * N:4 * N + D]
        junk = free[:, 4 * N + D:4 * N + 3 * D].rearrange("p (a d) -> p a d", a=2)
        b_cols = s.sb("pick_bk", [128, KC])
        score = s.sb("pick_score", [TP, NT])
        br_col = s.sb("pick_br", [TP, 1])
        scoreT = s.sb("pick_scoreT", [NT, TP])
        own = s.sb("pick_own", [TP, NT])
        rank = s.sb("pick_rank", [TP, NT])
        ones = s.sb("pick_ones", [TP, TP])
        total = s.sb("pick_total", [TP, 1])
        ps = s.ps("pick_ps", [128, 512])
        turn_ps = [s.ps(f"pick_turn{i}", [QT, 512]) for i in range(2)]
        picked_ps = s.ps("pick_picked", [128, 3, 512])
        key_ps = [s.ps(f"pick_key{i}", [128, 512]) for i in range(2)]
        wk_in, wm_in, bk_in = s.sem("pick_wk_in"), s.sem("pick_wm_in"), s.sem("pick_bk_in")
        key_made, key_out = s.sem("pick_key_made"), s.sem("pick_key_out")
        keys = [(f, k) for f in range(KC) for k in range(len(TOKENS))]
        EARLY = len(TOKENS)
        small_in, ready, scored, turned, score_out, srow_in = (
            s.sem(f"pick_{x}") for x in ("small_in", "ready", "scored", "turned", "score_out", "srow_in"))
        weighed, ranked, v_chain, dots, copied = (
            s.sem(f"pick_{x}") for x in ("weighed", "ranked", "vc", "dots", "copied"))
        picksT_turned, picksT_out, gathered, score_saved, rows_ready = (
            s.sem(f"pick_{x}") for x in ("picksT_turned", "picksT_out", "gathered", "score_saved", "rows_ready"))
        block = s.block()
        j1 = PICKED + 1

        @block.sync
        def _(sp):
            sp.dma_start(wr_rows, rows_of(wr, TP, 0, D)).then_inc(small_in, 16)
            sp.dma_start(br_col[:, :], rows_of(br, TP, 0, 1)).then_inc(small_in, 16)
            sp.dma_start(w_sb[:, :, :], wk.rearrange("(c p) f -> p c f", p=128)).then_inc(wk_in, 16)
            sp.dma_start(b_cols[:, :], columns_of(bk), allow_slow_non_contiguous=True).then_inc(bk_in, 16)
            sp.wait_ge(copied, 1)
            sp.dma_start(g.score_dram, scoreT[:, :]).then_inc(score_out, 16)
            sp.wait_ge(score_out, 16)
            sp.dma_start(srow, rows_of(g.score_dram, TP, 0, N)).then_inc(srow_in, 16)
            sp.wait_ge(rows_ready, 1)
            sp.dma_start(score_rows[0:1, :], rows_of(g.score_dram, 1, 0, N)).then_inc(score_saved, 16)
            sp.wait_ge(key_made, len(keys))
            sp.dma_start(w_sb[:, :, :], wm.rearrange("(c p) f -> p c f", p=128)).then_inc(wm_in, 16)
            sp.wait_ge(score_saved, 16)
            sp.wait_ge(wm_in, 16)

        @block.gpsimd
        def _(pool):
            pool.iota(node, [[1, N]], base=0, channel_multiplier=0,
                      allow_small_or_imprecise_dtypes=True).then_inc(ready, 1)
            pool.iota(own[:, :], [[TP, NT]], base=0, channel_multiplier=1,
                      allow_small_or_imprecise_dtypes=True).then_inc(ready, 1)
            pool.memset(ones[:, :], 1.0).then_inc(ready, 1)
            pool.memset(score_rows[:, :], 1.0).then_inc(rows_ready, 1)

        @block.scalar
        def _(act):
            def take_key(i):
                f, k = keys[i]
                a, b = TOKENS[k]
                act.wait_ge(key_made, i + 1)
                act.activation(kT[:, f, a:b], key_ps[i % 2][:, 0:b - a], ACT.Identity,
                               bias=b_cols[:, f:f + 1]).then_inc(key_out, 1)

            act.wait_ge(bk_in, 16)
            for i in range(EARLY):
                take_key(i)
            act.wait_ge(dots, NT)
            act.wait_ge(small_in, 32)
            act.activation(score[:, :], score[:, :], ACT.Sigmoid, bias=br_col[:, 0:1]).then_inc(scored, 1)
            for i in range(EARLY, len(keys)):
                take_key(i)
            for i in range(5):
                act.wait_ge(picksT_turned, i + 1)
                act.activation(picksT[:, :, 2 * i:2 * i + 2, 0:TP],
                               turn_ps[i % 2][:, 0:4 * TP].rearrange("p (q k t) -> p q k t", q=2, k=2),
                               ACT.Copy).then_inc(picksT_out, 1)
            act.wait_ge(gathered, 1)
            act.activation(picked_nT[:, :, :].rearrange("p (a b) j -> p a (b j)", b=2),
                           picked_ps[:, :, 0:2 * j1], ACT.Copy).then_inc(gathered, 1)
            act.wait_ge(gathered, 2)

        @block.tensor
        def _(pe):
            def make_key(i):
                f, k = keys[i]
                a, b = TOKENS[k]
                if i >= 2:
                    pe.wait_ge(key_out, i - 1)
                for c in range(KC):
                    last = pe.matmul(key_ps[i % 2][:, 0:b - a], w_sb[:, c, f * 128:(f + 1) * 128], nT[:, c, a:b],
                                     start=(c == 0), stop=(c == KC - 1))
                last.then_inc(key_made, 1)

            pe.wait_ge(wk_in, 16)
            for i in range(EARLY):
                make_key(i)
            pe.wait_ge(scored, 1)
            pe.wait_ge(ready, 3)
            pe.transpose(ps[0:NT, 0:TP], score[:, :], g.ident[0:TP, 0:TP])
            pe.matmul(ps[0:TP, 128:128 + NT], ones[:, :], score[:, :], start=True, stop=True).then_inc(turned, 1)
            for i in range(EARLY, len(keys)):
                make_key(i)
            for i in range(5):
                if i == 0:
                    pe.wait_ge(ranked, NT)
                if i >= 2:
                    pe.wait_ge(picksT_out, i - 1)
                for q in range(2):
                    for k in range(2):
                        last = pe.transpose(turn_ps[i % 2][:, (2 * q + k) * TP:(2 * q + k + 1) * TP],
                                            picks[:, 2 * i + k, q * QT:(q + 1) * QT], g.ident[0:TP, 0:TP])
                last.then_inc(picksT_turned, 1)
            pe.wait_ge(weighed, 1)
            for c in range(KC):
                for t in range(NT):
                    last = pe.matmul(picked_ps[:, c // 2, (c % 2) * j1:(c % 2 + 1) * j1],
                                     n[:, t, c * 128:(c + 1) * 128], picks[:, t, :],
                                     start=(t == 0), stop=(t == NT - 1))
            last.then_inc(gathered, 1)

        @block.vector
        def _(dve):
            link = chain(dve, v_chain)
            dve.wait_ge(small_in, 32)
            for t in range(NT):
                if t >= 2:
                    dve.wait_ge(dots, t - 1)
                dve.tensor_tensor_reduce(out=junk[:, t % 2, :], in0=n[:, t, :], in1=wr_rows, scale=1.0,
                                         scalar=0.0, op0=ALU.mult, op1=ALU.add,
                                         accum_out=score[:, t:t + 1]).then_inc(dots, 1)
            dve.wait_ge(turned, 1)
            dve.tensor_copy(scoreT[:, :], ps[0:NT, 0:TP]).then_inc(copied, 1)
            link(dve.tensor_reduce(out=total[:, :], in_=ps[0:TP, 128:128 + NT], op=ALU.add, axis=AX_X))
            link(dve.tensor_scalar(total[:, :], total[:, :], 1e-6, None, op0=ALU.add))
            link(dve.reciprocal(total[:, :], total[:, :]))
            dve.tensor_scalar(picks[:, :, PICKED:j1], score[:, :].unsqueeze(2), total[:, 0:1], None,
                              op0=ALU.mult).then_inc(weighed, 1)
            dve.wait_ge(srow_in, 16)
            for t in range(NT):
                link(dve.tensor_scalar(less, node, own[:, t:t + 1], None, op0=ALU.is_lt))
                link(dve.scalar_tensor_tensor(out=tie, in0=srow, scalar=score[:, t:t + 1],
                                              in1=less, op0=ALU.is_equal, op1=ALU.mult))
                link(dve.scalar_tensor_tensor(out=less, in0=srow, scalar=score[:, t:t + 1],
                                              in1=tie, op0=ALU.is_lt, op1=ALU.add))
                link(dve.tensor_reduce(out=rank[:, t:t + 1], in_=less, op=ALU.add, axis=AX_X))
                dve.tensor_scalar(picks[:, t, 0:PICKED], node[:, 0:PICKED], rank[:, t:t + 1], None,
                                  op0=ALU.is_equal).then_inc(ranked, 1)
            link(dve.tensor_scalar(keep[:, :], rank[:, :], PICKED - 0.5, None, op0=ALU.is_gt))


def columns_of(v):
    return v.rearrange("(c p) -> p c", p=128)


def mix_and_project(g, z, nT, picked_nT, score_rows, keep, bm, wv, wq, bq, v, qT, w_sb):
    with ExitStack() as ctx:
        s = Scope(g, ctx)
        w_sb = [w_sb, g.x_all[:, 0:KC, :]]
        mixed = s.sb("mix_rows", [2, D])
        b_cols = s.sb("mix_b", [128, KC])
        row_ps = s.ps("mix_row", [1, 2, 512])
        ps = [s.ps(f"mix_ps{i}", [128, 2, 512]) for i in range(3)]
        w_in, w_used, small_in, row_made, row_out = s.sems("mix_w_in", 2), s.sem("mix_w_used"), s.sem("mix_small"), s.sem("mix_row_made"), s.sem("mix_row_out")
        made, taken = s.sem("mix_made"), s.sem("mix_taken")
        block = s.block()
        jobs = [("mix", t) for t in range(NT)] + [("value", t) for t in range(NT)] + [("query", f) for f in range(KC)]
        weights = {"mix": 0, "value": 1, "query": 2}
        last_of = {kind: max(i for i, j in enumerate(jobs) if j[0] == kind) + 1 for kind in weights}

        @block.sync
        def _(sp):
            sp.dma_start(mixed[1:2, :], rows_of(bm, 1, 0, D)).then_inc(small_in, 16)
            sp.dma_start(b_cols[:, :], columns_of(bq), allow_slow_non_contiguous=True).then_inc(small_in, 16)
            sp.dma_start(w_sb[1], wv.rearrange("(c p) f -> p c f", p=128)).then_inc(w_in[1], 16)
            sp.wait_ge(made, last_of["mix"])
            sp.dma_start(w_sb[0][:, :, :], wq.rearrange("(c p) f -> p c f", p=128)).then_inc(w_in[0], 16)

        @block.tensor
        def _(pe):
            for a in range(2):
                for c in range(KC):
                    last = pe.matmul(row_ps[:, a, 0:384], picked_nT[:, c, PICKED:PICKED + 1],
                                     w_sb[0][:, c, a * 384:(a + 1) * 384], start=(c == 0), stop=(c == KC - 1))
            last.then_inc(row_made, 1)
            pe.wait_ge(row_out, 1)
            pe.wait_ge(small_in, 32)
            for i, (kind, at) in enumerate(jobs):
                w = w_sb[weights[kind] % 2]
                out = ps[i % 3]
                if kind != "mix":
                    pe.wait_ge(w_in[weights[kind] % 2], 16)
                if i >= 3:
                    pe.wait_ge(taken, i - 2)
                if kind in ("mix", "value"):
                    rows = slice(at * TP, (at + 1) * TP)
                    for a in range(2):
                        cols = slice(a * 384, (a + 1) * 384)
                        if kind == "mix":
                            pe.matmul(out[0:TP, a, 0:384], score_rows[:, rows], mixed[:, cols],
                                      start=True, stop=False)
                        for c in range(KC):
                            last = pe.matmul(out[0:TP, a, 0:384], nT[:, c, rows], w[:, c, cols],
                                             start=(c == 0 and kind == "value"), stop=(c == KC - 1))
                else:
                    for c in range(KC):
                        last = pe.matmul(out[:, 0, 0:PICKED], w[:, c, at * 128:(at + 1) * 128],
                                         picked_nT[:, c, 0:PICKED], start=(c == 0), stop=(c == KC - 1))
                last.then_inc(made, 1)

        @block.vector
        def _(dve):
            dve.wait_ge(row_made, 1)
            dve.tensor_copy(mixed[0:1, :].rearrange("p (a b) -> p a b", a=2), row_ps[:, :, 0:384]).then_inc(row_out, 1)
            dve.wait_ge(small_in, 32)
            for i, (kind, at) in enumerate(jobs):
                dve.wait_ge(made, i + 1)
                out = ps[i % 3]
                if kind == "mix":
                    z_t = z[:, at, :].rearrange("p (a b) -> p a b", a=2)
                    last = dve.scalar_tensor_tensor(out=z_t, in0=out[0:TP, :, 0:384], scalar=keep[:, at:at + 1],
                                                    in1=z_t, op0=ALU.mult, op1=ALU.add)
                elif kind == "value":
                    last = dve.tensor_copy(v[:, at, :].rearrange("p (a b) -> p a b", a=2), out[0:TP, :, 0:384])
                else:
                    last = dve.tensor_scalar(qT[:, at, :], out[:, 0, 0:PICKED], b_cols[:, at:at + 1], None,
                                             op0=ALU.add)
                last.then_inc(taken, 1)
            dve.wait_ge(taken, len(jobs))


def attend_picked(g, z, kT, v, qT, picksT, bv, wo, bo):
    SCALE = DH ** -0.5
    units = [(q, h) for q in range(2) for h in range(HEADS)]
    with ExitStack() as ctx:
        s = Scope(g, ctx)
        probs = [s.sb(f"att_probs{i}", [QT, N]) for i in range(2)]
        probsT = [s.sb(f"att_probsT{i}", [TP, NT, QT]) for i in range(2)]
        top = s.sb("att_top", [QT, len(units)])
        total = s.sb("att_total", [QT, len(units)])
        ctxT = s.sb("att_ctxT", [128, KC, PICKED])
        bv_cols = s.sb("att_bv", [128, KC])
        wo_sb = s.sb("att_wo", [128, KC, D])
        bo_row = s.sb("att_bo", [1, D])
        ones = s.sb("att_ones", [1, QT])
        out_parts = [s.sb(f"att_out{j}", [QT, 2, D], FR) for j in range(2)]
        score_ps = [s.ps(f"att_score{i}", [128, 3, 512]) for i in range(2)]
        turn_ps = [s.ps(f"att_turn{i}", [TP, 512]) for i in range(2)]
        flat = [x[0:QT, :, :].rearrange("p a b -> p (a b)") for x in score_ps]
        small_in, wo_in, one_set = s.sem("att_small"), s.sem("att_wo_in"), s.sem("att_one")
        scored, topped, exp_done, scaled, turned, turned_out = (
            s.sem(f"att_{x}") for x in ("scored", "topped", "exp", "scaled", "turned", "turned_out"))
        ctx_made, ctx_out, v_chain, out_made, out_taken, spread, added = (
            s.sem(f"att_{x}") for x in ("ctx_made", "ctx_out", "vc", "out_made", "out_taken", "spread", "added"))
        block = s.block()

        @block.sync
        def _(sp):
            sp.dma_start(bv_cols[:, :], columns_of(bv), allow_slow_non_contiguous=True).then_inc(small_in, 16)
            sp.dma_start(bo_row[:, :], rows_of(bo, 1, 0, D)).then_inc(small_in, 16)
            sp.dma_start(wo_sb[:, :, :], wo.rearrange("(c p) f -> p c f", p=128)).then_inc(wo_in, 16)

        @block.gpsimd
        def _(pool):
            pool.memset(ones[:, :], 1.0).then_inc(one_set, 1)

        @block.tensor
        def _(pe):
            def scores(i):
                q, h = units[i]
                at = slice(h % 2 * DH, h % 2 * DH + DH)
                if i >= 2:
                    pe.wait_ge(ctx_out, i - 1)
                for k in range(0, N, 512):
                    w = min(512, N - k)
                    last = pe.matmul(flat[i % 2][:, k:k + w], qT[at, h // 2, q * QT:(q + 1) * QT],
                                     kT[at, h // 2, k:k + w], start=True, stop=True)
                last.then_inc(scored, 1)

            def context(i):
                q, h = units[i]
                pe.wait_ge(scaled, i + 1)
                for half in range(2):
                    if i >= 1:
                        pe.wait_ge(turned_out, 2 * (i - 1) + half + 1)
                    for k in range(5):
                        t = half * 5 + k
                        last = pe.transpose(turn_ps[half][:, k * QT:(k + 1) * QT], probs[i % 2][:, t * TP:(t + 1) * TP],
                                            g.ident[0:QT, 0:QT])
                    last.then_inc(turned, 1)
                pe.wait_ge(turned_out, 2 * i + 2)
                at = slice(h % 2 * DH, h % 2 * DH + DH)
                for t in range(NT):
                    last = pe.matmul(score_ps[i % 2][at, 0, 0:QT], v[:, t, h * DH:(h + 1) * DH],
                                     probsT[i % 2][:, t, :], start=(t == 0), stop=(t == NT - 1))
                last.then_inc(ctx_made, 1)

            scores(0)
            for i in range(len(units)):
                if i + 1 < len(units):
                    scores(i + 1)
                context(i)
            pe.wait_ge(ctx_out, len(units))
            pe.wait_ge(wo_in, 16)
            pe.wait_ge(small_in, 32)
            pe.wait_ge(one_set, 1)
            for q in range(2):
                for a in range(2):
                    cols = slice(a * 384, (a + 1) * 384)
                    pe.matmul(score_ps[q][0:QT, a, 0:384], ones[:, :], bo_row[:, cols], start=True, stop=False)
                    for c in range(KC):
                        last = pe.matmul(score_ps[q][0:QT, a, 0:384], ctxT[:, c, q * QT:(q + 1) * QT],
                                         wo_sb[:, c, cols], start=False, stop=(c == KC - 1))
                last.then_inc(out_made, 1)
            pe.wait_ge(out_taken, 4)
            for t in range(NT):
                if t >= 2:
                    pe.wait_ge(added, t - 1)
                for a in range(2):
                    for q in range(2):
                        for j in range(2):
                            last = pe.matmul(score_ps[t % 2][0:TP, a, 0:384], picksT[:, q, t, 0:TP],
                                             out_parts[j][:, q, a * 384:(a + 1) * 384],
                                             start=(q == 0 and j == 0), stop=(q == 1 and j == 1))
                last.then_inc(spread, 1)

        @block.vector
        def _(dve):
            link = chain(dve, v_chain)
            dve.wait_ge(small_in, 32)

            def first_half(i):
                dve.wait_ge(scored, i + 1)
                link(dve.tensor_reduce(out=top[:, i:i + 1], in_=flat[i % 2][:, 0:N], op=ALU.max, axis=AX_X))
                dve.tensor_scalar(top[:, i:i + 1], top[:, i:i + 1], -SCALE, None, op0=ALU.mult).then_inc(topped, 1)

            def second_half(i):
                dve.wait_ge(exp_done, i + 1)
                link(dve.reciprocal(total[:, i:i + 1], total[:, i:i + 1]))
                dve.tensor_scalar(probs[i % 2][:, :], probs[i % 2][:, :], total[:, i:i + 1], None,
                                  op0=ALU.mult).then_inc(scaled, 1)

            def take_context(i):
                q, h = units[i]
                at = slice(h % 2 * DH, h % 2 * DH + DH)
                dve.wait_ge(ctx_made, i + 1)
                dve.tensor_scalar(ctxT[at, h // 2, q * QT:(q + 1) * QT], score_ps[i % 2][at, 0, 0:QT],
                                  bv_cols[at, h // 2:h // 2 + 1], None, op0=ALU.add).then_inc(ctx_out, 1)

            for i in range(len(units)):
                first_half(i)
                if i >= 1:
                    take_context(i - 1)
                second_half(i)
            take_context(len(units) - 1)
            for q in range(2):
                dve.wait_ge(out_made, q + 1)
                high, low = (x[:, q, :].rearrange("p (a b) -> p a b", a=2) for x in out_parts)
                dve.tensor_copy(high, score_ps[q][0:QT, 0:2, 0:384]).then_inc(out_taken, 1)
                dve.wait_ge(out_taken, 2 * q + 1)
                dve.tensor_tensor(low, score_ps[q][0:QT, 0:2, 0:384], high.bitcast(F32),
                                  op=ALU.subtract).then_inc(out_taken, 1)
            for t in range(NT):
                dve.wait_ge(spread, t + 1)
                z_t = z[:, t, :].rearrange("p (a b) -> p a b", a=2)
                dve.tensor_tensor(z_t, z_t, score_ps[t % 2][0:TP, 0:2, 0:384], op=ALU.add).then_inc(added, 1)
            dve.wait_ge(added, NT)

        @block.scalar
        def _(act):
            for i in range(len(units)):
                act.wait_ge(topped, i + 1)
                if i >= 2:
                    act.wait_ge(turned, 2 * (i - 1))
                act.activation(probs[i % 2][:, :], flat[i % 2][:, 0:N], ACT.Exp, bias=top[:, i:i + 1], scale=SCALE,
                               accum_out=total[:, i:i + 1]).then_inc(exp_done, 1)
                for half in range(2):
                    act.wait_ge(turned, 2 * i + half + 1)
                    if i >= 2:
                        act.wait_ge(ctx_made, i - 1)
                    act.activation(probsT[i % 2][:, half * 5:half * 5 + 5, :].rearrange("p t q -> p (t q)"),
                                   turn_ps[half][:, 0:5 * QT], ACT.Copy).then_inc(turned_out, 1)


def feed_forward(g, z, nT, w1, b1, w2, b2):
    F = w1.shape[1]
    FC = F // 128
    with ExitStack() as ctx:
        s = Scope(g, ctx)
        up_w = s.sb("ff_up_w", [128, KC, F])
        down_w = s.sb("ff_down_w", [128, FC, D])
        inner = s.sb("ff_inner", [128, FC, N])
        b1_cols = s.sb("ff_b1", [128, FC])
        b2_row = s.sb("ff_b2", [1, D])
        ones = s.sb("ff_ones", [1, TP])
        up_ps = [s.ps(f"ff_up{i}", [128, 512]) for i in range(4)]
        down_ps = [s.ps(f"ff_down{i}", [TP, 2, 512]) for i in range(2)]
        w_in, one_set, up_done, gelu_done, down_done, added, plus = (
            s.sem(f"ff_{x}") for x in ("w_in", "one_set", "up_done", "gelu_done", "down_done", "added", "plus"))
        x_in = s.sem("ff_x_in")
        block = s.block()
        ups = [(f, k) for f in range(FC) for k in range(len(TOKENS))]

        @block.sync
        def _(sp):
            sp.dma_start(g.x, g.x_dram).then_inc(x_in, 16)
            sp.dma_start(up_w[:, :, :], w1.rearrange("(c p) f -> p c f", p=128)).then_inc(w_in, 16)
            sp.dma_start(down_w[:, :, :], w2.rearrange("(c p) f -> p c f", p=128)).then_inc(w_in, 16)
            sp.dma_start(b1_cols[:, :], columns_of(b1), allow_slow_non_contiguous=True).then_inc(w_in, 16)
            sp.dma_start(b2_row[:, :], rows_of(b2, 1, 0, D)).then_inc(w_in, 16)

        @block.gpsimd
        def _(pool):
            pool.memset(ones[:, :], 1.0).then_inc(one_set, 1)
            pool.wait_ge(x_in, 16)
            for t in range(NT):
                pool.tensor_tensor(g.x[:, t, :], g.x[:, t, :], z[:, t, :], op=ALU.add).then_inc(plus, 1)

        @block.tensor
        def _(pe):
            pe.wait_ge(w_in, 64)
            pe.wait_ge(one_set, 1)
            for n, (f, k) in enumerate(ups):
                a, b = TOKENS[k]
                if n >= 4:
                    pe.wait_ge(gelu_done, n - 3)
                for c in range(KC):
                    last = pe.matmul(up_ps[n % 4][:, 0:b - a], up_w[:, c, f * 128:(f + 1) * 128], nT[:, c, a:b],
                                     start=(c == 0), stop=(c == KC - 1))
                last.then_inc(up_done, 1)
            pe.wait_ge(gelu_done, len(ups))
            for t in range(NT):
                if t >= 2:
                    pe.wait_ge(added, t - 1)
                for a in range(2):
                    cols = slice(a * 384, (a + 1) * 384)
                    pe.matmul(down_ps[t % 2][:, a, 0:384], ones[:, :], b2_row[:, cols], start=True, stop=False)
                    for f in range(FC):
                        last = pe.matmul(down_ps[t % 2][:, a, 0:384], inner[:, f, t * TP:(t + 1) * TP],
                                         down_w[:, f, cols], start=False, stop=(f == FC - 1))
                last.then_inc(down_done, 1)

        @block.scalar
        def _(act):
            act.wait_ge(w_in, 64)
            for n, (f, k) in enumerate(ups):
                a, b = TOKENS[k]
                act.wait_ge(up_done, n + 1)
                act.activation(inner[:, f, a:b], up_ps[n % 4][:, 0:b - a], ACT.Gelu,
                               bias=b1_cols[:, f:f + 1]).then_inc(gelu_done, 1)

        @block.vector
        def _(dve):
            for t in range(NT):
                dve.wait_ge(down_done, t + 1)
                dve.wait_ge(plus, t + 1)
                x_t = g.x[:, t, :].rearrange("p (a b) -> p a b", a=2)
                dve.tensor_tensor(x_t, x_t, down_ps[t % 2][:, :, 0:384], op=ALU.add).then_inc(added, 1)
            dve.wait_ge(added, NT)


def mixed_layer(g, g1, b1, g2, b2, wr, br, wq, bq, wk, bk, wv, bv, wo, bo, wm, bm, w1, bf1, w2, bf2):
    with ExitStack() as ctx:
        s = Scope(g, ctx)
        z = s.sb("mixed_z", [TP, NT, D])
        normalize(g, "z_ln", g.x, z, None, keep_in=g.x_dram)
        with ExitStack() as attention:
            sa = Scope(g, attention)
            keep = sa.sb("keep", [TP, NT])
            picksT = sa.sb("picksT", [QT, 2, NT, TP + 1], FR)
            qT = sa.sb("qT", [128, KC, PICKED])
            kT = sa.sb("kT", [128, KC, N])
            v = sa.sb("v", [TP, NT, D])
            with ExitStack() as inner:
                si = Scope(g, inner)
                nT = si.sb("nT", [128, KC, N])
                picked_nT = si.sb("picked_nT", [128, KC, PICKED + 1])
                score_rows = si.sb("score_rows", [2, N])
                w_sb = si.sb("mixed_w", [128, KC, D])
                normalize(g, "n_ln", z, v, nT, g1, b1)
                with ExitStack() as inmost:
                    picks = Scope(g, inmost).sb("picks", [TP, NT, PICKED + 1])
                    pick_tokens(g, v, nT, wr, br, wk, bk, wm, keep, picks, picksT, picked_nT, score_rows, kT, w_sb)
                mix_and_project(g, z, nT, picked_nT, score_rows, keep, bm, wv, wq, bq, v, qT, w_sb)
            attend_picked(g, z, kT, v, qT, picksT, bv, wo, bo)
        with ExitStack() as inner:
            si = Scope(g, inner)
            nT = si.sb("n2T", [128, KC, N])
            with ExitStack() as inmost:
                n2 = Scope(g, inmost).sb("n2", [TP, NT, D])
                normalize(g, "n2_ln", z, n2, nT, g2, b2)
            feed_forward(g, z, nT, w1, bf1, w2, bf2)


def load_x(g, x):
    with ExitStack() as ctx:
        s = Scope(g, ctx)
        x_in = s.sem("x_in")
        block = s.block()

        @block.sync
        def _(sp):
            sp.dma_start(g.x, x.rearrange("(t p) d -> p t d", p=TP)).then_inc(x_in, 16)
            sp.wait_ge(x_in, 16)


def store_x(g, out):
    with ExitStack() as ctx:
        s = Scope(g, ctx)
        x_out = s.sem("x_out")
        block = s.block()

        @block.sync
        def _(sp):
            sp.dma_start(out.rearrange("(t p) d -> p t d", p=TP), g.x).then_inc(x_out, 16)
            sp.wait_ge(x_out, 16)


def build(nc, io, out):
    g = Shared()
    g.nc = nc
    scratch(g)
    free = sorted(nc.free_semaphores)
    total = SEMAPHORES + SOFTWARE_SEMAPHORES
    first = min(i for i in free if all(k in free for k in range(i, i + total)))
    g.semaphore_ids, g.semaphores_used, g.semaphores_live = range(first, first + SEMAPHORES), 0, 0
    g.software_ids = list(range(first + SEMAPHORES, first + total))
    with ExitStack() as ctx:
        s = Scope(g, ctx)
        g.ident = s.sb("ident", [128, 128])
        g.x_all = s.sb("x_all", [128, NT, D])
        g.x = g.x_all[0:TP, :, :]
        constants(g)
        load_x(g, io["x"])
        relations = [[io[f"L1_gnn_{k}{n}"] for k in "Wqk"] for n in (1, 2)]
        score_weights = [s.sb(f"score_weights{n}", [128, KC, 2, R, q.shape[1]])
                         for n, (w, q, k) in enumerate(relations)]
        with ExitStack() as first:
            sf = Scope(g, first)
            g.counts_u = sf.sb("counts_u", [TP, NT, N], U16)
            g.far_u = sf.sb("far_u", [TP, NT, N], BF16)
            gat_layer(g, io["src"], io["dst"], io["edge_type_3"],
                      *[io["L0_gnn_" + k] for k in ("W_fc", "W_res", "attn_l", "attn_r")], relations, score_weights)
        moe_layer(g, *[io["L0_ffn_" + k] for k in ("router_w", "w1", "b1", "w2", "b2")])
        rgat_layers(g, *[io["L1_gnn_" + k] for k in ("W1", "b1", "W2", "b2")], score_weights)
        mixed_layer(g, *[io["L1_ffn_" + k] for k in (
            "g1", "b1", "g2", "b2", "Wr", "br", "Wq", "bq", "Wk", "bk", "Wv", "bv", "Wo", "bo", "Wm", "bm",
            "W1", "bf1", "W2", "bf2")])
        store_x(g, out)


def kernel(**inputs):
    import concourse.bacc as bacc
    from concourse.bass_utils import run_bass_kernel_spmd

    nc = bacc.Bacc("TRN2", target_bir_lowering=False, num_devices=1)
    arrays, io = {}, {}
    for name, a in inputs.items():
        a = np.ascontiguousarray(a)
        a = a.reshape(a.shape or (1,))
        arrays[f"in_{name}"] = a
        io[name] = nc.dram_tensor(f"in_{name}", a.shape, mybir.dt.from_np(a.dtype), kind="ExternalInput").ap()
    out = nc.dram_tensor("out", (N, D), F32, kind="ExternalOutput").ap()
    build(nc, io, out)
    return run_bass_kernel_spmd(nc, [arrays], core_ids=[0]).results[0]["out"]
```
